# Optimizing a Trainium2 kernel written in Bass

```python
import numpy as np
import jax
import jax.numpy as jnp

def _softmax(x, axis=-1):
    return jax.nn.softmax(x, axis=axis)

def _gelu(x):
    return jax.nn.gelu(x, approximate=True)

def _silu(x):
    return jax.nn.silu(x)

def _sigmoid(x):
    return jax.nn.sigmoid(x)

def _layernorm(x, axis=-1, eps=1e-05):
    m = jnp.mean(x, axis=axis, keepdims=True)
    v = jnp.var(x, axis=axis, keepdims=True)
    return (x - m) / jnp.sqrt(v + eps)

def _scatter_add(tgt, idx, src, axis=0):
    return tgt.at[idx].add(src)

def _segment_sum(src, seg, n):
    return jax.ops.segment_sum(src, seg, n)
kernel_name = 'mk_vit_tower_postln_d1_tok_img768_r4_138674'

def setup_inputs(seed: int=0):
    np.random.seed(seed)
    _w = jnp.asarray

    def _rec_inputs():
        import jax
        import jax.numpy as jnp
        _rk = jax.random.key(seed)
        x = 1.64766e-05 + 1.00005 * jax.random.normal(jax.random.fold_in(_rk, 1), (8, 3, 512, 192), jnp.float32)
        return x
    x = _rec_inputs()

    def _L0_tok_setup():
        import jax, jax.numpy as jnp
        import numpy as np
        NUM_BANDS = 6
        D_MODEL = 192
        B, N = (2, 512)
        IN_FEATURES = 3 * NUM_BANDS * 2 * D_MODEL
        key = jax.random.key(seed)
        k_xyz, k_w = jax.random.split(key)
        xyz = jax.random.normal(k_xyz, (B, 3, N, D_MODEL), dtype=jnp.float32)
        freq_bands = 2.0 ** jnp.linspace(0.0, NUM_BANDS - 1, NUM_BANDS).astype(jnp.float32)
        bound = 1.0 / np.sqrt(IN_FEATURES)
        W = jax.random.uniform(k_w, (D_MODEL, IN_FEATURES), dtype=jnp.float32, minval=-bound, maxval=bound)
        return {'xyz': xyz, 'freq_bands': freq_bands, 'W': W}
    _L0_tok_all = _L0_tok_setup()
    _L0_tok_in = {k: v for k, v in _L0_tok_all.items() if k in ('freq_bands', 'W')}
    del _L0_tok_all

    def _L0_attn_setup():
        import jax, jax.numpy as jnp
        import numpy as np
        EMBED_DIM = 192
        NUM_HEADS = 12
        HEAD_DIM = EMBED_DIM // NUM_HEADS
        key = jax.random.key(seed)
        k_x, k_wqkv, k_bqkv, k_wp, k_bp = jax.random.split(key, 5)
        B, N, C = (2, 512, EMBED_DIM)
        lim_qkv = 1.0 / np.sqrt(C)
        lim_p = 1.0 / np.sqrt(C)
        return {'x': jax.random.normal(k_x, (B, N, C), dtype=jnp.float32), 'w_qkv': jax.random.uniform(k_wqkv, (3 * C, C), minval=-lim_qkv, maxval=lim_qkv, dtype=jnp.float32), 'b_qkv': jax.random.uniform(k_bqkv, (3 * C,), minval=-lim_qkv, maxval=lim_qkv, dtype=jnp.float32), 'w_proj': jax.random.uniform(k_wp, (C, C), minval=-lim_p, maxval=lim_p, dtype=jnp.float32), 'b_proj': jax.random.uniform(k_bp, (C,), minval=-lim_p, maxval=lim_p, dtype=jnp.float32)}
    _L0_attn_all = _L0_attn_setup()
    _L0_attn_in = {k: v for k, v in _L0_attn_all.items() if k in ('w_qkv', 'b_qkv', 'w_proj', 'b_proj')}
    del _L0_attn_all

    def _L0_ffn_setup():
        import jax, jax.numpy as jnp
        import numpy as np
        import math
        B, S, D = (4, 1024, 192)
        E = 8
        TOP_K = 2
        H = 512
        CAP_F = 1.25
        EPS = 1e-06
        ALPHA = 1.0
        key = jax.random.key(seed)
        k0, k1, k2, k3 = jax.random.split(key, 4)
        x = jax.random.normal(k0, (B, S, D), jnp.float32)
        gate_w = jax.random.normal(k1, (E, D), jnp.float32) * 0.02
        w13 = jax.random.normal(k2, (E, 2 * H, D), jnp.float32) * 0.02
        w2 = jax.random.normal(k3, (E, D, H), jnp.float32) * 0.02
        norm_w = jnp.ones((E, D), jnp.float32)
        return {'x': x, 'gate_w': gate_w, 'w13': w13, 'w2': w2, 'norm_w': norm_w}
    _L0_ffn_all = _L0_ffn_setup()
    _L0_ffn_in = {k: v for k, v in _L0_ffn_all.items() if k in ('gate_w', 'w13', 'w2', 'norm_w')}
    del _L0_ffn_all
    return {'x': x, 'L0_tok_freq_bands': _L0_tok_in['freq_bands'], 'L0_tok_W': _L0_tok_in['W'], 'L0_attn_w_qkv': _L0_attn_in['w_qkv'], 'L0_attn_b_qkv': _L0_attn_in['b_qkv'], 'L0_attn_w_proj': _L0_attn_in['w_proj'], 'L0_attn_b_proj': _L0_attn_in['b_proj'], 'L0_ffn_gate_w': _L0_ffn_in['gate_w'], 'L0_ffn_w13': _L0_ffn_in['w13'], 'L0_ffn_w2': _L0_ffn_in['w2'], 'L0_ffn_norm_w': _L0_ffn_in['norm_w']}

def reference(x, L0_tok_freq_bands, L0_tok_W, L0_attn_w_qkv, L0_attn_b_qkv, L0_attn_w_proj, L0_attn_b_proj, L0_ffn_gate_w, L0_ffn_w13, L0_ffn_w2, L0_ffn_norm_w):
    import jax
    import jax.numpy as jnp

    def _L0_tok_ref(xyz, freq_bands, W):
        import jax, jax.numpy as jnp
        import numpy as np
        NUM_BANDS = 6
        D_MODEL = 192
        B, N = (2, 512)
        IN_FEATURES = 3 * NUM_BANDS * 2 * D_MODEL
        b, c, n, d = xyz.shape
        xb = 2.0 * jnp.pi * xyz[..., None] * freq_bands
        feat = jnp.concatenate([jnp.sin(xb), jnp.cos(xb)], axis=-1)
        feat = feat.reshape(b, n, -1)
        return jnp.einsum('bnf,of->bno', feat, W)

    def _L0_attn_ref(x, w_qkv, b_qkv, w_proj, b_proj):
        import jax, jax.numpy as jnp
        import numpy as np
        EMBED_DIM = 192
        NUM_HEADS = 12
        HEAD_DIM = EMBED_DIM // NUM_HEADS
        b, n, c = x.shape
        h, d = (NUM_HEADS, HEAD_DIM)
        qkv = x @ w_qkv.T + b_qkv
        qkv = qkv.reshape(b, n, 3, h, d).transpose(2, 0, 3, 1, 4)
        q, k, v = (qkv[0], qkv[1], qkv[2])
        scale = d ** (-0.5)
        attn = jnp.einsum('bhnd,bhmd->bhnm', q, k) * scale
        attn = jax.nn.softmax(attn, axis=-1)
        out = jnp.einsum('bhnm,bhmd->bhnd', attn, v)
        out = out.transpose(0, 2, 1, 3).reshape(b, n, c)
        return out @ w_proj.T + b_proj

    def _L0_ffn_ref(x, gate_w, w13, w2, norm_w):
        import jax, jax.numpy as jnp
        import numpy as np
        import math
        B, S, D = (4, 1024, 192)
        E = 8
        TOP_K = 2
        H = 512
        CAP_F = 1.25
        EPS = 1e-06
        ALPHA = 1.0
        Bx, Sx, Dx = x.shape
        N = Bx * Sx
        cap = int(math.ceil(CAP_F * TOP_K * N / E))
        xf = x.reshape(N, Dx)
        logits = xf.astype(jnp.float32) @ gate_w.T
        probs = jax.nn.softmax(logits, axis=-1)
        top_p, top_i = jax.lax.top_k(probs, TOP_K)
        w = top_p / jnp.sum(top_p, axis=-1, keepdims=True)
        flat_e = top_i.reshape(-1)
        onehot = jax.nn.one_hot(flat_e, E, dtype=jnp.int32)
        pos = jnp.take_along_axis(jnp.cumsum(onehot, axis=0) - 1, flat_e[:, None], axis=1)[:, 0]
        keep = pos < cap
        didx = flat_e * cap + jnp.minimum(pos, cap - 1)
        safe = jnp.where(keep, didx, E * cap)
        x_rep = jnp.repeat(xf, TOP_K, axis=0)
        buf = jnp.zeros((E * cap + 1, Dx), x.dtype).at[safe].set(x_rep)
        buf = buf[:-1].reshape(E, cap, Dx)
        z = 2.0 * buf
        z = z * jax.lax.rsqrt(jnp.mean(z * z, axis=-1, keepdims=True) + EPS)
        z = z * norm_w[:, None, :]
        gu = jnp.einsum('ecd,ehd->ech', z, w13)
        g, u = jnp.split(gu, 2, axis=-1)
        y = buf + ALPHA * jnp.einsum('ech,edh->ecd', jax.nn.silu(g) * u, w2)
        y_tok = y.reshape(E * cap, Dx)[didx]
        cw = (w.reshape(-1) * keep.astype(w.dtype)).astype(x.dtype)
        out = (cw[:, None] * y_tok).reshape(N, TOP_K, Dx).sum(axis=1)
        return out.reshape(Bx, Sx, Dx)
    h = _L0_tok_ref(x, L0_tok_freq_bands, L0_tok_W)
    h = _layernorm(h + _L0_attn_ref(h, L0_attn_w_qkv, L0_attn_b_qkv, L0_attn_w_proj, L0_attn_b_proj), axis=-1)
    h = _layernorm(h + _L0_ffn_ref(h, L0_ffn_gate_w, L0_ffn_w13, L0_ffn_w2, L0_ffn_norm_w), axis=-1)
    return h

_drawn_inputs = setup_inputs


def setup_inputs(seed=0):
    import zlib

    import numpy as np

    out = dict(_drawn_inputs(seed))
    spreads = {'L0_ffn_norm_w': (1.0, 0.6)}
    factors = {'L0_attn_w_qkv': 3.926, 'L0_ffn_gate_w': 8.0, 'L0_ffn_w13': 8.0, 'L0_ffn_w2': 8.0}
    for name, (base, spread) in spreads.items():
        noise = np.random.default_rng([zlib.crc32(name.encode()), seed]).standard_normal(out[name].shape)
        drawn = base * np.exp(spread * noise) if base else spread * noise
        out[name] = jnp.asarray(drawn.astype(out[name].dtype))
    for name, factor in factors.items():
        out[name] = (out[name] * factor).astype(out[name].dtype)
    return out
```

```python
from contextlib import ExitStack

import concourse.bass as bass
from concourse import mybir

F32 = mybir.dt.float32
F32R = mybir.dt.float32r
U32 = mybir.dt.uint32
ALU = mybir.AluOpType
ACT = mybir.ActivationFunctionType
AX = mybir.AxisListType

P = 128
BATCHES = 8
SEQ = 512
TILES = SEQ // P
TOKENS = BATCHES * SEQ
D = 192
HALF = D // 2
VALUES = 3 * D
BANDS = 6
XCHUNKS = 5
ANGLES = 4 * BANDS + BANDS // 2
KTILES = 2 * ANGLES
HEADS, HD = 12, 16
GROUPS = 4
QUADS = 3
E, TOPK, HID = 8, 2, 512
CAP = 1280
SLOTS = E * CAP
ROUND = 12582912.0
TWO_PI = 6.283185
HALF_PI = 1.5707963

RING_F, RING_T = 6, 3
A_UNITS = 2 + 8 + 48 + 4 + 2 + 1 + 1
B_UNITS = 4 + 48

P_ANGLES = {1: 0, 3: 1, 5: 2, 7: 3}
A_FIRST, A_LAST = 4, 22
T_ANGLES = [[22, 23], [24], [25], [26]]


def a_angles(u):
    n = A_LAST - A_FIRST
    return [A_FIRST + k for k in range(u * n // 48, (u + 1) * n // 48)]


C_ID, C_UP, C_ONE, C_IOTA, C_SEL, C_NHALF, C_HPI = 0, 128, 256, 384, 392, 393, 397
C_ALL = 398


def build(nc, x, fband, wtok, wqkv, wproj, gate, nw, w13, w2, consts, out):
    buf = nc.dram_tensor("slot_rows", (SLOTS, D), F32).ap()
    ybuf = nc.dram_tensor("slot_out", (SLOTS, D), F32).ap()
    with ExitStack() as keep:
        sb = lambda s, name, shape, dt=F32: s.enter_context(nc.sbuf_tensor(name, shape, dt))
        cst = sb(keep, "cst", [P, C_ALL])
        h1_all = sb(keep, "h1_all", [P, BATCHES * TILES, D])
        gidx_all = sb(keep, "gidx_all", [P, BATCHES * TILES * TOPK], U32)
        gap_all = sb(keep, "gap_all", [P, BATCHES * TILES])
        kept_all = sb(keep, "kept_all", [P, BATCHES * TILES * TOPK])
        tok_attention(nc, x, fband, wtok, wqkv, wproj, gate, consts, buf,
                      cst, h1_all, gidx_all, gap_all, kept_all)
        experts(nc, nw, w13, w2, buf, ybuf, cst)
        combine(nc, ybuf, out, cst, h1_all, gidx_all, gap_all, kept_all)


def tok_attention(nc, x, fband, wtok, wqkv, wproj, gate, consts, buf,
                  cst, h1_all, gidx_all, gap_all, kept_all):
    with ExitStack() as ctx:
        sb = lambda name, shape, dt=F32: ctx.enter_context(nc.sbuf_tensor(name, shape, dt))
        ps = lambda name, shape: ctx.enter_context(nc.psum_tensor(name, shape, F32))
        sem = lambda name: ctx.enter_context(nc.semaphore(name))

        wk = sb("wk", [P, KTILES, D])
        fb = sb("fb", [P, 9])
        xt = sb("xt", [P, XCHUNKS, SEQ])
        turn = sb("turn", [P, RING_T, SEQ])
        frac = sb("frac", [P, RING_T, SEQ])
        feat = sb("feat", [P, RING_F, SEQ])
        h = sb("h", [P, TILES, D])
        hT = sb("hT", [P, 2, SEQ])
        wqk = sb("wqk", [P, 2, 2 * GROUPS * HALF + D])
        qh = sb("qh", [P, GROUPS, SEQ], F32R)
        ql = sb("ql", [P, GROUPS, SEQ], F32R)
        kh = sb("kh", [HALF, SEQ], F32R)
        kx = sb("kx", [P, HEADS, SEQ], F32R)
        v = sb("v", [P, TILES, HEADS, 32])
        mx = sb("mx", [P, TILES, 32])
        pr = sb("pr", [P, 2, 4, SEQ])
        osb = sb("osb", [P, QUADS, SEQ])
        den = sb("den", [P, SEQ])
        onorm = sb("onorm", [P, QUADS, SEQ])
        wp = sb("wp", [P, QUADS, D])
        r = sb("r", [P, TILES, D])
        stats = sb("stats", [P, TILES, 6])
        mv = sb("mv", [P, TILES, 2])
        rstd = sb("rstd", [P, TILES])
        h1 = sb("h1", [P, TILES, D])
        ss = sb("ss", [P, TILES])
        rz = sb("rz", [P, TILES])
        z = sb("z", [P, TILES, D])
        gw = sb("gw", [HALF, 2, E])
        lg = sb("lg", [P, TILES, E])
        mx8 = sb("mx8", [P, TILES, 8])
        ix8 = sb("ix8", [P, TILES, 8], U32)
        idx = sb("idx", [P, TILES * TOPK])
        oh = sb("oh", [P, TILES * TOPK, E])
        both = sb("both", [P, TILES, E])
        run = sb("run", [P, TILES + 1, E])
        posx = sb("posx", [P, TILES, E])
        sel = sb("sel", [P, TILES * TOPK, E])
        pos = sb("pos", [P, TILES * TOPK])
        base = sb("base", [P, TILES * TOPK])
        far = sb("far", [P, TILES * TOPK])
        sidx_f = sb("sidx_f", [P, TILES * TOPK])
        sidx = sb("sidx", [P, TILES * TOPK], U32)

        tokacc = ps("tokacc", [P, TILES, 256])
        psA = [ps(f"psA{j}", [P, 512]) for j in range(2)]
        psB = [ps(f"psB{j}", [P, 512]) for j in range(2)]
        psO = ps("psO", [P, 512])
        psM = ps("psM", [P, 512])

        loaded = sem("loaded")
        x_in = [sem(f"x_in{c}") for c in range(XCHUNKS)]
        zeroed = sem("zeroed")
        preset = sem("preset")
        products = sem("products")
        sine_arg, cosine_arg = sem("sine_arg"), sem("cosine_arg")
        angle_free = sem("angle_free")
        feat_in, feat_free = sem("feat_in"), sem("feat_free")
        tok_done = sem("tok_done")
        h_in, h_free = sem("h_in"), sem("h_free")
        kh_free = sem("kh_free")
        hT_in = sem("hT_in")
        a_full, a_free = sem("a_full"), sem("a_free")
        b_full, b_free = sem("b_full"), sem("b_free")
        qh_in, ql_in, kh_in, kx_in = sem("qh_in"), sem("ql_in"), sem("kh_in"), sem("kx_in")
        v_in = sem("v_in")
        max_in = sem("max_in")
        mrow_full, mrow_in = sem("mrow_full"), sem("mrow_in")
        pr_in, pr_free = sem("pr_in"), sem("pr_free")
        o_full, o_free = sem("o_full"), sem("o_free")
        osb_in, onorm_in = sem("osb_in"), sem("onorm_in")
        var_in, rstd_in = sem("var_in"), sem("rstd_in")
        h1_in, h1_kept = sem("h1_in"), sem("h1_kept")
        ss_in, rz_in = sem("ss_in"), sem("rz_in")
        picks_in = sem("picks_in")
        z_in = sem("z_in")
        scattered = sem("scattered")
        dve_step = sem("dve_step")
        pool_step = sem("pool_step")
        DVE_STEPS, POOL_STEPS = 42, 2
        alone = sem("alone")

        ident = cst[:, C_ID:C_ID + P]
        block = ctx.enter_context(nc.Block())

        @block.sync
        def _(sp):
            for c in range(XCHUNKS):
                sp.dma_start(xt[:, c, :], x[0, :, c, :]).then_inc(x_in[c], 16)
            sp.dma_start(wk[:, :, :], wtok).then_inc(loaded, 16)
            sp.dma_start(wqk[0:HALF + 1, :, :], wqkv).then_inc(loaded, 16)
            sp.dma_start(wp[:, :, :], wproj).then_inc(loaded, 16)
            sp.dma_start(gw[:, :, :], gate).then_inc(loaded, 16)
            sp.wait_ge(preset, 1)
            zrows = buf.rearrange("(p s) d -> p (s d)", p=P)
            for j in range(8):
                n = SLOTS * D // P // 8
                sp.dma_start(zrows[:, j * n:(j + 1) * n],
                             ql[:, :, :].bitcast(F32).rearrange("p g s -> p (g s)")[:, 0:n]).then_inc(zeroed, 16)
            with sp.Fori(1, BATCHES) as bt:
                for c in range(XCHUNKS):
                    sp.wait_ge(products, (bt - 1) * ANGLES + min(6 * (c + 1), ANGLES))
                    sp.dma_start(xt[:, c, :], x[bass.ds(bt, 1), :, c, :].rearrange("a p s -> (a p) s")).then_inc(x_in[c], 16)

        @block.vector
        def _(dve):
            def angle_products(bt, a):
                c, f = (a // BANDS, a % BANDS) if a < 4 * BANDS else (4, BANDS + a - 4 * BANDS)
                if a % BANDS == 0:
                    dve.wait_ge(x_in[c], (bt + 1) * 16)
                dve.wait_ge(angle_free, bt * ANGLES + a + 1)
                s = a % RING_T
                nc.vector.tensor_scalar(turn[:, s, :], xt[:, c, :], fb[:, f:f + 1], ROUND, ALU.mult, ALU.add)
                nc.vector.tensor_scalar(frac[:, s, :], xt[:, c, :], fb[:, f:f + 1], None,
                                        ALU.mult).then_inc(products, 1)

            def angle(bt, a):
                if a == 0:
                    angle_products(bt, 0)
                s = a % RING_T
                dve.wait_ge(products, bt * ANGLES + a + 1)
                nc.vector.scalar_tensor_tensor(out=frac[:, s, :], in0=turn[:, s, :], scalar=ROUND,
                                               in1=frac[:, s, :], op0=ALU.subtract,
                                               op1=ALU.subtract).then_inc(sine_arg, 1)
                if a + 1 < ANGLES:
                    angle_products(bt, a + 1)
                dve.wait_ge(sine_arg, bt * ANGLES + a + 1)
                nc.vector.tensor_scalar(turn[:, s, :].bitcast(U32), frac[:, s, :].bitcast(U32), 0x7FFFFFFF, None,
                                        ALU.bitwise_and).then_inc(cosine_arg, 1)

            def attention(i, bt):
                ahead = lambda a: bt is not None and a + 2 < ANGLES and angle(bt, a + 2)
                steps = [0]

                def step(ins):
                    steps[0] += 1
                    ins.then_inc(dve_step, 1)

                def after_step():
                    dve.wait_ge(dve_step, i * DVE_STEPS + steps[0])

                def unit(u):
                    dve.wait_ge(a_full, i * A_UNITS + u + 1)
                    return psA[u % 2]

                if bt is not None:
                    angle(bt, 0)
                    angle(bt, 1)
                for k in range(2):
                    p = unit(k)
                    nc.vector.tensor_copy(hT[0:HALF, k, :], p[0:HALF, :]).then_inc(hT_in, 1)
                    dve.wait_ge(hT_in, 2 * i + k + 1)
                    dve.sem_inc(a_free, 1)
                for g in range(GROUPS):
                    p = unit(2 + g)
                    dve.wait_ge(qh_in, i * GROUPS + g + 1)
                    nc.vector.tensor_tensor(ql[0:HALF, g, :], p[0:HALF, :], qh[0:HALF, g, :].bitcast(F32),
                                            ALU.subtract).then_inc(ql_in, 1)
                    dve.wait_ge(ql_in, i * GROUPS + g + 1)
                    dve.sem_inc(a_free, 1)
                    if g in P_ANGLES:
                        ahead(P_ANGLES[g])
                for g in range(GROUPS):
                    p = unit(6 + g)
                    dve.wait_ge(kh_in, i * GROUPS + g + 1)
                    for j in range(3):
                        rows = slice(32 * j, 32 * j + 32)
                        last = nc.vector.scalar_tensor_tensor(
                            out=kx[rows, 3 * g + j, :], in0=kh[rows, :].bitcast(F32),
                            scalar=cst[rows, C_SEL:C_SEL + 1], in1=p[rows, :], op0=ALU.mult, op1=ALU.add)
                    last.then_inc(kx_in, 1)
                    dve.wait_ge(kx_in, i * GROUPS + g + 1)
                    dve.sem_inc(a_free, 1)
                    dve.sem_inc(kh_free, 1)
                    if GROUPS + g in P_ANGLES:
                        ahead(P_ANGLES[GROUPS + g])
                for u in range(HEADS * TILES):
                    hd, t = u // TILES, u % TILES
                    p = unit(10 + u)
                    last = nc.vector.tensor_reduce(mx[:, t, hd:hd + 1], p[:, :], AX.X, ALU.max)
                    last.then_inc(a_free, 1)
                    for a in a_angles(u):
                        ahead(a)
                dve.wait_ge(a_free, i * A_UNITS + 58 + 2)
                dve.sem_inc(max_in, 1)
                for q in range(QUADS):
                    dve.wait_ge(osb_in, i * QUADS + q + 1)
                    dve.sem_inc(alone, 1)
                    step(nc.vector.stream_shuffle(den[:, :], osb[:, q, :], [16 + m % 16 for m in range(32)]))
                    after_step()
                    step(nc.vector.reciprocal(den[:, :], den[:, :]))
                    after_step()
                    nc.vector.tensor_tensor(onorm[:, q, :], osb[:, q, :], den[:, :], ALU.mult).then_inc(onorm_in, 1)
                    dve.wait_ge(onorm_in, i * QUADS + q + 1)
                for t in range(TILES):
                    p = unit(58 + t)
                    nc.vector.tensor_tensor(r[:, t, :], p[:, 0:D], h[:, t, :], ALU.add).then_inc(a_free, 1)
                dve.wait_ge(a_free, i * A_UNITS + 62 + 2)
                for t in range(TILES):
                    step(nc.vector.bn_stats(stats[:, t, :], r[:, t, :]))
                after_step()
                dve.sem_inc(alone, 1)
                for t in range(TILES):
                    step(nc.vector.bn_aggr(mv[:, t, :], stats[:, t, :]))
                after_step()
                dve.sem_inc(var_in, 1)
                dve.sem_inc(h_free, 1)
                for a in T_ANGLES[0]:
                    ahead(a)
                dve.wait_ge(rstd_in, i + 1)
                dve.wait_ge(h1_kept, i + 1)
                for t in range(TILES):
                    last = nc.vector.tensor_scalar(h1[:, t, :], r[:, t, :], mv[:, t, 0:1], rstd[:, t:t + 1],
                                                   ALU.subtract, ALU.mult)
                last.then_inc(h1_in, 1)
                for k in range(2):
                    p = unit(62 + k)
                    nc.vector.tensor_copy(hT[0:HALF, k, :], p[0:HALF, :]).then_inc(a_free, 1)
                for a in T_ANGLES[1]:
                    ahead(a)
                dve.wait_ge(rz_in, i + 1)
                for t in range(TILES):
                    last = nc.vector.tensor_scalar(z[:, t, :], h1[:, t, :], rz[:, t:t + 1], 2.0, ALU.mult, ALU.mult)
                step(last)
                p = unit(64)
                step(nc.vector.tensor_copy(lg[:, :, :], p[:, 0:TILES * E].rearrange("p (t e) -> p t e", e=E)))
                after_step()
                dve.sem_inc(a_free, 1)
                for t in range(TILES):
                    step(nc.vector.max(mx8[:, t, :], lg[:, t, :]))
                after_step()
                dve.sem_inc(alone, 1)
                for t in range(TILES):
                    step(nc.vector.max_index(ix8[:, t, :], mx8[:, t, :], lg[:, t, :]))
                after_step()
                step(nc.vector.tensor_copy(idx[:, :].rearrange("p (t k) -> p t k", k=TOPK), ix8[:, :, 0:TOPK]))
                step(nc.vector.tensor_tensor(
                    gap_all[:, bass.ds(i * TILES, TILES)],
                    mx8[:, :, 1], mx8[:, :, 0], ALU.subtract))
                after_step()
                step(nc.vector.tensor_tensor(
                    oh[:, :, :], cst[:, C_IOTA:C_IOTA + E].unsqueeze(1).to_broadcast([P, TILES * TOPK, E]),
                    idx[:, :].unsqueeze(2).to_broadcast([P, TILES * TOPK, E]), ALU.is_equal))
                after_step()
                ohk = oh[:, :, :].rearrange("p (t k) e -> p t k e", k=TOPK)
                step(nc.vector.tensor_tensor(both[:, :, :], ohk[:, :, 0, :], ohk[:, :, 1, :], ALU.add))
                after_step()
                for t in range(TILES):
                    last = nc.vector.tensor_tensor(run[:, t + 1, :], run[:, t, :], both[:, t, :], ALU.add)
                    step(last)
                    after_step()
                dve.sem_inc(picks_in, 1)
                for a in T_ANGLES[2]:
                    ahead(a)
                p = unit(65)
                step(nc.vector.tensor_copy(posx[:, :, :], p[:, 0:TILES * E].rearrange("p (t e) -> p t e", e=E)))
                after_step()
                dve.sem_inc(a_free, 1)
                step(nc.vector.tensor_copy(run[:, 0, :], run[:, TILES, :]))
                step(nc.vector.tensor_tensor(
                    sel[:, :, :].rearrange("p (t k) e -> p t k e", k=TOPK), ohk,
                    posx[:, :, :].unsqueeze(2).to_broadcast([P, TILES, TOPK, E]), ALU.mult))
                step(nc.vector.tensor_scalar(base[:, :], idx[:, :], float(CAP), None, ALU.mult))
                after_step()
                step(nc.vector.tensor_reduce(pos[:, :], sel[:, :, :], AX.X, ALU.add))
                after_step()
                step(nc.vector.tensor_scalar(far[:, :], pos[:, :], float(CAP), float(SLOTS), ALU.is_ge, ALU.mult))
                step(nc.vector.tensor_scalar(kept_all[:, bass.ds(i * TILES * TOPK, TILES * TOPK)], pos[:, :],
                                             float(CAP), None, ALU.is_lt))
                step(nc.vector.tensor_tensor(sidx_f[:, :], pos[:, :], base[:, :], ALU.add))
                after_step()
                step(nc.vector.scalar_tensor_tensor(out=gidx_all[:, bass.ds(i * TILES * TOPK, TILES * TOPK)],
                                                    in0=pos[:, :], scalar=float(CAP - 1), in1=base[:, :],
                                                    op0=ALU.min, op1=ALU.add))
                step(nc.vector.tensor_tensor(sidx[:, :], sidx_f[:, :], far[:, :], ALU.add))
                after_step()
                dve.sem_inc(z_in, 1)
                for a in T_ANGLES[3]:
                    ahead(a)
                assert steps[0] == DVE_STEPS, steps[0]

            nc.vector.memset(ql[:, :, :].bitcast(F32), 0.0).then_inc(preset, 1)
            nc.vector.memset(kx[:, :, :].bitcast(F32), 0.0)
            nc.vector.memset(hT[HALF:P, :, :], 1.0)
            nc.vector.memset(v[:, :, :, :], 1.0)
            nc.vector.memset(run[:, 0, :], 0.0)
            nc.vector.memset(mx[:, :, :], 0.0).then_inc(preset, 1)
            dve.wait_ge(preset, 2)
            dve.wait_ge(loaded, 16 * 6)
            for hd in range(HEADS):
                last = nc.vector.tensor_copy(kx[HALF:P, hd, :],
                                             cst[HALF:P, C_ID + HALF + hd:C_ID + HALF + hd + 1].to_broadcast([P - HALF, SEQ]))
            last.then_inc(preset, 1)
            dve.sem_inc(a_free, 2)
            dve.sem_inc(h_free, 1)
            dve.sem_inc(kh_free, 1)
            for a in range(ANGLES):
                angle(0, a)
            dve.wait_ge(zeroed, 16 * 8)
            dve.wait_ge(preset, 3)
            with dve.Fori(0, BATCHES - 1) as i:
                attention(i, i + 1)
            attention(BATCHES - 1, None)

        @block.scalar
        def _(act):
            def features(bt, a):
                s = a % RING_T
                act.wait_ge(sine_arg, bt * ANGLES + a + 1)
                act.wait_ge(feat_free, bt * KTILES + 2 * a + 1)
                nc.scalar.activation(feat[:, 2 * a % RING_F, :], frac[:, s, :], ACT.Sin,
                                     scale=-TWO_PI).then_inc(feat_in, 1)
                act.wait_ge(cosine_arg, bt * ANGLES + a + 1)
                act.wait_ge(feat_free, bt * KTILES + 2 * a + 2)
                nc.scalar.activation(feat[:, (2 * a + 1) % RING_F, :], turn[:, s, :], ACT.Sin,
                                     bias=cst[:, C_HPI:C_HPI + 1], scale=-TWO_PI).then_inc(feat_in, 1)
                act.wait_ge(feat_in, bt * KTILES + 2 * a + 2)
                act.sem_inc(angle_free, 1)

            def attention(i, bt):
                ahead = lambda a: bt is not None and a + 2 < ANGLES and features(bt, a + 2)

                act.wait_ge(tok_done, i + 1)
                act.wait_ge(h_free, i + 1)
                nc.scalar.activation(h[:, :, :], tokacc[:, :, 0:D], ACT.Copy).then_inc(h_in, 1)
                if bt is not None:
                    features(bt, 0)
                    features(bt, 1)
                for g in range(GROUPS):
                    act.wait_ge(a_full, i * A_UNITS + 2 + g + 1)
                    nc.scalar.activation(qh[0:HALF, g, :], psA[g % 2][0:HALF, :], ACT.Copy).then_inc(qh_in, 1)
                    if g in P_ANGLES:
                        ahead(P_ANGLES[g])
                for g in range(GROUPS):
                    act.wait_ge(a_full, i * A_UNITS + 6 + g + 1)
                    act.wait_ge(kh_free, i * GROUPS + g + 1)
                    nc.scalar.activation(kh[:, :], psA[g % 2][0:HALF, :], ACT.Copy).then_inc(kh_in, 1)
                    if GROUPS + g in P_ANGLES:
                        ahead(P_ANGLES[GROUPS + g])
                for t in range(TILES):
                    act.wait_ge(b_full, i * B_UNITS + t + 1)
                    nc.scalar.activation(v[:, t, :, 0:HD],
                                         psB[t % 2][:, 0:D].rearrange("p (h d) -> p h d", d=HD),
                                         ACT.Copy).then_inc(b_free, 1)
                act.wait_ge(b_free, i * B_UNITS + TILES + 2)
                act.sem_inc(v_in, 1)
                for u in range(HEADS * TILES):
                    for a in a_angles(u):
                        ahead(a)
                act.wait_ge(mrow_full, i + 1)
                nc.scalar.activation(qh[HALF:P, :, :], psM[HALF:P, :].unsqueeze(1).to_broadcast([P - HALF, GROUPS, SEQ]),
                                     ACT.Copy, scale=-1.0).then_inc(mrow_in, 1)

                def leave(q):
                    act.wait_ge(o_full, i * QUADS + q + 1)
                    nc.scalar.activation(osb[:, q, :], psO[:, :], ACT.Copy).then_inc(osb_in, 1)
                    act.wait_ge(osb_in, i * QUADS + q + 1)
                    act.sem_inc(o_free, 1)

                for n in range(QUADS * TILES):
                    act.wait_ge(pr_free, i * QUADS * TILES + n + 1)
                    for j in range(4):
                        u = 4 + 4 * n + j
                        act.wait_ge(b_full, i * B_UNITS + u + 1)
                        nc.scalar.activation(pr[:, n % 2, j, :], psB[u % 2][:, :], ACT.Exp,
                                             scale=HD ** -0.5).then_inc(pr_in, 1)
                        act.wait_ge(pr_in, i * 4 * QUADS * TILES + 4 * n + j + 1)
                        act.sem_inc(b_free, 1)
                    if n % TILES == 0 and n > 0:
                        leave(n // TILES - 1)
                leave(QUADS - 1)
                for a in T_ANGLES[0]:
                    ahead(a)
                act.wait_ge(h1_in, i + 1)
                for t in range(TILES):
                    last = nc.scalar.activation(z[:, t, :], h1[:, t, :], ACT.Square, accum_out=ss[:, t:t + 1])
                last.then_inc(ss_in, 1)
                for gap in T_ANGLES[1:]:
                    for a in gap:
                        ahead(a)

            act.dma_start(cst[:, :], consts).then_inc(loaded, 16)
            act.dma_start(fb[:, :], fband).then_inc(loaded, 16)
            act.wait_ge(loaded, 16 * 6)
            act.sem_inc(angle_free, RING_T)
            act.sem_inc(b_free, 2)
            act.sem_inc(o_free, 1)
            for a in range(ANGLES):
                features(0, a)
            with act.Fori(0, BATCHES - 1) as i:
                attention(i, i + 1)
            attention(BATCHES - 1, None)

        @block.tensor
        def _(pe):
            def embed(bt, a):
                for kt in (2 * a, 2 * a + 1):
                    pe.wait_ge(feat_in, bt * KTILES + kt + 1)
                    if kt == 0 and not isinstance(bt, int):
                        pe.wait_ge(h_in, bt)
                    for t in range(TILES):
                        last = nc.tensor.matmul(tokacc[:, t, 0:D], feat[:, kt % RING_F, t * P:(t + 1) * P],
                                                wk[:, kt, :], start=(kt == 0 and t % 2 == 0),
                                                stop=(kt == KTILES - 1), skip_group_check=True)
                    last.then_inc(feat_free, 1)
                    if kt == KTILES - 1:
                        pe.wait_ge(feat_free, bt * KTILES + KTILES + RING_F)
                        pe.sem_inc(tok_done, 1)

            def attention(i, bt):
                angle = lambda a: bt is not None and embed(bt, a)

                def unit(u):
                    pe.wait_ge(a_free, i * A_UNITS + u + 1)
                    return psA[u % 2]

                def bunit(u):
                    pe.wait_ge(b_free, i * B_UNITS + u + 1)
                    return psB[u % 2]

                pe.wait_ge(h_in, i + 1)
                for k in range(2):
                    p = unit(k)
                    for t in range(TILES):
                        last = nc.tensor.transpose(p[0:HALF, t * P:(t + 1) * P],
                                                   h[:, t, k * HALF:(k + 1) * HALF], ident)
                    last.then_inc(a_full, 1)
                pe.wait_ge(hT_in, 2 * i + 2)
                for c in range(2 * GROUPS):
                    p = unit(2 + c)
                    cols = slice(c * HALF, (c + 1) * HALF)
                    nc.tensor.matmul(p[0:HALF, :], wqk[0:HALF + 1, 0, cols], hT[0:HALF + 1, 0, :], start=True, stop=False)
                    nc.tensor.matmul(p[0:HALF, :], wqk[0:HALF, 1, cols], hT[0:HALF, 1, :],
                                     start=False, stop=True).then_inc(a_full, 1)
                    if c in P_ANGLES:
                        angle(P_ANGLES[c])
                vcols = slice(2 * GROUPS * HALF, 2 * GROUPS * HALF + D)
                for t in range(TILES):
                    p = bunit(t)
                    rows = slice(t * P, (t + 1) * P)
                    nc.tensor.matmul(p[:, 0:D], hT[0:HALF + 1, 0, rows], wqk[0:HALF + 1, 0, vcols], start=True, stop=False)
                    nc.tensor.matmul(p[:, 0:D], hT[0:HALF, 1, rows], wqk[0:HALF, 1, vcols],
                                     start=False, stop=True).then_inc(b_full, 1)
                pe.wait_ge(kx_in, i * GROUPS + GROUPS)
                for u in range(HEADS * TILES):
                    hd, t = u // TILES, u % TILES
                    p = unit(10 + u)
                    nc.tensor.matmul(p[:, :], qh[0:HALF, hd // 3, t * P:(t + 1) * P], kx[0:HALF, hd, :],
                                     start=True, stop=True).then_inc(a_full, 1)
                    for a in a_angles(u):
                        angle(a)
                pe.wait_ge(max_in, i + 1)
                for t in range(TILES):
                    last = nc.tensor.matmul(psM[HALF:P, t * P:(t + 1) * P], mx[:, t, :], ident, start=True, stop=True)
                last.then_inc(mrow_full, 1)
                pe.wait_ge(mrow_in, i + 1)
                pe.wait_ge(ql_in, i * GROUPS + GROUPS)

                def weigh(n):
                    q, t = n // TILES, n % TILES
                    pe.wait_ge(pr_in, i * 4 * QUADS * TILES + 4 * n + 4)
                    if t == 0:
                        pe.wait_ge(o_free, i * QUADS + q + 1)
                    if n == 0:
                        pe.wait_ge(v_in, i + 1)
                    for j in range(4):
                        last = nc.tensor.matmul(psO[32 * j:32 * j + 32, :], v[:, t, 4 * q + j, :], pr[:, n % 2, j, :],
                                                start=(t == 0), stop=(t == TILES - 1))
                    last.then_inc(pr_free, 1)
                    if t == TILES - 1:
                        pe.wait_ge(pr_free, i * QUADS * TILES + n + 1 + 2)
                        pe.sem_inc(o_full, 1)

                for n in range(QUADS * TILES):
                    for j in range(4):
                        hd, t = 4 * (n // TILES) + j, n % TILES
                        p = bunit(4 + 4 * n + j)
                        keys = kx[:, hd, t * P:(t + 1) * P]
                        nc.tensor.matmul(p[:, :], keys, qh[:, hd // 3, :], start=True, stop=False)
                        nc.tensor.matmul(p[:, :], keys, ql[:, hd // 3, :], start=False, stop=True).then_inc(b_full, 1)
                    if n:
                        weigh(n - 1)
                weigh(QUADS * TILES - 1)
                pe.wait_ge(onorm_in, i * QUADS + QUADS)
                for t in range(TILES):
                    p = unit(58 + t)
                    for q in range(QUADS):
                        last = nc.tensor.matmul(p[:, 0:D], onorm[:, q, t * P:(t + 1) * P], wp[:, q, :],
                                                start=(q == 0), stop=(q == QUADS - 1))
                    last.then_inc(a_full, 1)
                for a in T_ANGLES[0]:
                    angle(a)
                pe.wait_ge(h1_in, i + 1)
                for k in range(2):
                    p = unit(62 + k)
                    for t in range(TILES):
                        last = nc.tensor.transpose(p[0:HALF, t * P:(t + 1) * P],
                                                   h1[:, t, k * HALF:(k + 1) * HALF], ident)
                    last.then_inc(a_full, 1)
                for a in T_ANGLES[1]:
                    angle(a)
                p = unit(64)
                pe.wait_ge(a_free, i * A_UNITS + 64 + 2)
                for t in range(TILES):
                    for k in range(2):
                        last = nc.tensor.matmul(p[:, t * E:(t + 1) * E], hT[0:HALF, k, t * P:(t + 1) * P], gw[:, k, :],
                                                start=(k == 0), stop=(k == 1))
                last.then_inc(a_full, 1)
                for a in T_ANGLES[2]:
                    angle(a)
                pe.wait_ge(picks_in, i + 1)
                p = unit(65)
                nc.tensor.matmul(p[:, 0:TILES * E], cst[:, C_UP:C_UP + P],
                                 both[:, :, :].rearrange("p t e -> p (t e)"), start=True, stop=False)
                nc.tensor.matmul(p[:, 0:TILES * E], cst[:, C_ONE:C_ONE + P],
                                 run[:, 0:TILES, :].rearrange("p t e -> p (t e)"), start=False, stop=True).then_inc(a_full, 1)
                for a in T_ANGLES[3]:
                    angle(a)

            pe.wait_ge(loaded, 16 * 6)
            pe.wait_ge(preset, 3)
            pe.sem_inc(feat_free, RING_F)
            pe.sem_inc(pr_free, 2)
            for a in range(ANGLES):
                embed(0, a)
            with pe.Fori(0, BATCHES - 1) as i:
                attention(i, i + 1)
            attention(BATCHES - 1, None)

        @block.gpsimd
        def _(pool):
            nhalf = cst[:, C_NHALF:C_NHALF + TILES]
            pool.wait_ge(loaded, 16 * 6)
            pool.sem_inc(h1_kept, 1)
            with pool.Fori(0, BATCHES) as i:
                pool.wait_ge(var_in, i + 1)
                pool.sem_inc(alone, 1)
                nc.gpsimd.tensor_scalar(rstd[:, :], mv[:, :, 1], 1e-5, None, ALU.add).then_inc(pool_step, 1)
                pool.wait_ge(pool_step, i * POOL_STEPS + 1)
                nc.gpsimd.tensor_tensor(rstd[:, :], rstd[:, :], nhalf, ALU.pow).then_inc(rstd_in, 1)
                pool.wait_ge(ss_in, i + 1)
                pool.sem_inc(alone, 1)
                nc.gpsimd.tensor_scalar(rz[:, :], ss[:, :], 4.0 / D, 1e-6, ALU.mult, ALU.add).then_inc(pool_step, 1)
                pool.wait_ge(pool_step, i * POOL_STEPS + 2)
                nc.gpsimd.tensor_tensor(rz[:, :], rz[:, :], nhalf, ALU.pow).then_inc(rz_in, 1)
                nc.gpsimd.tensor_copy(h1_all[:, bass.ds(i * TILES, TILES), :], h1[:, :, :])
                pool.wait_ge(z_in, i + 1)
                pool.sem_inc(alone, 1)
                for t in range(TILES):
                    for k in range(TOPK):
                        c = t * TOPK + k
                        nc.gpsimd.indirect_dma_start(
                            out=buf, out_offset=bass.IndirectOffsetOnAxis(ap=sidx[:, c:c + 1], axis=0),
                            in_=z[:, t, :], in_offset=None, bounds_check=SLOTS - 1,
                            oob_is_err=False).then_inc(scattered, 16)
                pool.wait_ge(scattered, i * 16 * TILES * TOPK + 16 * TILES * TOPK)
                pool.sem_inc(h1_kept, 1)


def experts(nc, nw, w13, w2, buf, ybuf, cst):
    NG, GS = 5, 2 * P
    CH = HID // P
    with ExitStack() as ctx:
        sb = lambda name, shape, dt=F32: ctx.enter_context(nc.sbuf_tensor(name, shape, dt))
        ps = lambda name, shape: ctx.enter_context(nc.psum_tensor(name, shape, F32))
        sem = lambda name: ctx.enter_context(nc.semaphore(name))
        nws = sb("nws", [HALF, 2, E])
        nwp = sb("nwp", [HALF, 2, 2])
        w13r = [sb(f"w13r{p}", [HALF, 2, 2 * HID]) for p in range(2)]
        w2r = [sb(f"w2r{p}", [P, CH, D]) for p in range(2)]
        w13h = [sb(f"w13h{p}", [HALF, 2, 2 * HID], F32R) for p in range(2)]
        w13l = [sb(f"w13l{p}", [HALF, 2, 2 * HID], F32R) for p in range(2)]
        w2h = [sb(f"w2h{p}", [P, CH, D], F32R) for p in range(2)]
        w2l = [sb(f"w2l{p}", [P, CH, D], F32R) for p in range(2)]
        zin = [sb(f"zin{s}", [P, 2, D]) for s in range(2)]
        zh = [sb(f"zh{s}", [HALF, 2, GS], F32R) for s in range(2)]
        zl = [sb(f"zl{s}", [HALF, 2, GS], F32R) for s in range(2)]
        sg = sb("sg", [P, CH, GS])
        av = sb("av", [P, CH, GS])
        ah = [sb(f"ah{s}", [P, CH, GS], F32R) for s in range(2)]
        al = [sb(f"al{s}", [P, CH, GS], F32R) for s in range(2)]
        ysb = [sb(f"ysb{s}", [P, 2, D]) for s in range(2)]
        psT = [ps(f"psT{s}", [P, 2, GS]) for s in range(2)]
        psG = [ps(f"psG{c}", [P, 2, GS]) for c in range(CH)]
        psY = [ps(f"psY{s}", [P, 2, 256]) for s in range(2)]

        nw_in = sem("nw_in")
        w_in = [sem(f"w_in{p}") for p in range(2)]
        z_got = [sem(f"z_got{s}") for s in range(2)]
        zT_full = sem("zT_full")
        zh_in, zl_in = sem("zh_in"), sem("zl_in")
        nwp_in = sem("nwp_in")
        wh_in, wl_in = sem("wh_in"), sem("wl_in")
        g_full, g_free = sem("g_full"), sem("g_free")
        sg_in, av_in, ah_in, al_in = sem("sg_in"), sem("av_in"), sem("ah_in"), sem("al_in")
        mm1_done = sem("mm1_done")
        raw_free, w_free = sem("raw_free"), sem("w_free")
        y_full, y_in = sem("y_full"), sem("y_in")
        y_out = [sem(f"y_out{s}") for s in range(2)]
        ident = cst[:, C_ID:C_ID + P]
        N = NG * E
        block = ctx.enter_context(nc.Block())

        @block.sync
        def _(sp):
            sp.dma_start(nws[:, :, :], nw).then_inc(nw_in, 16)
            with sp.Fori(0, E // 2) as ep:
                for p in range(2):
                    sp.wait_ge(raw_free, ep * 2 + 1)
                    sp.dma_start(w13r[p][:, :, :], w13[bass.ds(2 * ep + p, 1)].rearrange("a p k n -> (a p) k n")).then_inc(w_in[p], 16)
                    sp.dma_start(w2r[p][:, :, :], w2[bass.ds(2 * ep + p, 1)].rearrange("a p k n -> (a p) k n")).then_inc(w_in[p], 16)
                    for g in range(NG):
                        m = NG * p + g
                        sp.wait_ge(zT_full, ep * 10 + m + 1)
                        row = (2 * ep + p) * CAP + g * GS
                        sp.dma_start(zin[m % 2][:, :, :], buf[bass.ds(row, GS), :].rearrange("(s p) d -> p s d", p=P)).then_inc(z_got[m % 2], 16)

        @block.tensor
        def _(pe):
            def turn(ep, m):
                pe.wait_ge(z_got[m % 2], (ep * 5 + m // 2 + 1) * 16)
                pe.wait_ge(zl_in, ep * 10 + m + 1)
                for k in range(2):
                    for s in range(2):
                        last = nc.tensor.transpose(psT[m % 2][0:HALF, k, s * P:(s + 1) * P],
                                                   zin[m % 2][:, s, k * HALF:(k + 1) * HALF], ident)
                last.then_inc(zT_full, 1)

            def hidden(ep, m):
                p, g = m // NG, m % NG
                pe.wait_ge(zl_in, ep * 10 + m + 1 + 2)
                if g == 0:
                    pe.wait_ge(wl_in, (2 * ep + p) * 3 + 3)
                for c in range(CH):
                    pe.wait_ge(g_free, ep * 10 * CH + m * CH + c + 1)
                    for j in range(2):
                        cols = slice(j * HID + c * P, j * HID + (c + 1) * P)
                        terms = [(w, zz, k) for w, zz in ((w13h, zh), (w13l, zh), (w13h, zl)) for k in range(2)]
                        for x, (w, zz, k) in enumerate(terms):
                            last = nc.tensor.matmul(psG[c][:, j, :], w[p][:, k, cols], zz[m % 2][:, k, :],
                                                    start=(x == 0), stop=(x == 5))
                    last.then_inc(g_full, 1)

            def output(ep, m):
                p = (m // NG) % 2
                pe.wait_ge(al_in, ep * 10 * CH + (m + 1) * CH + 1)
                pe.wait_ge(y_in, ep * 10 + m + 1)
                for s in range(2):
                    terms = [(a, w, c) for c in range(CH) for a, w in ((ah, w2h), (ah, w2l), (al, w2h))]
                    for x, (a, w, c) in enumerate(terms):
                        last = nc.tensor.matmul(psY[m % 2][:, s, 0:D], a[m % 2][:, c, s * P:(s + 1) * P], w[p][:, c, :],
                                                start=(x == 0), stop=(x == len(terms) - 1))
                last.then_inc(y_full, 1)

            pe.sem_inc(zT_full, 2)
            pe.sem_inc(w_free, 1)
            with pe.Fori(0, E // 2) as ep:
                turn(ep, 0)
                for m in range(2 * NG):
                    if m + 1 < 2 * NG:
                        turn(ep, m + 1)
                    hidden(ep, m)
                    if m:
                        output(ep, m - 1)
                output(ep, 2 * NG - 1)
                pe.wait_ge(y_full, ep * 10 + 10)
                pe.sem_inc(w_free, 1)

        def split_step(p):
            return [(w13r[p][:, k, :], w13h[p][:, k, :], w13l[p][:, k, :], nwp[:, k, p:p + 1]) for k in range(2)] + \
                   [(w2r[p][:, :, :], w2h[p][:, :, :], w2l[p][:, :, :], 1.0)]

        @block.scalar
        def _(act):
            def split(ep, p, x):
                raw, hi, _, scale = split_step(p)[x]
                if x == 0:
                    act.wait_ge(w_in[p], (ep + 1) * 32)
                    act.wait_ge(nwp_in, ep + 1)
                    act.wait_ge(w_free, ep + 1)
                nc.scalar.activation(hi, raw, ACT.Copy, scale=scale).then_inc(wh_in, 1)

            def group(ep, m):
                act.wait_ge(zT_full, ep * 10 + m + 1 + 2)
                if m >= 2:
                    act.wait_ge(g_full, ep * 10 * CH + (m - 1) * CH)
                nc.scalar.activation(zh[m % 2][:, :, :], psT[m % 2][0:HALF, :, :], ACT.Copy).then_inc(zh_in, 1)

            def high(ep, m, c):
                act.wait_ge(av_in, ep * 10 * CH + m * CH + c + 1)
                if c == 0 and m >= 2:
                    act.wait_ge(y_full, ep * 10 + m - 1)
                nc.scalar.activation(ah[m % 2][:, c, :], av[:, c, :], ACT.Copy).then_inc(ah_in, 1)

            def leave(ep, m):
                act.wait_ge(y_full, ep * 10 + m + 1)
                act.wait_ge(y_out[m % 2], (ep * 5 + m // 2 + 1) * 16)
                nc.scalar.activation(ysb[m % 2][:, :, :], psY[m % 2][:, :, 0:D], ACT.Copy).then_inc(y_in, 1)
                act.wait_ge(y_in, ep * 10 + m + 1 + 2)
                p, g = m // NG, m % NG
                row = (2 * ep + p) * CAP + g * GS
                act.dma_start(ybuf[bass.ds(row, GS), :].rearrange("(s p) d -> p s d", p=P),
                              ysb[m % 2][:, :, :]).then_inc(y_out[m % 2], 16)

            act.sem_inc(y_in, 2)
            act.sem_inc(y_out[0], 16)
            act.sem_inc(y_out[1], 16)
            with act.Fori(0, E // 2) as ep:
                for x in range(3):
                    split(ep, 0, x)
                group(ep, 0)
                for m in range(2 * NG):
                    if m + 1 < 2 * NG:
                        group(ep, m + 1)
                    for c in range(CH):
                        act.wait_ge(g_full, ep * 10 * CH + m * CH + c + 1)
                        if c == 0:
                            act.wait_ge(g_free, ep * 10 * CH + m * CH + CH)
                        nc.scalar.activation(sg[:, c, :], psG[c][:, 0, :], ACT.Silu).then_inc(sg_in, 1)
                        if c:
                            high(ep, m, c - 1)
                    high(ep, m, CH - 1)
                    if m:
                        leave(ep, m - 1)
                    if 0 < m <= 3:
                        split(ep, 1, m - 1)
                leave(ep, 2 * NG - 1)
            act.wait_ge(y_out[0], (N // 2 + 1) * 16)
            act.wait_ge(y_out[1], (N // 2 + 1) * 16)

        @block.vector
        def _(dve):
            def split(ep, p, x):
                e3 = (2 * ep + p) * 3
                raw, hi, lo, scale = split_step(p)[x]
                dve.wait_ge(wh_in, e3 + x + 1)
                nc.vector.scalar_tensor_tensor(out=lo, in0=raw, scalar=scale, in1=hi.bitcast(F32), op0=ALU.mult,
                                               op1=ALU.subtract).then_inc(wl_in, 1)

            def group(ep, m):
                dve.wait_ge(zh_in, ep * 10 + m + 1)
                nc.vector.tensor_tensor(zl[m % 2][:, :, :], psT[m % 2][0:HALF, :, :], zh[m % 2][:, :, :].bitcast(F32),
                                        ALU.subtract).then_inc(zl_in, 1)

            def low(ep, m, c):
                dve.wait_ge(ah_in, ep * 10 * CH + m * CH + c + 1)
                nc.vector.tensor_tensor(al[m % 2][:, c, :], av[:, c, :], ah[m % 2][:, c, :].bitcast(F32),
                                        ALU.subtract).then_inc(al_in, 1)

            dve.wait_ge(nw_in, 16)
            dve.sem_inc(g_free, CH)
            dve.sem_inc(al_in, 1)
            dve.sem_inc(zl_in, 2)
            dve.sem_inc(raw_free, 1)
            with dve.Fori(0, E // 2) as ep:
                dve.wait_ge(raw_free, 2 * ep + 1)
                nc.vector.tensor_copy(nwp[:, :, :], nws[:, :, bass.ds(2 * ep, 2)]).then_inc(nwp_in, 1)
                dve.wait_ge(nwp_in, ep + 1)
                for x in range(3):
                    split(ep, 0, x)
                dve.wait_ge(wl_in, 6 * ep + 3)
                dve.sem_inc(raw_free, 1)
                group(ep, 0)
                for m in range(2 * NG):
                    if m + 1 < 2 * NG:
                        group(ep, m + 1)
                    for c in range(CH):
                        n = m * CH + c
                        dve.wait_ge(sg_in, ep * 10 * CH + n + 1)
                        if c == 0:
                            dve.wait_ge(al_in, ep * 10 * CH + m * CH + 1)
                        nc.vector.tensor_tensor(av[:, c, :], sg[:, c, :], psG[c][:, 1, :], ALU.mult).then_inc(av_in, 1)
                        dve.wait_ge(av_in, ep * 10 * CH + n + 1)
                        dve.sem_inc(g_free, 1)
                        if c:
                            low(ep, m, c - 1)
                    low(ep, m, CH - 1)
                    if 0 < m <= 3:
                        split(ep, 1, m - 1)
                    if m == 3:
                        dve.wait_ge(wl_in, 6 * ep + 6)
                        dve.sem_inc(raw_free, 1)


def combine(nc, ybuf, out, cst, h1_all, gidx_all, gap_all, kept_all):
    with ExitStack() as ctx:
        sb = lambda name, shape, dt=F32: ctx.enter_context(nc.sbuf_tensor(name, shape, dt))
        sem = lambda name: ctx.enter_context(nc.semaphore(name))
        NT = BATCHES * TILES
        second = sb("second", [P, NT])
        total = sb("total", [P, NT])
        cw = sb("cw", [P, NT, TOPK])
        keepw = sb("keepw", [P, NT])
        gix = sb("gix", [P, 2, TILES * TOPK], U32)
        cws = sb("cws", [P, TILES, TOPK])
        kws = sb("kws", [P, TILES])
        f = [[sb(f"f{s}{c}", [P, D]) for c in range(TILES * TOPK)] for s in range(2)]
        r = sb("r2", [P, TILES, D])
        stats = sb("stats2", [P, TILES, 6])
        mv = sb("mv2", [P, TILES, 2])
        rstd = sb("rstd2", [P, TILES])
        res = sb("res", [P, TILES, D])
        exp_in = sem("exp_in")
        alone = sem("alone2")
        got = [[sem(f"got{s}{t}") for t in range(TILES)] for s in range(2)]
        gix_in = sem("gix_in")
        step_ = sem("combine_step")
        var_in, rstd_in, pool_step = sem("var2_in"), sem("rstd2_in"), sem("pool2_step")
        res_in, written = sem("res_in"), sem("written")
        block = ctx.enter_context(nc.Block())

        @block.scalar
        def _(act):
            nc.scalar.activation(second[:, :], gap_all[:, :], ACT.Exp).then_inc(exp_in, 1)

        @block.gpsimd
        def _(pool):
            def gathers(i, s):
                nc.gpsimd.tensor_copy(gix[:, s, :], gidx_all[:, bass.ds(i * TILES * TOPK, TILES * TOPK)]).then_inc(gix_in, 1)
                pool.wait_ge(gix_in, i + 1)
                pool.sem_inc(alone, 1)
                for t in range(TILES):
                    for k in range(TOPK):
                        c = t * TOPK + k
                        nc.gpsimd.indirect_dma_start(
                            out=f[s][c][:, :], out_offset=None, in_=ybuf,
                            in_offset=bass.IndirectOffsetOnAxis(ap=gix[:, s, c:c + 1], axis=0),
                            bounds_check=SLOTS - 1, oob_is_err=False).then_inc(got[s][t], 16)

            def deviations(i):
                pool.wait_ge(var_in, i + 1)
                pool.sem_inc(alone, 1)
                nc.gpsimd.tensor_scalar(rstd[:, :], mv[:, :, 1], 1e-5, None, ALU.add).then_inc(pool_step, 1)
                pool.wait_ge(pool_step, i + 1)
                nc.gpsimd.tensor_tensor(rstd[:, :], rstd[:, :], cst[:, C_NHALF:C_NHALF + TILES], ALU.pow).then_inc(rstd_in, 1)

            gathers(0, 0)
            with pool.Fori(0, BATCHES // 2 - 1) as j:
                gathers(2 * j + 1, 1)
                deviations(2 * j)
                gathers(2 * j + 2, 0)
                deviations(2 * j + 1)
            gathers(BATCHES - 1, 1)
            deviations(BATCHES - 2)
            deviations(BATCHES - 1)

        @block.vector
        def _(dve):
            dve.wait_ge(exp_in, 1)
            s = [0]

            def go(ins):
                s[0] += 1
                ins.then_inc(step_, 1)
                dve.wait_ge(step_, s[0])

            go(nc.vector.tensor_scalar(total[:, :], second[:, :], 1.0, None, ALU.add))
            go(nc.vector.reciprocal(total[:, :], total[:, :]))
            kept = kept_all[:, :].rearrange("p (t k) -> p t k", k=TOPK)
            go(nc.vector.tensor_tensor(cw[:, :, 0], total[:, :], kept[:, :, 0], ALU.mult))
            go(nc.vector.tensor_tensor(cw[:, :, 1], total[:, :], second[:, :], ALU.mult))
            go(nc.vector.tensor_tensor(cw[:, :, 1], cw[:, :, 1], kept[:, :, 1], ALU.mult))
            go(nc.vector.scalar_tensor_tensor(out=keepw[:, :], in0=cw[:, :, 0], scalar=1.0, in1=cw[:, :, 1],
                                              op0=ALU.add, op1=ALU.add))
            s0 = s[0]
            PER = 2 + 4 * TILES + TILES
            def rows(i, j, b):
                n = [0]

                def did(ins):
                    n[0] += 1
                    ins.then_inc(step_, 1)

                def upto(k):
                    dve.wait_ge(step_, i * PER + s0 + k)

                did(nc.vector.tensor_copy(cws[:, :, :], cw[:, bass.ds(i * TILES, TILES), :]))
                did(nc.vector.tensor_copy(kws[:, :], keepw[:, bass.ds(i * TILES, TILES)]))
                upto(2)
                for t in range(TILES):
                    did(nc.vector.tensor_scalar(r[:, t, :], h1_all[:, bass.ds(i * TILES + t, 1), :].rearrange("p a d -> p (a d)"),
                                                kws[:, t:t + 1], None, ALU.mult))
                for k in range(TOPK):
                    for t in range(TILES):
                        if k == 0:
                            dve.wait_ge(got[b][t], (j + 1) * 16 * TOPK)
                        upto(n[0] - TILES + 1)
                        did(nc.vector.scalar_tensor_tensor(out=r[:, t, :], in0=f[b][t * TOPK + k][:, :],
                                                           scalar=cws[:, t, k:k + 1], in1=r[:, t, :],
                                                           op0=ALU.mult, op1=ALU.add))
                for t in range(TILES):
                    upto(n[0] - TILES + 1)
                    did(nc.vector.bn_stats(stats[:, t, :], r[:, t, :]))
                for t in range(TILES):
                    if t == 0:
                        upto(n[0])
                        dve.sem_inc(alone, 1)
                    did(nc.vector.bn_aggr(mv[:, t, :], stats[:, t, :]))
                upto(n[0])
                assert n[0] == PER, n[0]
                dve.sem_inc(var_in, 1)
                dve.wait_ge(rstd_in, i + 1)
                dve.wait_ge(written, i * 16 + 16)
                for t in range(TILES):
                    last = nc.vector.tensor_scalar(res[:, t, :], r[:, t, :], mv[:, t, 0:1], rstd[:, t:t + 1],
                                                   ALU.subtract, ALU.mult)
                last.then_inc(res_in, 1)
                dve.wait_ge(res_in, i + 1)

            with dve.Fori(0, BATCHES // 2) as j:
                rows(2 * j, j, 0)
                rows(2 * j + 1, j, 1)

        @block.sync
        def _(sp):
            sp.sem_inc(written, 16)
            with sp.Fori(0, BATCHES) as i:
                sp.wait_ge(res_in, i + 1)
                sp.dma_start(out[bass.ds(i, 1)].rearrange("a (t p) d -> p (a t) d", p=P), res[:, :, :]).then_inc(written, 16)
            sp.wait_ge(written, BATCHES * 16 + 16)


def _layout(x, L0_tok_freq_bands, L0_tok_W, L0_attn_w_qkv, L0_attn_b_qkv, L0_attn_w_proj, L0_attn_b_proj,
            L0_ffn_gate_w, L0_ffn_w13, L0_ffn_w2, L0_ffn_norm_w):
    import numpy as np
    a = {}
    xv = np.asarray(x).reshape(BATCHES, SEQ, VALUES).transpose(0, 2, 1)
    xv = np.concatenate([xv, xv[:, 4 * P:]], axis=1).reshape(BATCHES, XCHUNKS, P, SEQ)
    a["x"] = np.ascontiguousarray(xv.transpose(0, 2, 1, 3))
    fr = np.asarray(L0_tok_freq_bands)
    f = np.empty((P, 9), fr.dtype)
    f[:, 0:6] = fr
    for m in range(3):
        f[:64, 6 + m], f[64:, 6 + m] = fr[2 * m], fr[2 * m + 1]
    a["fband"] = f
    w = np.asarray(L0_tok_W).T.reshape(VALUES, 2, BANDS, D)
    wk = np.empty((KTILES, P, D), w.dtype)
    for n in range(ANGLES):
        for s in range(2):
            if n < 4 * BANDS:
                c, b = n // BANDS, n % BANDS
                wk[2 * n + s] = w[c * P:(c + 1) * P, s, b]
            else:
                m = n - 4 * BANDS
                wk[2 * n + s, :64] = w[4 * P:, s, 2 * m]
                wk[2 * n + s, 64:] = w[4 * P:, s, 2 * m + 1]
    a["wtok"] = np.ascontiguousarray(wk.transpose(1, 0, 2))
    wq, bq = np.asarray(L0_attn_w_qkv), np.asarray(L0_attn_b_qkv)
    cols = [np.repeat(np.arange(HEADS * HD).reshape(HEADS, 1, HD) + s * D, 2, axis=1).ravel() for s in range(2)]
    cols = np.concatenate(cols + [np.arange(D) + 2 * D])
    wt = np.zeros((HALF + 1, 2, len(cols)), wq.dtype)
    wt[:HALF, 0], wt[:HALF, 1], wt[HALF, 0] = wq[cols, :HALF].T, wq[cols, HALF:].T, bq[cols]
    a["wqkv"] = wt
    wp, bp = np.asarray(L0_attn_w_proj), np.asarray(L0_attn_b_proj)
    pw = np.zeros((QUADS, 4, 32, D), wp.dtype)
    pw[:, :, :HD] = wp.T.reshape(QUADS, 4, HD, D)
    pw[0, 0, HD] = bp
    a["wproj"] = np.ascontiguousarray(pw.reshape(QUADS, P, D).transpose(1, 0, 2))
    a["gate"] = np.ascontiguousarray(np.asarray(L0_ffn_gate_w).T.reshape(2, HALF, E).transpose(1, 0, 2))
    a["nw"] = np.ascontiguousarray(np.asarray(L0_ffn_norm_w).T.reshape(2, HALF, E).transpose(1, 0, 2))
    a["w13"] = np.ascontiguousarray(np.asarray(L0_ffn_w13).transpose(0, 2, 1).reshape(E, 2, HALF, 2 * HID).transpose(0, 2, 1, 3))
    a["w2"] = np.ascontiguousarray(np.asarray(L0_ffn_w2).transpose(0, 2, 1).reshape(E, HID // P, P, D).transpose(0, 2, 1, 3))
    c = np.zeros((P, C_ALL), np.float32)
    c[:, C_ID:C_ID + P] = np.eye(P)
    c[:, C_UP:C_UP + P] = np.triu(np.ones((P, P)), 1)
    c[:, C_ONE:C_ONE + P] = 1.0
    c[:, C_IOTA:C_IOTA + E] = np.arange(E)
    c[:, C_SEL] = np.where(np.arange(P) % 32 < HD, 0.0, -1.0)
    c[:, C_NHALF:C_NHALF + TILES] = -0.5
    c[:, C_HPI] = HALF_PI
    a["consts"] = c
    return a


def kernel(**inputs):
    import numpy as _np
    import concourse.bacc as _bacc
    from concourse import mybir as _mybir
    from concourse.bass_utils import run_bass_kernel_spmd as _run

    nc = _bacc.Bacc("TRN2", target_bir_lowering=False, num_devices=1)
    laid = _layout(**inputs)
    aps = {n: nc.dram_tensor(f"in_{n}", a.shape, _mybir.dt.from_np(a.dtype), kind="ExternalInput").ap()
           for n, a in laid.items()}
    out = nc.dram_tensor("out_0_dram", (BATCHES, SEQ, D), _mybir.dt.float32, kind="ExternalOutput").ap()
    build(nc, out=out, **aps)
    r = _run(nc, [{f"in_{n}": a for n, a in laid.items()}], core_ids=[0])
    return r.results[0]["out_0_dram"]
```

```python
from contextlib import ExitStack

import concourse.bass as bass
from concourse import mybir

F32 = mybir.dt.float32
F32R = mybir.dt.float32r
U32 = mybir.dt.uint32
ALU = mybir.AluOpType
ACT = mybir.ActivationFunctionType
AX = mybir.AxisListType

P = 128
BATCHES = 8
SEQ = 512
TILES = SEQ // P
TOKENS = BATCHES * SEQ
D = 192
HALF = D // 2
VALUES = 3 * D
BANDS = 6
XCHUNKS = 5
ANGLES = 4 * BANDS + BANDS // 2
KTILES = 2 * ANGLES
HEADS, HD = 12, 16
GROUPS = 4
QUADS = 3
E, TOPK, HID = 8, 2, 512
CAP = 1280
SLOTS = E * CAP
ROW = D + 1
NOWHERE = 1 << 20
ROUND = 12582912.0
TWO_PI = 6.283185
HALF_PI = 1.5707963

RING_F, RING_T = 6, 3
WPIECES = 9

P_UNITS, TAIL_UNITS, A_UNITS, B_UNITS = 5, 4, 24, 24
UNITS = P_UNITS + TAIL_UNITS + A_UNITS + 1 + B_UNITS
NPV = QUADS * TILES

T_ANGLES = [[0, 1], [2], [3], []]
A_FIRST = 4


def a_angles(u):
    n = ANGLES - A_FIRST
    return [A_FIRST + k for k in range(u * n // A_UNITS, (u + 1) * n // A_UNITS)]


def place(i, u):
    if isinstance(i, int) and i == 0:
        return (1 + u) % 2, (1 + u) // 2
    return (u + 1) % 2, UNITS // 2 * i + (1 - TAIL_UNITS + u) // 2


def first_a(i):
    return P_UNITS + (0 if isinstance(i, int) and i == 0 else TAIL_UNITS)


def first_b(i, more):
    return first_a(i) + A_UNITS + (1 if more else 0)


C_ID, C_UP, C_ONE, C_IOTA, C_SEL, C_HPI, C_NHALF, C_DST = 0, 128, 256, 384, 392, 393, 394, 398
C_ALL = 406


def build(nc, x, fband, wtok, wqkv, wproj, gate, nw, w13, w2, consts, out):
    buf = nc.dram_tensor("slot_rows", (SLOTS, ROW), F32).ap()
    ybuf = nc.dram_tensor("pick_out", (TOKENS * TOPK, D), F32).ap()
    h1d = nc.dram_tensor("h1_rows", (BATCHES, P, TILES * D), F32).ap()
    with ExitStack() as keep:
        sb = lambda name, shape: keep.enter_context(nc.sbuf_tensor(name, shape, F32))
        cst = sb("cst", [P, C_ALL])
        gap_all = sb("gap_all", [P, BATCHES * TILES])
        kept_all = sb("kept_all", [P, BATCHES * TILES * TOPK])
        tok_attention(nc, x, fband, wtok, wqkv, wproj, gate, consts, buf, ybuf, h1d, cst, gap_all, kept_all)
        h1_all = sb("h1_all", [P, BATCHES * TILES, D])
        cw = sb("cw", [P, BATCHES * TILES, TOPK])
        experts(nc, nw, w13, w2, buf, ybuf, h1d, cst, h1_all, cw, gap_all, kept_all)
        combine(nc, ybuf, out, cst, h1_all, cw)


def tok_attention(nc, x, fband, wtok, wqkv, wproj, gate, consts, buf, ybuf, h1d, cst, gap_all, kept_all):
    with ExitStack() as ctx:
        sb = lambda name, shape, dt=F32: ctx.enter_context(nc.sbuf_tensor(name, shape, dt))
        ps = lambda name, shape: ctx.enter_context(nc.psum_tensor(name, shape, F32))
        sem = lambda name: ctx.enter_context(nc.semaphore(name))

        wk = sb("wk", [P, KTILES, D])
        fb = sb("fb", [P, 9])
        xt = sb("xt", [P, XCHUNKS, SEQ])
        turn = sb("turn", [P, RING_T, SEQ])
        frac = sb("frac", [P, RING_T, SEQ])
        feat = sb("feat", [P, RING_F, SEQ])
        h = sb("h", [P, TILES, D])
        hres = sb("hres", [P, TILES, D])
        hT = sb("hT", [P, 2, SEQ])
        wqk = sb("wqk", [P, 2, 2 * GROUPS * HALF + D])
        qh = sb("qh", [P, GROUPS, SEQ], F32R)
        ql = sb("ql", [P, GROUPS, SEQ], F32R)
        kh = sb("kh", [HALF, 2, SEQ], F32R)
        kx = sb("kx", [P, HEADS, SEQ], F32R)
        v = sb("v", [P, TILES, HEADS, 32])
        mx = sb("mx", [P, TILES, 32])
        pr = sb("pr", [P, 2, 4, SEQ])
        osb = sb("osb", [P, QUADS, SEQ])
        den = sb("den", [P, SEQ])
        onorm = sb("onorm", [P, QUADS, SEQ])
        wp = sb("wp", [P, QUADS, D])
        r = sb("r", [P, TILES, D])
        stats = sb("stats", [P, TILES, 6])
        mv = sb("mv", [P, TILES, 2])
        rstd = sb("rstd", [P, TILES])
        h1 = sb("h1", [P, TILES, D])
        ss = sb("ss", [P, TILES])
        rz = sb("rz", [P, TILES])
        z = sb("z", [P, TILES, TOPK, ROW])
        dst = sb("dst", [P, TILES * TOPK])
        gw = sb("gw", [HALF, 2, E])
        lg = sb("lg", [P, TILES, E])
        mx8 = sb("mx8", [P, TILES, 8])
        ix8 = sb("ix8", [P, TILES, 8], U32)
        idx = sb("idx", [P, TILES * TOPK])
        oh = sb("oh", [P, TILES * TOPK, E])
        both = sb("both", [P, TILES, E])
        run = sb("run", [P, TILES + 1, E])
        posx = sb("posx", [P, TILES, E])
        sel = sb("sel", [P, TILES * TOPK, E])
        pos = sb("pos", [P, TILES * TOPK])
        base = sb("base", [P, TILES * TOPK])
        far = sb("far", [P, TILES * TOPK])
        sidx_f = sb("sidx_f", [P, TILES * TOPK])
        sidx = sb("sidx", [P, TILES * TOPK], U32)

        tokacc = ps("tokacc", [P, TILES, 256])
        pair = [ps(f"pair{j}", [P, 2, 512]) for j in range(2)]
        psO = ps("psO", [P, 512])
        psM = ps("psM", [P, 512])

        loaded = sem("loaded")
        fband_in = sem("fband_in")
        wk_in = [sem(f"wk_in{j}") for j in range(WPIECES)]
        x_in = [sem(f"x_in{c}") for c in range(XCHUNKS)]
        fills = sem("fills")
        filled = sem("filled")
        preset = sem("preset")
        turn_in, frac_in = sem("turn_in"), sem("frac_in")
        sine_arg, cosine_arg = sem("sine_arg"), sem("cosine_arg")
        feat_in, feat_free = sem("feat_in"), sem("feat_free")
        h_in, hres_in = sem("h_in"), sem("hres_in")
        full = sem("full")
        left = [sem(f"left{j}") for j in range(2)]
        qh_in, kh_in, kh_free = sem("qh_in"), sem("kh_in"), sem("kh_free")
        mrow_full, mrow_in = sem("mrow_full"), sem("mrow_in")
        pr_free = sem("pr_free")
        osb_in, onorm_in = sem("osb_in"), sem("onorm_in")
        var_in, rstd_in = sem("var_in"), sem("rstd_in")
        h1_in, h1_saved, z_free = sem("h1_in"), sem("h1_saved"), sem("z_free")
        ss_in, rz_in = sem("ss_in"), sem("rz_in")
        picks_in, z_in = sem("picks_in"), sem("z_in")
        scattered = sem("scattered")
        norm_step, tail_step = sem("norm_step"), sem("tail_step")
        pool_step = sem("pool_step")
        alone = sem("alone")
        NORM_STEPS, TAIL_STEPS, POOL_STEPS = 2 * QUADS, 30, 2

        ident = cst[:, C_ID:C_ID + P]
        block = ctx.enter_context(nc.Block())

        def filled_up(eng, i, u):
            p, n = place(i, u)
            eng.wait_ge(full, 2 * n + p + 1)
            return pair[p]

        def has_left(eng, i, u):
            p, n = place(i, u)
            eng.wait_ge(left[p], n + 2)

        @block.sync
        def _(sp):
            per = KTILES // WPIECES
            sp.dma_start(xt[:, 0, :], x[0, :, 0, :]).then_inc(x_in[0], 16)
            for j in range(WPIECES):
                sp.dma_start(wk[:, j * per:(j + 1) * per, :], wtok[:, j * per:(j + 1) * per, :]).then_inc(wk_in[j], 16)
                if j % 2 == 0 and j // 2 + 1 < XCHUNKS:
                    c = j // 2 + 1
                    sp.dma_start(xt[:, c, :], x[0, :, c, :]).then_inc(x_in[c], 16)
            sp.dma_start(wqk[0:HALF + 1, :, :], wqkv).then_inc(loaded, 16)
            sp.dma_start(wp[:, :, :], wproj).then_inc(loaded, 16)
            sp.dma_start(gw[:, :, :], gate).then_inc(loaded, 16)
            sp.wait_ge(fills, 3)
            rows = buf.rearrange("(p s) d -> p (s d)", p=P)
            n = 20 * ROW
            for j in range(SLOTS // P // 20):
                sp.dma_start(rows[:, j * n:(j + 1) * n],
                             pr[:, :, :, :].rearrange("p a b s -> p (a b s)")[:, 0:n]).then_inc(filled, 16)
            rows = ybuf.rearrange("(p s) d -> p (s d)", p=P)
            n = QUADS * SEQ
            for j in range(8):
                sp.dma_start(rows[:, j * n:(j + 1) * n],
                             osb[:, :, :].rearrange("p q s -> p (q s)")).then_inc(filled, 16)

            def load_x(bt):
                for c in range(XCHUNKS):
                    last = min(6 * (c + 1), ANGLES)
                    sp.wait_ge(turn_in, (bt - 1) * ANGLES + last)
                    sp.wait_ge(frac_in, (bt - 1) * ANGLES + last)
                    sp.dma_start(xt[:, c, :], x[bass.ds(bt, 1), :, c, :].rearrange("a p s -> (a p) s")).then_inc(x_in[c], 16)

            def save_h1(j):
                sp.wait_ge(h1_in, j + 1)
                sp.dma_start(h1d[bass.ds(j, 1)].rearrange("a p n -> (a p) n"),
                             h1[:, :, :].rearrange("p t d -> p (t d)")).then_inc(h1_saved, 16)

            load_x(1)
            with sp.Fori(2, BATCHES) as bt:
                load_x(bt)
                save_h1(bt - 2)
            save_h1(BATCHES - 2)
            save_h1(BATCHES - 1)
            sp.wait_ge(h1_saved, (BATCHES + 1) * 16)

        @block.vector
        def _(dve):
            def band(a):
                return (a // BANDS, a % BANDS) if a < 4 * BANDS else (4, BANDS + a - 4 * BANDS)

            def turns(bt, a):
                c, f = band(a)
                if a % BANDS == 0:
                    dve.wait_ge(x_in[c], (bt + 1) * 16)
                if not isinstance(bt, int) or bt * KTILES + 2 * a > 2 * RING_T - 2:
                    dve.wait_ge(feat_in, bt * KTILES + 2 * (a - RING_T) + 2)
                nc.vector.tensor_scalar(turn[:, a % RING_T, :], xt[:, c, :], fb[:, f:f + 1], ROUND,
                                        ALU.mult, ALU.add).then_inc(turn_in, 1)

            def angle(bt, a):
                if a == 0:
                    turns(bt, 0)
                s = a % RING_T
                dve.wait_ge(turn_in, bt * ANGLES + a + 1)
                dve.wait_ge(frac_in, bt * ANGLES + a + 1)
                nc.vector.scalar_tensor_tensor(out=frac[:, s, :], in0=turn[:, s, :], scalar=ROUND,
                                               in1=frac[:, s, :], op0=ALU.subtract,
                                               op1=ALU.subtract).then_inc(sine_arg, 1)
                if a + 1 < ANGLES:
                    turns(bt, a + 1)
                dve.wait_ge(sine_arg, bt * ANGLES + a + 1)
                nc.vector.tensor_scalar(turn[:, s, :].bitcast(U32), frac[:, s, :].bitcast(U32), 0x7FFFFFFF, None,
                                        ALU.bitwise_and).then_inc(cosine_arg, 1)

            def transposed(i, u):
                p = filled_up(dve, i, u)
                nc.vector.tensor_copy(hT[0:HALF, :, :], p[0:HALF, :, :]).then_inc(left[place(i, u)[0]], 1)

            def normalise(i, q):
                dve.wait_ge(osb_in, i * QUADS + q + 1)
                dve.sem_inc(alone, 1)
                nc.vector.stream_shuffle(den[:, :], osb[:, q, :], [16 + m % 16 for m in range(32)]).then_inc(norm_step, 1)
                dve.wait_ge(norm_step, i * NORM_STEPS + 2 * q + 1)
                nc.vector.reciprocal(den[:, :], den[:, :]).then_inc(norm_step, 1)
                dve.wait_ge(norm_step, i * NORM_STEPS + 2 * q + 2)
                nc.vector.tensor_tensor(onorm[:, q, :], osb[:, q, :], den[:, :], ALU.mult).then_inc(onorm_in, 1)
                dve.wait_ge(onorm_in, i * QUADS + q + 1)

            def tail(j, i, u0, bt):
                ahead = lambda a: bt is not None and a + 2 < ANGLES and angle(bt, a + 2)
                steps = [0]

                def step(ins):
                    steps[0] += 1
                    ins.then_inc(tail_step, 1)

                def after_step():
                    dve.wait_ge(tail_step, j * TAIL_STEPS + steps[0])

                p = filled_up(dve, i, u0)
                dve.wait_ge(hres_in, j + 1)
                nc.vector.tensor_tensor(r[:, :, :], p[:, :, :].rearrange("p b (t n) -> p (b t) n", n=256)[:, :, 0:D],
                                        hres[:, :, :], ALU.add).then_inc(left[place(i, u0)[0]], 1)
                has_left(dve, i, u0)
                for t in range(TILES):
                    step(nc.vector.bn_stats(stats[:, t, :], r[:, t, :]))
                after_step()
                dve.sem_inc(alone, 1)
                for t in range(TILES):
                    last = nc.vector.bn_aggr(mv[:, t, :], stats[:, t, :])
                last.then_inc(var_in, 1)
                for a in T_ANGLES[0]:
                    ahead(a)
                dve.wait_ge(rstd_in, j + 1)
                dve.wait_ge(h1_saved, j * 16 + 16)
                for t in range(TILES):
                    last = nc.vector.tensor_scalar(h1[:, t, :], r[:, t, :], mv[:, t, 0:1], rstd[:, t:t + 1],
                                                   ALU.subtract, ALU.mult)
                last.then_inc(h1_in, 1)
                transposed(i, u0 + 1)
                for a in T_ANGLES[1]:
                    ahead(a)
                dve.wait_ge(rz_in, j + 1)
                dve.wait_ge(z_free, j + 1)
                for t in range(TILES):
                    nc.vector.tensor_scalar(z[:, t, :, 0:D], h1[:, t, :].unsqueeze(1).to_broadcast([P, TOPK, D]),
                                            rz[:, t:t + 1], 2.0, ALU.mult, ALU.mult)
                step(nc.vector.tensor_scalar(z[:, :, :, D].bitcast(U32),
                                             dst[:, :].rearrange("p (t k) -> p t k", k=TOPK), 0.0, None, ALU.add))
                after_step()
                step(nc.vector.tensor_scalar(dst[:, :], dst[:, :], float(SEQ * TOPK), None, ALU.add))
                p = filled_up(dve, i, u0 + 2)
                nc.vector.tensor_copy(lg[:, :, :], p[:, 0, 0:TILES * E].rearrange("p (t e) -> p t e", e=E)
                                      ).then_inc(left[place(i, u0 + 2)[0]], 1)
                has_left(dve, i, u0 + 2)
                dve.sem_inc(alone, 1)
                for t in range(TILES):
                    step(nc.vector.max(mx8[:, t, :], lg[:, t, :]))
                after_step()
                dve.sem_inc(alone, 1)
                for t in range(TILES):
                    step(nc.vector.max_index(ix8[:, t, :], mx8[:, t, :], lg[:, t, :]))
                after_step()
                step(nc.vector.tensor_copy(idx[:, :].rearrange("p (t k) -> p t k", k=TOPK), ix8[:, :, 0:TOPK]))
                step(nc.vector.tensor_tensor(gap_all[:, bass.ds(j * TILES, TILES)],
                                             mx8[:, :, 1], mx8[:, :, 0], ALU.subtract))
                after_step()
                step(nc.vector.tensor_tensor(
                    oh[:, :, :], cst[:, C_IOTA:C_IOTA + E].unsqueeze(1).to_broadcast([P, TILES * TOPK, E]),
                    idx[:, :].unsqueeze(2).to_broadcast([P, TILES * TOPK, E]), ALU.is_equal))
                after_step()
                ohk = oh[:, :, :].rearrange("p (t k) e -> p t k e", k=TOPK)
                step(nc.vector.tensor_tensor(both[:, :, :], ohk[:, :, 0, :], ohk[:, :, 1, :], ALU.add))
                after_step()
                for t in range(TILES):
                    step(nc.vector.tensor_tensor(run[:, t + 1, :], run[:, t, :], both[:, t, :], ALU.add))
                    after_step()
                dve.sem_inc(picks_in, 1)
                for a in T_ANGLES[2]:
                    ahead(a)
                p = filled_up(dve, i, u0 + 3)
                nc.vector.tensor_copy(posx[:, :, :], p[:, 0, 0:TILES * E].rearrange("p (t e) -> p t e", e=E)
                                      ).then_inc(left[place(i, u0 + 3)[0]], 1)
                has_left(dve, i, u0 + 3)
                step(nc.vector.tensor_copy(run[:, 0, :], run[:, TILES, :]))
                step(nc.vector.tensor_tensor(
                    sel[:, :, :].rearrange("p (t k) e -> p t k e", k=TOPK), ohk,
                    posx[:, :, :].unsqueeze(2).to_broadcast([P, TILES, TOPK, E]), ALU.mult))
                step(nc.vector.tensor_scalar(base[:, :], idx[:, :], float(CAP), None, ALU.mult))
                after_step()
                step(nc.vector.tensor_reduce(pos[:, :], sel[:, :, :], AX.X, ALU.add))
                after_step()
                step(nc.vector.tensor_scalar(far[:, :], pos[:, :], float(CAP), float(SLOTS), ALU.is_ge, ALU.mult))
                step(nc.vector.tensor_scalar(kept_all[:, bass.ds(j * TILES * TOPK, TILES * TOPK)], pos[:, :],
                                             float(CAP), None, ALU.is_lt))
                step(nc.vector.tensor_tensor(sidx_f[:, :], pos[:, :], base[:, :], ALU.add))
                after_step()
                step(nc.vector.tensor_tensor(sidx[:, :], sidx_f[:, :], far[:, :], ALU.add))
                after_step()
                dve.sem_inc(z_in, 1)
                for a in T_ANGLES[3]:
                    ahead(a)
                assert steps[0] == TAIL_STEPS, steps[0]

            def attention(i, bt, has_tail=True):
                ahead = lambda a: bt is not None and a + 2 < ANGLES and angle(bt, a + 2)
                if has_tail:
                    normalise(i - 1, QUADS - 1)
                for u in range(2):
                    p = filled_up(dve, i, u)
                    dve.wait_ge(qh_in, i * 2 + u + 1)
                    nc.vector.tensor_tensor(ql[0:HALF, 2 * u:2 * u + 2, :], p[0:HALF, :, :],
                                            qh[0:HALF, 2 * u:2 * u + 2, :].bitcast(F32),
                                            ALU.subtract).then_inc(left[place(i, u)[0]], 1)
                for u in range(2):
                    p = filled_up(dve, i, 2 + u)
                    dve.wait_ge(kh_in, i * 2 + u + 1)
                    for g in range(2):
                        for j in range(3):
                            rows = slice(32 * j, 32 * j + 32)
                            last = nc.vector.scalar_tensor_tensor(
                                out=kx[rows, 3 * (2 * u + g) + j, :], in0=kh[rows, g, :].bitcast(F32),
                                scalar=cst[rows, C_SEL:C_SEL + 1], in1=p[rows, g, :], op0=ALU.mult, op1=ALU.add)
                    last.then_inc(left[place(i, 2 + u)[0]], 1)
                    has_left(dve, i, 2 + u)
                    dve.sem_inc(kh_free, 1)
                if bt is not None:
                    angle(bt, 0)
                    angle(bt, 1)
                if has_tail:
                    tail(i - 1, i, P_UNITS, bt)
                else:
                    for a in range(A_FIRST):
                        ahead(a)
                for u in range(A_UNITS):
                    hd, t = u // 2, 2 * (u % 2)
                    w = first_a(i) + u
                    p = filled_up(dve, i, w)
                    nc.vector.tensor_reduce(mx[:, t:t + 2, hd], p[:, :, :], AX.X, ALU.max
                                            ).then_inc(left[place(i, w)[0]], 1)
                    for a in a_angles(u):
                        ahead(a)
                if bt is not None:
                    transposed(i, first_a(i) + A_UNITS)
                for q in range(QUADS - 1):
                    normalise(i, q)

            nc.vector.memset(pr[:, :, :, :], 0.0).then_inc(fills, 1)
            nc.vector.memset(osb[:, :, :], 0.0).then_inc(fills, 1)
            dve.wait_ge(fills, 2)
            nc.vector.memset(pr[:, :, :, :].rearrange("p a b s -> p (a b s)")[:, 0:20 * ROW]
                             .rearrange("p (s d) -> p s d", d=ROW)[:, :, D].bitcast(U32), NOWHERE).then_inc(fills, 1)
            dve.sem_inc(left[0], 1)
            dve.sem_inc(left[1], 1)
            dve.sem_inc(kh_free, 1)
            dve.sem_inc(h1_saved, 16)
            dve.wait_ge(fband_in, 16)
            for a in range(ANGLES):
                angle(0, a)
                if a == 3:
                    nc.vector.memset(ql[:, :, :].bitcast(F32), 0.0)
                    nc.vector.memset(kx[:, :, :].bitcast(F32), 0.0).then_inc(preset, 1)
                if a == 6:
                    nc.vector.memset(hT[HALF:P, :, :], 1.0)
                    nc.vector.memset(v[:, :, :, :], 1.0)
                    nc.vector.memset(run[:, 0, :], 0.0)
                    nc.vector.memset(mx[:, :, :], 0.0).then_inc(preset, 1)
                if a >= 8 and a < 8 + HEADS:
                    if a == 8:
                        dve.wait_ge(preset, 2)
                        dve.wait_ge(loaded, 16 * 4)
                        nc.vector.tensor_copy(dst[:, :], cst[:, C_DST:C_DST + TILES * TOPK])
                    hd = a - 8
                    nc.vector.tensor_copy(kx[HALF:P, hd, :],
                                          cst[HALF:P, C_ID + HALF + hd:C_ID + HALF + hd + 1].to_broadcast([P - HALF, SEQ])
                                          ).then_inc(preset, 1)
            dve.wait_ge(preset, 2 + HEADS)
            p = pair[0]
            dve.wait_ge(full, 1)
            nc.vector.tensor_copy(hT[0:HALF, :, :], p[0:HALF, :, :]).then_inc(left[0], 1)
            attention(0, 1, has_tail=False)
            with dve.Fori(1, BATCHES - 1) as i:
                attention(i, i + 1)
            attention(BATCHES - 1, None)
            normalise(BATCHES - 1, QUADS - 1)
            tail(BATCHES - 1, BATCHES - 1, UNITS - 1, None)

        @block.scalar
        def _(act):
            def product(bt, a):
                c, f = (a // BANDS, a % BANDS) if a < 4 * BANDS else (4, BANDS + a - 4 * BANDS)
                if a % BANDS == 0:
                    act.wait_ge(x_in[c], (bt + 1) * 16)
                if not isinstance(bt, int) or bt * KTILES + 2 * a > 2 * RING_T - 2:
                    act.wait_ge(feat_in, bt * KTILES + 2 * (a - RING_T) + 1)
                nc.scalar.activation(frac[:, a % RING_T, :], xt[:, c, :], ACT.Copy,
                                     scale=fb[:, f:f + 1]).then_inc(frac_in, 1)

            def features(bt, a):
                s = a % RING_T
                act.wait_ge(sine_arg, bt * ANGLES + a + 1)
                act.wait_ge(feat_free, bt * KTILES + 2 * a + 1)
                nc.scalar.activation(feat[:, 2 * a % RING_F, :], frac[:, s, :], ACT.Sin,
                                     scale=-TWO_PI).then_inc(feat_in, 1)
                act.wait_ge(cosine_arg, bt * ANGLES + a + 1)
                act.wait_ge(feat_free, bt * KTILES + 2 * a + 2)
                nc.scalar.activation(feat[:, (2 * a + 1) % RING_F, :], turn[:, s, :], ACT.Sin,
                                     bias=cst[:, C_HPI:C_HPI + 1], scale=-TWO_PI).then_inc(feat_in, 1)
                if a + RING_T < ANGLES:
                    product(bt, a + RING_T)

            def embedding_leaves(bt):
                act.wait_ge(feat_free, bt * KTILES + KTILES + RING_F)
                if not isinstance(bt, int):
                    act.wait_ge(hres_in, bt)
                elif bt > 0:
                    act.wait_ge(hres_in, bt)
                nc.scalar.activation(h[:, :, :], tokacc[:, :, 0:D], ACT.Copy).then_inc(h_in, 1)

            def tail(j, bt):
                ahead = lambda a: bt is not None and a + 2 < ANGLES and features(bt, a + 2)
                for a in T_ANGLES[0]:
                    ahead(a)
                act.wait_ge(h1_in, j + 1)
                act.wait_ge(z_free, j + 1)
                for t in range(TILES):
                    last = nc.scalar.activation(z[:, t, 0, 0:D], h1[:, t, :], ACT.Square, accum_out=ss[:, t:t + 1])
                last.then_inc(ss_in, 1)
                for gap in T_ANGLES[1:]:
                    for a in gap:
                        ahead(a)

            def attention(i, bt, has_tail=True):
                ahead = lambda a: bt is not None and a + 2 < ANGLES and features(bt, a + 2)
                for u in range(2):
                    p = filled_up(act, i, u)
                    nc.scalar.activation(qh[0:HALF, 2 * u:2 * u + 2, :], p[0:HALF, :, :], ACT.Copy).then_inc(qh_in, 1)
                for u in range(2):
                    p = filled_up(act, i, 2 + u)
                    act.wait_ge(kh_free, i * 2 + u + 1)
                    nc.scalar.activation(kh[:, :, :], p[0:HALF, :, :], ACT.Copy).then_inc(kh_in, 1)
                if bt is not None:
                    for a in range(RING_T):
                        product(bt, a)
                p = filled_up(act, i, 4)
                nc.scalar.activation(v[:, 0:2, :, 0:HD],
                                     p[:, 0, :].rearrange("p (t n) -> p t n", n=256)[:, :, 0:D]
                                     .rearrange("p t (h d) -> p t h d", d=HD), ACT.Copy)
                nc.scalar.activation(v[:, 2:4, :, 0:HD],
                                     p[:, 1, :].rearrange("p (t n) -> p t n", n=256)[:, :, 0:D]
                                     .rearrange("p t (h d) -> p t h d", d=HD), ACT.Copy).then_inc(left[place(i, 4)[0]], 1)
                if bt is not None:
                    features(bt, 0)
                    features(bt, 1)
                if has_tail:
                    tail(i - 1, bt)
                else:
                    for a in range(A_FIRST):
                        ahead(a)
                for u in range(A_UNITS):
                    for a in a_angles(u):
                        ahead(a)
                if bt is not None:
                    embedding_leaves(bt)
                act.wait_ge(mrow_full, i + 1)
                nc.scalar.activation(qh[HALF:P, :, :], psM[HALF:P, :].unsqueeze(1).to_broadcast([P - HALF, GROUPS, SEQ]),
                                     ACT.Copy, scale=-1.0).then_inc(mrow_in, 1)

                def leave(q):
                    act.wait_ge(pr_free, i * NPV + TILES * (q + 1) + 2)
                    nc.scalar.activation(osb[:, q, :], psO[:, :], ACT.Copy).then_inc(osb_in, 1)

                ub = first_b(i, bt is not None)
                for n in range(NPV):
                    act.wait_ge(pr_free, i * NPV + n + 1)
                    for j in range(2):
                        u = ub + 2 * n + j
                        p = filled_up(act, i, u)
                        nc.scalar.activation(pr[:, n % 2, 2 * j:2 * j + 2, :], p[:, :, :], ACT.Exp,
                                             scale=HD ** -0.5).then_inc(left[place(i, u)[0]], 1)
                    if n % TILES == 0 and n > 0:
                        leave(n // TILES - 1)
                leave(QUADS - 1)

            act.dma_start(fb[:, :], fband).then_inc(fband_in, 16)
            act.dma_start(cst[:, :], consts).then_inc(loaded, 16)
            act.wait_ge(fband_in, 16)
            for a in range(RING_T):
                product(0, a)
            act.wait_ge(loaded, 16 * 4)
            for a in range(ANGLES):
                features(0, a)
            embedding_leaves(0)
            act.wait_ge(filled, 16 * 12)
            act.wait_ge(preset, 2 + HEADS)
            attention(0, 1, has_tail=False)
            with act.Fori(1, BATCHES - 1) as i:
                attention(i, i + 1)
            attention(BATCHES - 1, None)
            tail(BATCHES - 1, None)

        @block.tensor
        def _(pe):
            def embed(bt, a):
                for kt in (2 * a, 2 * a + 1):
                    pe.wait_ge(feat_in, bt * KTILES + kt + 1)
                    if kt == 0 and not (isinstance(bt, int) and bt == 0):
                        pe.wait_ge(h_in, bt)
                    if isinstance(bt, int) and bt == 0 and kt % (KTILES // WPIECES) == 0:
                        pe.wait_ge(wk_in[kt // (KTILES // WPIECES)], 16)
                    for t in range(TILES):
                        last = nc.tensor.matmul(tokacc[:, t, 0:D], feat[:, kt % RING_F, t * P:(t + 1) * P],
                                                wk[:, kt, :], start=(kt == 0 and t % 2 == 0),
                                                stop=(kt == KTILES - 1), skip_group_check=True)
                    last.then_inc(feat_free, 1)

            def pair_free(i, u):
                p, n = place(i, u)
                pe.wait_ge(left[p], n + 1)
                return pair[p]

            def transposes(src, p):
                for k in range(2):
                    for t in range(TILES):
                        last = nc.tensor.transpose(p[0:HALF, k, t * P:(t + 1) * P],
                                                   src[:, t, k * HALF:(k + 1) * HALF], ident)
                last.then_inc(full, 1)

            def tail(j, i, u0, bt):
                angle = lambda a: bt is not None and embed(bt, a)
                pe.wait_ge(onorm_in, j * QUADS + QUADS)
                p = pair_free(i, u0)
                for t in range(TILES):
                    for q in range(QUADS):
                        last = nc.tensor.matmul(p[:, t // 2, (t % 2) * 256:(t % 2) * 256 + D],
                                                onorm[:, q, t * P:(t + 1) * P], wp[:, q, :],
                                                start=(q == 0), stop=(q == QUADS - 1))
                last.then_inc(full, 1)
                for a in T_ANGLES[0]:
                    angle(a)
                pe.wait_ge(h1_in, j + 1)
                transposes(h1, pair_free(i, u0 + 1))
                for a in T_ANGLES[1]:
                    angle(a)
                has_left(pe, i, u0 + 1)
                p = pair_free(i, u0 + 2)
                for t in range(TILES):
                    for k in range(2):
                        last = nc.tensor.matmul(p[:, 0, t * E:(t + 1) * E], hT[0:HALF, k, t * P:(t + 1) * P], gw[:, k, :],
                                                start=(k == 0), stop=(k == 1))
                last.then_inc(full, 1)
                for a in T_ANGLES[2]:
                    angle(a)
                pe.wait_ge(picks_in, j + 1)
                p = pair_free(i, u0 + 3)
                nc.tensor.matmul(p[:, 0, 0:TILES * E], cst[:, C_UP:C_UP + P],
                                 both[:, :, :].rearrange("p t e -> p (t e)"), start=True, stop=False)
                nc.tensor.matmul(p[:, 0, 0:TILES * E], cst[:, C_ONE:C_ONE + P],
                                 run[:, 0:TILES, :].rearrange("p t e -> p (t e)"), start=False, stop=True).then_inc(full, 1)
                for a in T_ANGLES[3]:
                    angle(a)

            def attention(i, bt, has_tail=True):
                angle = lambda a: bt is not None and embed(bt, a)
                for u in range(4):
                    p = pair_free(i, u)
                    for g in range(2):
                        cols = slice((2 * u + g) * HALF, (2 * u + g + 1) * HALF)
                        nc.tensor.matmul(p[0:HALF, g, :], wqk[0:HALF + 1, 0, cols], hT[0:HALF + 1, 0, :], start=True, stop=False)
                        last = nc.tensor.matmul(p[0:HALF, g, :], wqk[0:HALF, 1, cols], hT[0:HALF, 1, :],
                                                start=False, stop=True)
                    last.then_inc(full, 1)
                vcols = slice(2 * GROUPS * HALF, 2 * GROUPS * HALF + D)
                p = pair_free(i, 4)
                for t in range(TILES):
                    rows = slice(t * P, (t + 1) * P)
                    o = p[:, t // 2, (t % 2) * 256:(t % 2) * 256 + D]
                    nc.tensor.matmul(o, hT[0:HALF + 1, 0, rows], wqk[0:HALF + 1, 0, vcols], start=True, stop=False)
                    last = nc.tensor.matmul(o, hT[0:HALF, 1, rows], wqk[0:HALF, 1, vcols], start=False, stop=True)
                last.then_inc(full, 1)
                if has_tail:
                    tail(i - 1, i, P_UNITS, bt)
                else:
                    for a in range(A_FIRST):
                        angle(a)
                has_left(pe, i, 2)
                has_left(pe, i, 3)
                for u in range(A_UNITS):
                    hd, t = u // 2, 2 * (u % 2)
                    p = pair_free(i, first_a(i) + u)
                    for s in range(2):
                        last = nc.tensor.matmul(p[:, s, :], qh[0:HALF, hd // 3, (t + s) * P:(t + s + 1) * P],
                                                kx[0:HALF, hd, :], start=True, stop=True)
                    last.then_inc(full, 1)
                    for a in a_angles(u):
                        angle(a)
                has_left(pe, i, first_a(i) + A_UNITS - 1)
                for t in range(TILES):
                    last = nc.tensor.matmul(psM[HALF:P, t * P:(t + 1) * P], mx[:, t, :], ident, start=True, stop=True)
                last.then_inc(mrow_full, 1)
                if bt is not None:
                    pe.wait_ge(h_in, bt + 1)
                    transposes(h, pair_free(i, first_a(i) + A_UNITS))
                pe.wait_ge(mrow_in, i + 1)
                ub = first_b(i, bt is not None)

                def weigh(n):
                    q, t = n // TILES, n % TILES
                    has_left(pe, i, ub + 2 * n)
                    has_left(pe, i, ub + 2 * n + 1)
                    if t == 0 and not (isinstance(i, int) and i * QUADS + q == 0):
                        pe.wait_ge(osb_in, i * QUADS + q)
                    for j in range(4):
                        last = nc.tensor.matmul(psO[32 * j:32 * j + 32, :], v[:, t, 4 * q + j, :], pr[:, n % 2, j, :],
                                                start=(t == 0), stop=(t == TILES - 1))
                    last.then_inc(pr_free, 1)

                for n in range(NPV):
                    t = n % TILES
                    for s in range(2):
                        p = pair_free(i, ub + 2 * n + s)
                        for m in range(2):
                            hd = 4 * (n // TILES) + 2 * s + m
                            keys = kx[:, hd, t * P:(t + 1) * P]
                            nc.tensor.matmul(p[:, m, :], keys, qh[:, hd // 3, :], start=True, stop=False)
                            last = nc.tensor.matmul(p[:, m, :], keys, ql[:, hd // 3, :], start=False, stop=True)
                        last.then_inc(full, 1)
                    if n:
                        weigh(n - 1)
                weigh(NPV - 1)

            pe.sem_inc(feat_free, RING_F)
            pe.sem_inc(pr_free, 2)
            for a in range(ANGLES):
                embed(0, a)
            pe.wait_ge(loaded, 16 * 4)
            pe.wait_ge(preset, 2 + HEADS)
            pe.wait_ge(h_in, 1)
            transposes(h, pair[0])
            pe.wait_ge(left[0], 2)
            attention(0, 1, has_tail=False)
            with pe.Fori(1, BATCHES - 1) as i:
                has_left(pe, i - 1, UNITS - B_UNITS - 1)
                attention(i, i + 1)
            has_left(pe, BATCHES - 2, UNITS - B_UNITS - 1)
            attention(BATCHES - 1, None)
            tail(BATCHES - 1, BATCHES - 1, UNITS - 1, None)

        @block.gpsimd
        def _(pool):
            nhalf = cst[:, C_NHALF:C_NHALF + TILES]

            def keep_h(i):
                pool.wait_ge(h_in, i + 1)
                pool.sem_inc(alone, 1)
                nc.gpsimd.tensor_copy(hres[:, :, :], h[:, :, :]).then_inc(hres_in, 1)

            def tail(j):
                pool.wait_ge(var_in, j + 1)
                pool.sem_inc(alone, 1)
                nc.gpsimd.tensor_scalar(rstd[:, :], mv[:, :, 1], 1e-5, None, ALU.add).then_inc(pool_step, 1)
                pool.wait_ge(pool_step, j * POOL_STEPS + 1)
                nc.gpsimd.tensor_tensor(rstd[:, :], rstd[:, :], nhalf, ALU.pow).then_inc(rstd_in, 1)
                pool.wait_ge(ss_in, j + 1)
                pool.sem_inc(alone, 1)
                nc.gpsimd.tensor_scalar(rz[:, :], ss[:, :], 4.0 / D, 1e-6, ALU.mult, ALU.add).then_inc(pool_step, 1)
                pool.wait_ge(pool_step, j * POOL_STEPS + 2)
                nc.gpsimd.tensor_tensor(rz[:, :], rz[:, :], nhalf, ALU.pow).then_inc(rz_in, 1)

            def scatter(j):
                pool.wait_ge(z_in, j + 1)
                pool.sem_inc(alone, 1)
                for t in range(TILES):
                    for k in range(TOPK):
                        c = t * TOPK + k
                        nc.gpsimd.indirect_dma_start(
                            out=buf, out_offset=bass.IndirectOffsetOnAxis(ap=sidx[:, c:c + 1], axis=0),
                            in_=z[:, t, k, :], in_offset=None, bounds_check=SLOTS - 1,
                            oob_is_err=False).then_inc(scattered, 16)
                pool.wait_ge(scattered, (j + 1) * 16 * TILES * TOPK)
                pool.sem_inc(z_free, 1)

            pool.sem_inc(z_free, 1)
            pool.wait_ge(loaded, 16 * 4)
            pool.wait_ge(filled, 16 * 12)
            keep_h(0)
            with pool.Fori(1, BATCHES) as i:
                tail(i - 1)
                keep_h(i)
                scatter(i - 1)
            tail(BATCHES - 1)
            scatter(BATCHES - 1)


def experts(nc, nw, w13, w2, buf, ybuf, h1d, cst, h1_all, cw, gap_all, kept_all):
    NG, GS = 5, 2 * P
    CH = HID // P
    PG = 2 * NG
    NT = BATCHES * TILES
    with ExitStack() as ctx:
        sb = lambda name, shape, dt=F32: ctx.enter_context(nc.sbuf_tensor(name, shape, dt))
        ps = lambda name, shape: ctx.enter_context(nc.psum_tensor(name, shape, F32))
        sem = lambda name: ctx.enter_context(nc.semaphore(name))
        nws = sb("nws", [HALF, 2, E])
        nwp = sb("nwp", [HALF, 2, 1])
        nwq = sb("nwq", [HALF, 2, 1])
        w13r = [sb(f"w13r{p}", [HALF, 2, 2 * HID]) for p in range(2)]
        w2r = [sb(f"w2r{p}", [P, CH, D]) for p in range(2)]
        w13h = [sb(f"w13h{p}", [HALF, 2, 2 * HID], F32R) for p in range(2)]
        w13l = [sb(f"w13l{p}", [HALF, 2, 2 * HID], F32R) for p in range(2)]
        w2h = [sb(f"w2h{p}", [P, CH, D], F32R) for p in range(2)]
        w2l = [sb(f"w2l{p}", [P, CH, D], F32R) for p in range(2)]
        zin = [sb(f"zin{s}", [P, 2, ROW]) for s in range(NG)]
        zh = [sb(f"zh{s}", [HALF, 2, GS], F32R) for s in range(2)]
        zl = [sb(f"zl{s}", [HALF, 2, GS], F32R) for s in range(2)]
        sg = sb("sg", [P, CH, GS])
        av = sb("av", [P, CH, GS])
        ah = [sb(f"ah{s}", [P, CH, GS], F32R) for s in range(2)]
        al = [sb(f"al{s}", [P, CH, GS], F32R) for s in range(2)]
        ysb = [sb(f"ysb{s}", [P, 2, D]) for s in range(2)]
        second = sb("second", [P, NT])
        total = sb("total", [P, NT])
        keepw = sb("keepw", [P, NT])
        psT = [ps(f"psT{s}", [P, 2, GS]) for s in range(2)]
        psG = [ps(f"psG{c}", [P, 2, GS]) for c in range(CH)]
        psY = [ps(f"psY{s}", [P, 2, 256]) for s in range(2)]

        nw_in = sem("nw_in")
        w_in = [sem(f"w_in{p}") for p in range(2)]
        z_got = [sem(f"z_got{s}") for s in range(NG)]
        h1_got = sem("h1_got")
        exp_in, weight_step, scaled = sem("exp_in"), sem("weight_step"), sem("scaled")
        zT_full = sem("zT_full")
        zh_in, zl_in = sem("zh_in"), sem("zl_in")
        nwp_in = sem("nwp_in")
        wh_in, wl_in = sem("wh_in"), sem("wl_in")
        g_full, g_free = sem("g_full"), sem("g_free")
        sg_in, av_in, ah_in, al_in = sem("sg_in"), sem("av_in"), sem("ah_in"), sem("al_in")
        y_full, y_in = sem("y_full"), sem("y_in")
        y_out = [sem(f"y_out{s}") for s in range(2)]
        ident = cst[:, C_ID:C_ID + P]
        block = ctx.enter_context(nc.Block())

        def following(ep, m, more):
            return (ep, m + 1) if m + 1 < PG else (ep + 1, 0) if more else None

        @block.sync
        def _(sp):
            def weights(ep, p):
                if not (isinstance(ep, int) and ep == 0):
                    sp.wait_ge(wl_in, 3 * (2 * ep + p) - 3)
                sp.dma_start(w13r[p][:, :, :], w13[bass.ds(2 * ep + p, 1)].rearrange("a p k n -> (a p) k n")).then_inc(w_in[p], 16)
                sp.dma_start(w2r[p][:, :, :], w2[bass.ds(2 * ep + p, 1)].rearrange("a p k n -> (a p) k n")).then_inc(w_in[p], 16)

            def rows(ep, m):
                if m >= NG or not (isinstance(ep, int) and ep == 0):
                    sp.wait_ge(y_out[(m + 1) % 2], 32 * (NG * ep + (m - NG) // 2 + 1))
                sp.dma_start(zin[m % NG][:, :, :],
                             buf[bass.ds(ep * 2 * CAP + m * GS, GS), :].rearrange("(s p) d -> p s d", p=P)
                             ).then_inc(z_got[m % NG], 16)

            def pair(ep, first=False):
                for m in range(PG):
                    rows(ep, m)
                    if m == 1:
                        weights(ep, 1)
                    if first and m == 4:
                        sp.dma_start(h1_all[:, :, :].rearrange("p (i t) d -> p i (t d)", t=TILES),
                                     h1d.rearrange("i p n -> p i n")).then_inc(h1_got, 16)

            sp.dma_start(nws[:, :, :], nw).then_inc(nw_in, 16)
            weights(0, 0)
            pair(0, first=True)
            with sp.Fori(1, E // 2) as ep:
                weights(ep, 0)
                pair(ep)

        @block.tensor
        def _(pe):
            def turn(ep, m):
                pe.wait_ge(z_got[m % NG], (ep * 2 + m // NG + 1) * 16)
                pe.wait_ge(zl_in, ep * PG + m + 1)
                for k in range(2):
                    for s in range(2):
                        last = nc.tensor.transpose(psT[m % 2][0:HALF, k, s * P:(s + 1) * P],
                                                   zin[m % NG][:, s, k * HALF:(k + 1) * HALF], ident)
                last.then_inc(zT_full, 1)

            def hidden(ep, m):
                p, g = m // NG, m % NG
                pe.wait_ge(zl_in, ep * PG + m + 3)
                if g == 0:
                    pe.wait_ge(wl_in, (2 * ep + p) * 3 + 3)
                for c in range(CH):
                    pe.wait_ge(g_free, (ep * PG + m) * CH + c + 1)
                    for j in range(2):
                        cols = slice(j * HID + c * P, j * HID + (c + 1) * P)
                        terms = [(w, zz, k) for w, zz in ((w13h, zh), (w13l, zh), (w13h, zl)) for k in range(2)]
                        for x, (w, zz, k) in enumerate(terms):
                            last = nc.tensor.matmul(psG[c][:, j, :], w[p][:, k, cols], zz[m % 2][:, k, :],
                                                    start=(x == 0), stop=(x == 5))
                    last.then_inc(g_full, 1)

            def output(ep, m):
                p = (m // NG) % 2
                pe.wait_ge(al_in, (ep * PG + m + 1) * CH + 1)
                pe.wait_ge(y_in, ep * PG + m + 1)
                for s in range(2):
                    terms = [(a, w, c) for c in range(CH) for a, w in ((ah, w2h), (ah, w2l), (al, w2h))]
                    for x, (a, w, c) in enumerate(terms):
                        last = nc.tensor.matmul(psY[m % 2][:, s, 0:D], a[m % 2][:, c, s * P:(s + 1) * P], w[p][:, c, :],
                                                start=(x == 0), stop=(x == len(terms) - 1))
                last.then_inc(y_full, 1)

            def pair(ep, more, first=False):
                for m in range(PG):
                    nxt = following(ep, m, more)
                    if nxt:
                        turn(*nxt)
                    hidden(ep, m)
                    if m:
                        output(ep, m - 1)
                    elif not first:
                        output(ep - 1, PG - 1)

            turn(0, 0)
            pair(0, True, first=True)
            with pe.Fori(1, E // 2 - 1) as ep:
                pair(ep, True)
            pair(E // 2 - 1, False)
            output(E // 2 - 1, PG - 1)

        def pieces(p, scale):
            return [(w13r[p][:, k, :], w13h[p][:, k, :], w13l[p][:, k, :], scale[:, k, :]) for k in range(2)] + \
                   [(w2r[p][:, :, :], w2h[p][:, :, :], w2l[p][:, :, :], 1.0)]

        SPLITS = {1: (0, 1, 0), 2: (0, 1, 1), 3: (0, 1, 2), 6: (1, 0, 0), 7: (1, 0, 1), 8: (1, 0, 2)}

        @block.scalar
        def _(act):
            def split(ep, p, x):
                raw, hi, _, scale = pieces(p, (nwp, nwq)[p])[x]
                if x == 0:
                    act.wait_ge(w_in[p], (ep + 1) * 32)
                    act.wait_ge(nwp_in, 2 * ep + p + 1)
                    if not (isinstance(ep, int) and ep == 0):
                        act.wait_ge(y_full, (ep - 1) * PG + (p + 1) * NG)
                nc.scalar.activation(hi, raw, ACT.Copy, scale=scale).then_inc(wh_in, 1)

            def group(ep, m):
                act.wait_ge(zT_full, ep * PG + m + 1)
                if not (isinstance(ep, int) and ep == 0 and m < 2):
                    act.wait_ge(g_full, (ep * PG + m - 1) * CH)
                nc.scalar.activation(zh[m % 2][:, :, :], psT[m % 2][0:HALF, :, :], ACT.Copy).then_inc(zh_in, 1)

            def high(ep, m, c):
                act.wait_ge(av_in, (ep * PG + m) * CH + c + 1)
                if c == 0 and not (isinstance(ep, int) and ep == 0 and m < 2):
                    act.wait_ge(y_full, ep * PG + m - 1)
                nc.scalar.activation(ah[m % 2][:, c, :], av[:, c, :], ACT.Copy).then_inc(ah_in, 1)

            def leave(ep, m):
                act.wait_ge(y_full, ep * PG + m + 1)
                if m >= 2 or not (isinstance(ep, int) and ep == 0):
                    act.wait_ge(y_out[m % 2], 32 * (ep * NG + m // 2))
                nc.scalar.activation(ysb[m % 2][:, :, :], psY[m % 2][:, :, 0:D], ACT.Copy).then_inc(y_in, 1)

            def pair(ep, more, first=False):
                for m in range(PG):
                    nxt = following(ep, m, more)
                    if nxt:
                        group(*nxt)
                    for c in range(CH):
                        act.wait_ge(g_full, (ep * PG + m) * CH + c + 1)
                        if c == 0:
                            act.wait_ge(g_free, (ep * PG + m) * CH + CH)
                        nc.scalar.activation(sg[:, c, :], psG[c][:, 0, :], ACT.Silu).then_inc(sg_in, 1)
                        if c:
                            high(ep, m, c - 1)
                    high(ep, m, CH - 1)
                    if m:
                        leave(ep, m - 1)
                    elif not first:
                        leave(ep - 1, PG - 1)
                    if m in SPLITS and (more or not SPLITS[m][0]):
                        later, p, x = SPLITS[m]
                        split(ep + later, p, x)

            act.sem_inc(y_in, 2)
            nc.scalar.activation(second[:, :], gap_all[:, :], ACT.Exp).then_inc(exp_in, 1)
            for x in range(3):
                split(0, 0, x)
            group(0, 0)
            pair(0, True, first=True)
            with act.Fori(1, E // 2 - 1) as ep:
                pair(ep, True)
            pair(E // 2 - 1, False)
            leave(E // 2 - 1, PG - 1)

        @block.vector
        def _(dve):
            def scale_of(ep, p):
                e = 2 * ep + p
                if not (isinstance(ep, int) and ep == 0):
                    dve.wait_ge(wl_in, 3 * e - 3)
                nc.vector.tensor_copy((nwp, nwq)[p][:, :, :], nws[:, :, bass.ds(e, 1)]).then_inc(nwp_in, 1)
                dve.wait_ge(nwp_in, e + 1)

            def split(ep, p, x):
                if x == 0:
                    scale_of(ep, p)
                raw, hi, lo, scale = pieces(p, (nwp, nwq)[p])[x]
                dve.wait_ge(wh_in, (2 * ep + p) * 3 + x + 1)
                nc.vector.scalar_tensor_tensor(out=lo, in0=raw, scalar=scale, in1=hi.bitcast(F32), op0=ALU.mult,
                                               op1=ALU.subtract).then_inc(wl_in, 1)

            def group(ep, m):
                dve.wait_ge(zh_in, ep * PG + m + 1)
                nc.vector.tensor_tensor(zl[m % 2][:, :, :], psT[m % 2][0:HALF, :, :], zh[m % 2][:, :, :].bitcast(F32),
                                        ALU.subtract).then_inc(zl_in, 1)

            def low(ep, m, c):
                dve.wait_ge(ah_in, (ep * PG + m) * CH + c + 1)
                nc.vector.tensor_tensor(al[m % 2][:, c, :], av[:, c, :], ah[m % 2][:, c, :].bitcast(F32),
                                        ALU.subtract).then_inc(al_in, 1)

            def pair(ep, more):
                for m in range(PG):
                    nxt = following(ep, m, more)
                    if nxt:
                        group(*nxt)
                    for c in range(CH):
                        n = (ep * PG + m) * CH + c
                        dve.wait_ge(sg_in, n + 1)
                        if c == 0:
                            dve.wait_ge(al_in, (ep * PG + m) * CH + 1)
                        nc.vector.tensor_tensor(av[:, c, :], sg[:, c, :], psG[c][:, 1, :], ALU.mult).then_inc(av_in, 1)
                        dve.wait_ge(av_in, n + 1)
                        dve.sem_inc(g_free, 1)
                        if c:
                            low(ep, m, c - 1)
                    low(ep, m, CH - 1)
                    if m in SPLITS and (more or not SPLITS[m][0]):
                        later, p, x = SPLITS[m]
                        split(ep + later, p, x)

            dve.sem_inc(g_free, CH)
            dve.sem_inc(al_in, 1)
            dve.sem_inc(zl_in, 2)
            done = [0]

            def step(ins):
                done[0] += 1
                ins.then_inc(weight_step, 1)
                dve.wait_ge(weight_step, done[0])

            dve.wait_ge(exp_in, 1)
            kept = kept_all[:, :].rearrange("p (t k) -> p t k", k=TOPK)
            step(nc.vector.tensor_scalar(total[:, :], second[:, :], 1.0, None, ALU.add))
            step(nc.vector.reciprocal(total[:, :], total[:, :]))
            step(nc.vector.tensor_tensor(cw[:, :, 0], total[:, :], kept[:, :, 0], ALU.mult))
            step(nc.vector.tensor_tensor(cw[:, :, 1], total[:, :], second[:, :], ALU.mult))
            step(nc.vector.tensor_tensor(cw[:, :, 1], cw[:, :, 1], kept[:, :, 1], ALU.mult))
            step(nc.vector.scalar_tensor_tensor(out=keepw[:, :], in0=cw[:, :, 0], scalar=1.0, in1=cw[:, :, 1],
                                                op0=ALU.add, op1=ALU.add))
            dve.wait_ge(nw_in, 16)
            for x in range(3):
                split(0, 0, x)
            group(0, 0)
            pair(0, True)
            with dve.Fori(1, E // 2 - 1) as ep:
                pair(ep, True)
            pair(E // 2 - 1, False)

        @block.gpsimd
        def _(pool):
            def write(ep, m):
                pool.wait_ge(y_in, ep * PG + m + 3)
                pool.sem_inc(scaled, 1)
                for s in range(2):
                    nc.gpsimd.indirect_dma_start(
                        out=ybuf, out_offset=bass.IndirectOffsetOnAxis(ap=zin[m % NG][:, s, D:ROW].bitcast(U32), axis=0),
                        in_=ysb[m % 2][:, s, :], in_offset=None, bounds_check=TOKENS * TOPK - 1,
                        oob_is_err=False).then_inc(y_out[m % 2], 16)

            for m in range(PG):
                write(0, m)
            pool.wait_ge(h1_got, 16)
            pool.wait_ge(weight_step, 6)
            for t in range(NT):
                nc.gpsimd.tensor_scalar(h1_all[:, t, :], h1_all[:, t, :], keepw[:, t:t + 1], 1.0, ALU.mult, ALU.mult)
            with pool.Fori(1, E // 2) as ep:
                for m in range(PG):
                    write(ep, m)
            for s in range(2):
                pool.wait_ge(y_out[s], 32 * NG * E // 2)


def combine(nc, ybuf, out, cst, h1_all, cw):
    with ExitStack() as ctx:
        sb = lambda name, shape, dt=F32: ctx.enter_context(nc.sbuf_tensor(name, shape, dt))
        sem = lambda name: ctx.enter_context(nc.semaphore(name))
        f = sb("f", [P, BATCHES, TILES, TOPK, D])
        r = sb("r2", [P, 2, TILES, D])
        stats = sb("stats2", [P, TILES, 6])
        mv = sb("mv2", [P, 2, TILES, 2])
        rstd = sb("rstd2", [P, 2, TILES])
        shift = sb("shift", [P, 2, TILES])
        res = sb("res", [P, 2, TILES, D])
        got = [sem(f"got{b}") for b in range(BATCHES)]
        sum_step, r_done = sem("sum_step"), sem("r_done")
        var_in, rstd_in, pool_step = sem("var2_in"), sem("rstd2_in"), sem("pool2_step")
        shift_in, res_in = sem("shift_in"), sem("res_in")
        written = [sem(f"written{s}") for s in range(2)]
        block = ctx.enter_context(nc.Block())
        PER = 2 * TILES + TILES

        @block.sync
        def _(sp):
            for b in range(BATCHES):
                sp.dma_start(f[:, b, :, :, :].rearrange("p t k d -> p t (k d)"),
                             ybuf.rearrange("(b t p k) d -> b p t (k d)", t=TILES, p=P, k=TOPK)[b]).then_inc(got[b], 16)
            for b in range(BATCHES):
                sp.wait_ge(res_in, b + 1)
                sp.dma_start(out[b].rearrange("(t p) d -> p t d", p=P), res[:, b % 2, :, :]).then_inc(written[b % 2], 16)
            for s in range(2):
                sp.wait_ge(written[s], BATCHES // 2 * 16)

        @block.vector
        def _(dve):
            def normal(b):
                dve.wait_ge(rstd_in, b + 1)
                nc.vector.scalar_tensor_tensor(out=shift[:, b % 2, :], in0=mv[:, b % 2, :, 0], scalar=-1.0,
                                               in1=rstd[:, b % 2, :], op0=ALU.mult, op1=ALU.mult).then_inc(shift_in, 1)

            for b in range(BATCHES):
                n = [0]

                def step(ins):
                    n[0] += 1
                    ins.then_inc(sum_step, 1)

                dve.wait_ge(got[b], 16)
                if b >= 2:
                    dve.wait_ge(res_in, b - 1)
                for k in range(TOPK):
                    for t in range(TILES):
                        if k:
                            dve.wait_ge(sum_step, b * PER + n[0] - TILES + 1)
                        step(nc.vector.scalar_tensor_tensor(
                            out=r[:, b % 2, t, :], in0=f[:, b, t, k, :], scalar=cw[:, b * TILES + t, k:k + 1],
                            in1=r[:, b % 2, t, :] if k else h1_all[:, b * TILES + t, :], op0=ALU.mult, op1=ALU.add))
                for t in range(TILES):
                    dve.wait_ge(sum_step, b * PER + n[0] - TILES + 1)
                    step(nc.vector.bn_stats(stats[:, t, :], r[:, b % 2, t, :]))
                dve.wait_ge(sum_step, b * PER + n[0])
                for t in range(TILES):
                    last = nc.vector.bn_aggr(mv[:, b % 2, t, :], stats[:, t, :])
                last.then_inc(var_in, 1)
                assert n[0] == PER
                dve.wait_ge(var_in, b + 1)
                if b:
                    normal(b - 1)
            normal(BATCHES - 1)

        @block.gpsimd
        def _(pool):
            for b in range(BATCHES):
                pool.wait_ge(var_in, b + 1)
                nc.gpsimd.tensor_scalar(rstd[:, b % 2, :], mv[:, b % 2, :, 1], 1e-5, None, ALU.add).then_inc(pool_step, 1)
                pool.wait_ge(pool_step, b + 1)
                nc.gpsimd.tensor_tensor(rstd[:, b % 2, :], rstd[:, b % 2, :], cst[:, C_NHALF:C_NHALF + TILES],
                                        ALU.pow).then_inc(rstd_in, 1)

        @block.scalar
        def _(act):
            for b in range(BATCHES):
                act.wait_ge(shift_in, b + 1)
                if b >= 2:
                    act.wait_ge(written[b % 2], b // 2 * 16)
                for t in range(TILES):
                    last = nc.scalar.activation(res[:, b % 2, t, :], r[:, b % 2, t, :], ACT.Identity,
                                                scale=rstd[:, b % 2, t:t + 1], bias=shift[:, b % 2, t:t + 1])
                last.then_inc(res_in, 1)


def _layout(x, L0_tok_freq_bands, L0_tok_W, L0_attn_w_qkv, L0_attn_b_qkv, L0_attn_w_proj, L0_attn_b_proj,
            L0_ffn_gate_w, L0_ffn_w13, L0_ffn_w2, L0_ffn_norm_w):
    import numpy as np
    a = {}
    xv = np.asarray(x).reshape(BATCHES, SEQ, VALUES).transpose(0, 2, 1)
    xv = np.concatenate([xv, xv[:, 4 * P:]], axis=1).reshape(BATCHES, XCHUNKS, P, SEQ)
    a["x"] = np.ascontiguousarray(xv.transpose(0, 2, 1, 3))
    fr = np.asarray(L0_tok_freq_bands)
    f = np.empty((P, 9), fr.dtype)
    f[:, 0:6] = fr
    for m in range(3):
        f[:64, 6 + m], f[64:, 6 + m] = fr[2 * m], fr[2 * m + 1]
    a["fband"] = f
    w = np.asarray(L0_tok_W).T.reshape(VALUES, 2, BANDS, D)
    wk = np.empty((KTILES, P, D), w.dtype)
    for n in range(ANGLES):
        for s in range(2):
            if n < 4 * BANDS:
                c, b = n // BANDS, n % BANDS
                wk[2 * n + s] = w[c * P:(c + 1) * P, s, b]
            else:
                m = n - 4 * BANDS
                wk[2 * n + s, :64] = w[4 * P:, s, 2 * m]
                wk[2 * n + s, 64:] = w[4 * P:, s, 2 * m + 1]
    a["wtok"] = np.ascontiguousarray(wk.transpose(1, 0, 2))
    wq, bq = np.asarray(L0_attn_w_qkv), np.asarray(L0_attn_b_qkv)
    cols = [np.repeat(np.arange(HEADS * HD).reshape(HEADS, 1, HD) + s * D, 2, axis=1).ravel() for s in range(2)]
    cols = np.concatenate(cols + [np.arange(D) + 2 * D])
    wt = np.zeros((HALF + 1, 2, len(cols)), wq.dtype)
    wt[:HALF, 0], wt[:HALF, 1], wt[HALF, 0] = wq[cols, :HALF].T, wq[cols, HALF:].T, bq[cols]
    a["wqkv"] = wt
    wp, bp = np.asarray(L0_attn_w_proj), np.asarray(L0_attn_b_proj)
    pw = np.zeros((QUADS, 4, 32, D), wp.dtype)
    pw[:, :, :HD] = wp.T.reshape(QUADS, 4, HD, D)
    pw[0, 0, HD] = bp
    a["wproj"] = np.ascontiguousarray(pw.reshape(QUADS, P, D).transpose(1, 0, 2))
    a["gate"] = np.ascontiguousarray(np.asarray(L0_ffn_gate_w).T.reshape(2, HALF, E).transpose(1, 0, 2))
    a["nw"] = np.ascontiguousarray(np.asarray(L0_ffn_norm_w).T.reshape(2, HALF, E).transpose(1, 0, 2))
    a["w13"] = np.ascontiguousarray(np.asarray(L0_ffn_w13).transpose(0, 2, 1).reshape(E, 2, HALF, 2 * HID).transpose(0, 2, 1, 3))
    a["w2"] = np.ascontiguousarray(np.asarray(L0_ffn_w2).transpose(0, 2, 1).reshape(E, HID // P, P, D).transpose(0, 2, 1, 3))
    c = np.zeros((P, C_ALL), np.float32)
    c[:, C_ID:C_ID + P] = np.eye(P)
    c[:, C_UP:C_UP + P] = np.triu(np.ones((P, P)), 1)
    c[:, C_ONE:C_ONE + P] = 1.0
    c[:, C_IOTA:C_IOTA + E] = np.arange(E)
    c[:, C_SEL] = np.where(np.arange(P) % 32 < HD, 0.0, -1.0)
    c[:, C_NHALF:C_NHALF + TILES] = -0.5
    c[:, C_HPI] = HALF_PI
    c[:, C_DST:C_DST + TILES * TOPK] = 2 * np.arange(P)[:, None] + np.array([2 * P * t + k for t in range(TILES) for k in range(TOPK)])
    a["consts"] = c
    return a


def kernel(**inputs):
    import numpy as _np
    import concourse.bacc as _bacc
    from concourse import mybir as _mybir
    from concourse.bass_utils import run_bass_kernel_spmd as _run

    nc = _bacc.Bacc("TRN2", target_bir_lowering=False, num_devices=1)
    laid = _layout(**inputs)
    aps = {n: nc.dram_tensor(f"in_{n}", a.shape, _mybir.dt.from_np(a.dtype), kind="ExternalInput").ap()
           for n, a in laid.items()}
    out = nc.dram_tensor("out_0_dram", (BATCHES, SEQ, D), _mybir.dt.float32, kind="ExternalOutput").ap()
    build(nc, out=out, **aps)
    r = _run(nc, [{f"in_{n}": a for n, a in laid.items()}], core_ids=[0])
    return r.results[0]["out_0_dram"]
```

```python
from contextlib import ExitStack

import concourse.bass as bass
from concourse import mybir

F32 = mybir.dt.float32
F32R = mybir.dt.float32r
U32 = mybir.dt.uint32
ALU = mybir.AluOpType
ACT = mybir.ActivationFunctionType
AX = mybir.AxisListType

P = 128
BATCHES = 8
SEQ = 512
TILES = SEQ // P
TOKENS = BATCHES * SEQ
D = 192
HALF = D // 2
VALUES = 3 * D
BANDS = 6
XCHUNKS = 5
ANGLES = 4 * BANDS + BANDS // 2
KTILES = 2 * ANGLES
HEADS, HD = 12, 16
GROUPS = 6
QUADS = 3
E, TOPK, HID = 8, 2, 512
CAP = 1280
SLOTS = E * CAP
ROW = D + 1
NOWHERE = 1 << 20
ROUND = 12582912.0
TWO_PI = 6.283185
HALF_PI = 1.5707963

RING_F, RING_T = 6, 3
SLOT_FILLS, PICK_FILLS = 4, 8
FILLS = SLOT_FILLS + PICK_FILLS
WPIECES = 9

P_UNITS, TAIL_UNITS, A_UNITS, B_UNITS = 6, 4, 24, 24
QS, KS = 0, 3
UNITS = P_UNITS + TAIL_UNITS + A_UNITS + B_UNITS
NPV = QUADS * TILES
EARLY = 8

ROWS_AT = 18
LATE_ROWS_AT = 1

H_AT = 0
Q_STEPS = {n: range(3 * (n - 2), 3 * (n - 1)) for n in range(2, 6)}
K_STEPS = {n: range(3 * (n - 7), 3 * (n - 6)) for n in range(7, 11)}
LATE_TAIL = [2, 4, 6, 8]

P_ANGLES = {0: [0], 2: [1], 4: [2], 5: [3, 4]}
T_ANGLES = [[5, 6, 7], [8], [9, 10], []]
A_FIRST, A_SPREAD = 11, 22


def a_angles(u):
    n = ANGLES - A_FIRST
    return [] if u >= A_SPREAD else [A_FIRST + k for k in range(u * n // A_SPREAD, (u + 1) * n // A_SPREAD)]


def place(i, u):
    if isinstance(i, int) and i == 0:
        return u % 2, u // 2
    return u % 2, UNITS // 2 * i + (u - TAIL_UNITS) // 2


def first_a(i):
    return P_UNITS + (0 if isinstance(i, int) and i in (0, BATCHES - 1) else TAIL_UNITS)


def b_unit(i, n, s=0):
    tails = sum(n >= at for at in LATE_TAIL) if isinstance(i, int) and i == BATCHES - 1 else 0
    return first_a(i) + A_UNITS + 2 * n + s + tails


def tail_units(i):
    if isinstance(i, int) and i == BATCHES - 1:
        return [b_unit(i, at) - 1 for at in LATE_TAIL]
    return [P_UNITS + x for x in range(TAIL_UNITS)]


C_ID, C_UP, C_ONE, C_IOTA, C_MASK, C_HPI, C_NHALF, C_DST = 0, 128, 256, 384, 392, 394, 395, 399
C_ALL = 407


def build(nc, x, fband, wtok, wqkv, wproj, gate, nw, w13, w2, consts, spread, out):
    buf = nc.dram_tensor("slot_rows", (SLOTS, ROW), F32).ap()
    ybuf = nc.dram_tensor("pick_out", (TOKENS * TOPK, D), F32).ap()
    h1d = nc.dram_tensor("h1_rows", (BATCHES, P, TILES * D), F32).ap()
    with ExitStack() as keep:
        sb = lambda name, shape: keep.enter_context(nc.sbuf_tensor(name, shape, F32))
        cst = sb("cst", [P, C_ALL])
        gap_all = sb("gap_all", [P, BATCHES * TILES])
        kept_all = sb("kept_all", [P, BATCHES * TILES * TOPK])
        early = sb("early", [P, XCHUNKS + RING_T, SEQ])
        nws = sb("nws", [P, 3, E])
        flat = early[:, :, :].rearrange("p c s -> p (c s)")
        w13_first = flat[:, 0:3 * 2 * HID].rearrange("p (k n) -> p k n", k=3)
        w2_first = flat[:, 6 * HID:6 * HID + HID // P * D].rearrange("p (c n) -> p c n", n=D)
        firsts = (nws, w13_first, w2_first)
        tok_attention(nc, x, fband, wtok, wqkv, wproj, gate, nw, w13, w2, consts, spread, buf, ybuf, h1d, cst, early,
                      firsts, gap_all, kept_all)
        h1_all = sb("h1_all", [P, BATCHES * TILES, D])
        cw = sb("cw", [P, BATCHES * TILES, TOPK])
        experts(nc, w13, w2, buf, ybuf, h1d, cst, firsts, h1_all, cw, gap_all, kept_all)
        combine(nc, ybuf, out, cst, h1_all, cw)


def tok_attention(nc, x, fband, wtok, wqkv, wproj, gate, nw, w13, w2, consts, spread, buf, ybuf, h1d, cst, early,
                  firsts, gap_all, kept_all):
    with ExitStack() as ctx:
        sb = lambda name, shape, dt=F32: ctx.enter_context(nc.sbuf_tensor(name, shape, dt))
        ps = lambda name, shape: ctx.enter_context(nc.psum_tensor(name, shape, F32))
        sem = lambda name: ctx.enter_context(nc.semaphore(name))

        wk = sb("wk", [P, KTILES, D])
        fb = sb("fb", [P, 9])
        xt, frac = early[:, 0:XCHUNKS, :], early[:, XCHUNKS:, :]
        turn = sb("turn", [P, RING_T, SEQ])
        feat = sb("feat", [P, RING_F, SEQ])
        h = sb("h", [P, TILES, D])
        hres = sb("hres", [P, TILES, D])
        hTh = sb("hTh", [P, 2, SEQ], F32R)
        hTl = sb("hTl", [HALF, 2, SEQ], F32R)
        h1T = sb("h1T", [HALF, 2, SEQ])
        wqh = sb("wqh", [HALF + 1, 2, 3 * D], F32R)
        wql = sb("wql", [HALF + 1, 2, 3 * D], F32R)
        spr = sb("spr", [HALF, 2, 3, 2, HALF], F32R)
        high = sb("high", [HALF, 2, 2, SEQ], F32R)
        low = sb("low", [HALF, 2, 2, SEQ], F32R)
        qx = sb("qx", [P, GROUPS, SEQ], F32R)
        kx = sb("kx", [P, HEADS, SEQ], F32R)
        v = sb("v", [P, TILES, HEADS, 32])
        mx = [sb(f"mx{x}", [P, TILES, 32]) for x in range(2)]
        pr = sb("pr", [P, 2, 4, SEQ])
        osb = sb("osb", [P, QUADS, SEQ])
        den = sb("den", [P, SEQ])
        wp = sb("wp", [P, QUADS, D])
        r = sb("r", [P, TILES, D])
        stats = sb("stats", [P, TILES, 6])
        mv = sb("mv", [P, TILES, 2])
        rstd = sb("rstd", [P, TILES])
        h1 = sb("h1", [P, TILES, D])
        ss = sb("ss", [P, TILES])
        rz = sb("rz", [P, TILES])
        z = sb("z", [P, TILES, TOPK, ROW])
        dst = sb("dst", [P, TILES * TOPK])
        gw = sb("gw", [HALF, 2, E])
        lg = sb("lg", [P, TILES, E])
        mx8 = sb("mx8", [P, TILES, 8])
        ix8 = sb("ix8", [P, TILES, 8], U32)
        idx = sb("idx", [P, TILES * TOPK])
        oh = sb("oh", [P, TILES * TOPK, E])
        both = sb("both", [P, TILES, E])
        run = sb("run", [P, TILES + 1, E])
        posx = sb("posx", [P, TILES, E])
        sel = sb("sel", [P, TILES * TOPK, E])
        pos = sb("pos", [P, TILES * TOPK])
        base = sb("base", [P, TILES * TOPK])
        far = sb("far", [P, TILES * TOPK])
        sidx_f = sb("sidx_f", [P, TILES * TOPK])
        sidx = sb("sidx", [P, TILES * TOPK], U32)

        tokacc = ps("tokacc", [P, TILES, 256])
        pair = [ps(f"pair{j}", [P, 2, 512]) for j in range(2)]
        side = ps("side", [P, 2, 512])
        psO = side[:, 0, :]
        psM = side[:, 1, :]

        loaded = sem("loaded")
        fband_in, const_in = sem("fband_in"), sem("const_in")
        wk_in = [sem(f"wk_in{j}") for j in range(WPIECES)]
        x_in = [sem(f"x_in{c}") for c in range(XCHUNKS)]
        first_in = sem("first_in")
        fills = sem("fills")
        filled = sem("filled")
        preset = sem("preset")
        turn_in, frac_in = sem("turn_in"), sem("frac_in")
        sine_arg, cosine_arg = sem("sine_arg"), sem("cosine_arg")
        feat_in, feat_free = sem("feat_in"), sem("feat_free")
        h_in, hres_in = sem("h_in"), sem("hres_in")
        full = sem("full")
        left = [sem(f"left{j}") for j in range(2)]
        parts_in = sem("parts_in")
        raw_full, low_in = sem("raw_full"), sem("low_in")
        high_in = sem("high_in")
        kx_in, hTh_in = sem("kx_in"), sem("hTh_in")
        mrow_full, mrow_in = sem("mrow_full"), sem("mrow_in")
        mdup_in, mlate_full, mlate_in = sem("mdup_in"), sem("mlate_full"), sem("mlate_in")
        hT_full, hTl_in, v_full, v_in = sem("hT_full"), sem("hTl_in"), sem("v_full"), sem("v_in")
        pr_free = sem("pr_free")
        osb_in, onorm_in = sem("osb_in"), sem("onorm_in")
        var_in, rstd_in = sem("var_in"), sem("rstd_in")
        h1_in, h1_saved, z_free = sem("h1_in"), sem("h1_saved"), sem("z_free")
        ss_in, rz_in = sem("ss_in"), sem("rz_in")
        picks_in, z_in = sem("picks_in"), sem("z_in")
        scattered = sem("scattered")
        norm_step, tail_step = sem("norm_step"), sem("tail_step")
        pool_step = sem("pool_step")
        alone = sem("alone")
        NORM_STEPS, TAIL_STEPS, POOL_STEPS = 2 * QUADS, 30, 2
        PRESETS = 1 + HEADS + 1

        ident = cst[:, C_ID:C_ID + P]
        wq_raw = z[0:HALF + 1, :, :, :].rearrange("p t k d -> p (t k d)")[:, 0:6 * D].rearrange("p (h n) -> p h n", h=2)
        spread_raw = [b[0:HALF, :, :].rearrange("p t d -> p (t d)")[:, 0:6 * HALF] for b in (r, h1)]
        block = ctx.enter_context(nc.Block())

        def following(make, bt, nxt):
            def ahead(a):
                if bt is not None and a + RING_T < ANGLES:
                    make(bt, a + RING_T)
                elif nxt is not None:
                    make(nxt, a + RING_T - ANGLES)
            return ahead

        def heads(u, s):
            return kx[0:HALF, 4 * u:4 * u + 4, :].rearrange("p (g s) n -> p g s n", s=2)[:, :, s, :]

        raw = tokacc[0:HALF, :, :].rearrange("p (g t) n -> p g (t n)", g=2)

        def filled_up(eng, i, u):
            p, n = place(i, u)
            eng.wait_ge(full, 2 * n + p + 1)
            return pair[p]

        def has_left(eng, i, u):
            p, n = place(i, u)
            eng.wait_ge(left[p], n + 2)

        @block.sync
        def _(sp):
            per = KTILES // WPIECES
            sp.dma_start(xt[:, 0, :], x[0, :, 0, :]).then_inc(x_in[0], 16)
            for j in range(WPIECES):
                sp.dma_start(wk[:, j * per:(j + 1) * per, :], wtok[:, j * per:(j + 1) * per, :]).then_inc(wk_in[j], 16)
                if j % 2 == 0 and j // 2 + 1 < XCHUNKS:
                    c = j // 2 + 1
                    sp.dma_start(xt[:, c, :], x[0, :, c, :]).then_inc(x_in[c], 16)
            sp.dma_start(wq_raw, wqkv).then_inc(loaded, 16)
            for w in range(2):
                sp.dma_start(spread_raw[w], spread[:, w * 6 * HALF:(w + 1) * 6 * HALF]).then_inc(loaded, 16)
            sp.dma_start(wp[:, :, :], wproj).then_inc(loaded, 16)
            sp.dma_start(gw[:, :, :], gate).then_inc(loaded, 16)
            sp.wait_ge(fills, 3)
            rows = buf.rearrange("(p s) d -> p (s d)", p=P)
            n = SLOTS // P // SLOT_FILLS * ROW
            for j in range(SLOT_FILLS):
                sp.dma_start(rows[:, j * n:(j + 1) * n],
                             pr[:, :, :, :].rearrange("p a b s -> p (a b s)")[:, 0:n]).then_inc(filled, 16)
            rows = ybuf.rearrange("(p s) d -> p (s d)", p=P)
            n = TOKENS * TOPK // P * D // PICK_FILLS
            for j in range(PICK_FILLS):
                sp.dma_start(rows[:, j * n:(j + 1) * n],
                             osb[:, :, :].rearrange("p q s -> p (q s)")).then_inc(filled, 16)

            def load_x(bt):
                for c in range(XCHUNKS):
                    last = min(6 * (c + 1), ANGLES)
                    sp.wait_ge(turn_in, (bt - 1) * ANGLES + last)
                    sp.wait_ge(frac_in, (bt - 1) * ANGLES + last)
                    sp.dma_start(xt[:, c, :], x[bass.ds(bt, 1), :, c, :].rearrange("a p s -> (a p) s")).then_inc(x_in[c], 16)

            def save_h1(j):
                sp.wait_ge(h1_in, j + 1)
                sp.dma_start(h1d[bass.ds(j, 1)].rearrange("a p n -> (a p) n"),
                             h1[:, :, :].rearrange("p t d -> p (t d)")).then_inc(h1_saved, 16)

            load_x(1)
            with sp.Fori(2, BATCHES) as bt:
                load_x(bt)
                save_h1(bt - 2)
            sp.wait_ge(feat_in, BATCHES * KTILES)
            for got, wanted in zip(firsts, (nw, w13[0], w2[0])):
                sp.dma_start(got[:, :, :], wanted).then_inc(first_in, 16)
            save_h1(BATCHES - 2)
            save_h1(BATCHES - 1)
            sp.wait_ge(h1_saved, (BATCHES + 1) * 16)
            sp.wait_ge(first_in, 3 * 16)

        @block.vector
        def _(dve):
            def band(a):
                return (a // BANDS, a % BANDS) if a < 4 * BANDS else (4, BANDS + a - 4 * BANDS)

            def turns(bt, a):
                c, f = band(a)
                if a % BANDS == 0:
                    dve.wait_ge(x_in[c], (bt + 1) * 16)
                if not isinstance(bt, int) or bt * KTILES + 2 * a > 2 * RING_T - 2:
                    dve.wait_ge(feat_in, bt * KTILES + 2 * (a - RING_T) + 2)
                nc.vector.tensor_scalar(turn[:, a % RING_T, :], xt[:, c, :], fb[:, f:f + 1], ROUND,
                                        ALU.mult, ALU.add).then_inc(turn_in, 1)

            def angle(bt, a):
                if a == 0:
                    turns(bt, 0)
                s = a % RING_T
                dve.wait_ge(turn_in, bt * ANGLES + a + 1)
                dve.wait_ge(frac_in, bt * ANGLES + a + 1)
                nc.vector.scalar_tensor_tensor(out=frac[:, s, :], in0=turn[:, s, :], scalar=ROUND,
                                               in1=frac[:, s, :], op0=ALU.subtract,
                                               op1=ALU.subtract).then_inc(sine_arg, 1)
                if a + 1 < ANGLES:
                    turns(bt, a + 1)
                dve.wait_ge(sine_arg, bt * ANGLES + a + 1)
                nc.vector.tensor_scalar(turn[:, s, :].bitcast(U32), frac[:, s, :].bitcast(U32), 0x7FFFFFFF, None,
                                        ALU.bitwise_and).then_inc(cosine_arg, 1)

            def transposed(bt):
                dve.wait_ge(hT_full, bt + 1)
                nc.vector.tensor_copy(hTh[0:HALF, :, :], raw).then_inc(hTh_in, 1)
                dve.wait_ge(hTh_in, bt + 1)
                nc.vector.tensor_tensor(hTl[:, :, :], raw, hTh[0:HALF, :, :].bitcast(F32),
                                        ALU.subtract).then_inc(hTl_in, 1)

            def split(bt, w):
                dve.wait_ge(raw_full, 2 * bt + w + 1)
                nc.vector.tensor_copy(high[:, w, :, :], raw).then_inc(high_in, 1)
                dve.wait_ge(high_in, 2 * bt + w + 1)
                nc.vector.tensor_tensor(low[:, w, :, :], raw, high[:, w, :, :].bitcast(F32),
                                        ALU.subtract).then_inc(low_in, 1)

            def normalise(i, q):
                dve.wait_ge(osb_in, i * QUADS + q + 1)
                dve.sem_inc(alone, 1)
                nc.vector.stream_shuffle(den[:, :], osb[:, q, :], [16 + m % 16 for m in range(32)]).then_inc(norm_step, 1)
                dve.wait_ge(norm_step, i * NORM_STEPS + 2 * q + 1)
                nc.vector.reciprocal(den[:, :], den[:, :]).then_inc(norm_step, 1)
                dve.wait_ge(norm_step, i * NORM_STEPS + 2 * q + 2)
                nc.vector.tensor_tensor(osb[:, q, :], osb[:, q, :], den[:, :], ALU.mult).then_inc(onorm_in, 1)
                dve.wait_ge(onorm_in, i * QUADS + q + 1)

            def tail(j, i, units, between):
                steps = [0]

                def step(ins):
                    steps[0] += 1
                    ins.then_inc(tail_step, 1)

                def after_step():
                    dve.wait_ge(tail_step, j * TAIL_STEPS + steps[0])

                p = filled_up(dve, i, units[0])
                dve.wait_ge(hres_in, j + 1)
                nc.vector.tensor_tensor(r[:, :, :], p[:, :, :].rearrange("p b (t n) -> p (b t) n", n=256)[:, :, 0:D],
                                        hres[:, :, :], ALU.add).then_inc(left[place(i, units[0])[0]], 1)
                has_left(dve, i, units[0])
                for t in range(TILES):
                    step(nc.vector.bn_stats(stats[:, t, :], r[:, t, :]))
                after_step()
                dve.sem_inc(alone, 1)
                for t in range(TILES):
                    last = nc.vector.bn_aggr(mv[:, t, :], stats[:, t, :])
                last.then_inc(var_in, 1)
                between(0)
                dve.wait_ge(rstd_in, j + 1)
                dve.wait_ge(h1_saved, j * 16 + 16)
                for t in range(TILES):
                    last = nc.vector.tensor_scalar(h1[:, t, :], r[:, t, :], mv[:, t, 0:1], rstd[:, t:t + 1],
                                                   ALU.subtract, ALU.mult)
                last.then_inc(h1_in, 1)
                p = filled_up(dve, i, units[1])
                nc.vector.tensor_copy(h1T[:, :, :], p[0:HALF, :, :]).then_inc(left[place(i, units[1])[0]], 1)
                between(1)
                dve.wait_ge(rz_in, j + 1)
                dve.wait_ge(z_free, j + 1)
                for t in range(TILES):
                    nc.vector.tensor_scalar(z[:, t, :, 0:D], h1[:, t, :].unsqueeze(1).to_broadcast([P, TOPK, D]),
                                            rz[:, t:t + 1], 2.0, ALU.mult, ALU.mult)
                step(nc.vector.tensor_scalar(z[:, :, :, D].bitcast(U32),
                                             dst[:, :].rearrange("p (t k) -> p t k", k=TOPK), 0.0, None, ALU.add))
                after_step()
                step(nc.vector.tensor_scalar(dst[:, :], dst[:, :], float(SEQ * TOPK), None, ALU.add))
                p = filled_up(dve, i, units[2])
                nc.vector.tensor_copy(lg[:, :, :], p[:, 0, 0:TILES * E].rearrange("p (t e) -> p t e", e=E)
                                      ).then_inc(left[place(i, units[2])[0]], 1)
                has_left(dve, i, units[2])
                dve.sem_inc(alone, 1)
                for t in range(TILES):
                    step(nc.vector.max(mx8[:, t, :], lg[:, t, :]))
                after_step()
                dve.sem_inc(alone, 1)
                for t in range(TILES):
                    step(nc.vector.max_index(ix8[:, t, :], mx8[:, t, :], lg[:, t, :]))
                after_step()
                step(nc.vector.tensor_copy(idx[:, :].rearrange("p (t k) -> p t k", k=TOPK), ix8[:, :, 0:TOPK]))
                step(nc.vector.tensor_tensor(gap_all[:, bass.ds(j * TILES, TILES)],
                                             mx8[:, :, 1], mx8[:, :, 0], ALU.subtract))
                after_step()
                step(nc.vector.tensor_tensor(
                    oh[:, :, :], cst[:, C_IOTA:C_IOTA + E].unsqueeze(1).to_broadcast([P, TILES * TOPK, E]),
                    idx[:, :].unsqueeze(2).to_broadcast([P, TILES * TOPK, E]), ALU.is_equal))
                after_step()
                ohk = oh[:, :, :].rearrange("p (t k) e -> p t k e", k=TOPK)
                step(nc.vector.tensor_tensor(both[:, :, :], ohk[:, :, 0, :], ohk[:, :, 1, :], ALU.add))
                after_step()
                for t in range(TILES):
                    step(nc.vector.tensor_tensor(run[:, t + 1, :], run[:, t, :], both[:, t, :], ALU.add))
                    after_step()
                dve.sem_inc(picks_in, 1)
                between(2)
                p = filled_up(dve, i, units[3])
                nc.vector.tensor_copy(posx[:, :, :], p[:, 0, 0:TILES * E].rearrange("p (t e) -> p t e", e=E)
                                      ).then_inc(left[place(i, units[3])[0]], 1)
                has_left(dve, i, units[3])
                step(nc.vector.tensor_copy(run[:, 0, :], run[:, TILES, :]))
                step(nc.vector.tensor_tensor(
                    sel[:, :, :].rearrange("p (t k) e -> p t k e", k=TOPK), ohk,
                    posx[:, :, :].unsqueeze(2).to_broadcast([P, TILES, TOPK, E]), ALU.mult))
                step(nc.vector.tensor_scalar(base[:, :], idx[:, :], float(CAP), None, ALU.mult))
                after_step()
                step(nc.vector.tensor_reduce(pos[:, :], sel[:, :, :], AX.X, ALU.add))
                after_step()
                step(nc.vector.tensor_scalar(far[:, :], pos[:, :], float(CAP), float(SLOTS), ALU.is_ge, ALU.mult))
                step(nc.vector.tensor_scalar(kept_all[:, bass.ds(j * TILES * TOPK, TILES * TOPK)], pos[:, :],
                                             float(CAP), None, ALU.is_lt))
                step(nc.vector.tensor_tensor(sidx_f[:, :], pos[:, :], base[:, :], ALU.add))
                after_step()
                step(nc.vector.tensor_tensor(sidx[:, :], sidx_f[:, :], far[:, :], ALU.add))
                after_step()
                dve.sem_inc(z_in, 1)
                between(3)
                assert steps[0] == TAIL_STEPS, steps[0]

            def attention(i, bt, nxt, has_tail=True):
                ahead = following(angle, bt, nxt)
                last_one = isinstance(i, int) and i == BATCHES - 1

                def gap(x):
                    for a in T_ANGLES[x]:
                        ahead(a)

                for u in range(QS, P_UNITS):
                    if u < KS and (u - QS) % 2:
                        p = filled_up(dve, i, u)
                        nc.vector.tensor_copy(qx[0:HALF, 2 * (u - QS):2 * (u - QS) + 2, :], p[0:HALF, :, :]
                                              ).then_inc(left[place(i, u)[0]], 1)
                    if u >= KS:
                        p = filled_up(dve, i, u)
                        dve.wait_ge(kx_in, i * 3 + u - KS + 1)
                        nc.vector.tensor_scalar(heads(u - KS, 1), p[0:HALF, :, :], cst[0:HALF, C_MASK + 1:C_MASK + 2],
                                                None, ALU.mult).then_inc(left[place(i, u)[0]], 1)
                    for a in P_ANGLES.get(u, []):
                        ahead(a)
                    if u == 2 and has_tail:
                        normalise(i - 1, QUADS - 1)
                if has_tail:
                    if not last_one:
                        tail(i - 1, i, tail_units(i), gap)
                else:
                    for x in range(4):
                        gap(x)
                for u in range(A_UNITS):
                    hd, t = u // 2, 2 * (u % 2)
                    p = filled_up(dve, i, first_a(i) + u)
                    nc.vector.tensor_reduce(mx[hd >= EARLY][:, t:t + 2, hd], p[:, :, :], AX.X, ALU.max
                                            ).then_inc(left[place(i, first_a(i) + u)[0]], 1)
                    for a in a_angles(u):
                        ahead(a)
                    if u == ROWS_AT + 2:
                        dve.wait_ge(mrow_in, i + 1)
                        nc.vector.tensor_copy(qx[HALF:P, 2:4, :], qx[HALF:P, 0, :].bitcast(F32).unsqueeze(1)
                                              .to_broadcast([P - HALF, 2, SEQ])).then_inc(mdup_in, 1)
                dve.wait_ge(mlate_full, i + 1)
                nc.vector.tensor_scalar(qx[HALF:P, 4:GROUPS, :],
                                        psM[HALF:P, :].unsqueeze(1).to_broadcast([P - HALF, GROUPS - 4, SEQ]),
                                        -1.0, None, ALU.mult).then_inc(mlate_in, 1)
                if bt is not None:
                    transposed(bt)
                    split(bt, 0)
                if last_one:
                    tail(i - 1, i, tail_units(i), lambda x: normalise(i, 0) if x == 3 else None)
                else:
                    normalise(i, 0)
                if bt is not None:
                    split(bt, 1)
                normalise(i, 1)

            nc.vector.memset(pr[:, :, :, :], 0.0).then_inc(fills, 1)
            nc.vector.memset(osb[:, :, :], 0.0).then_inc(fills, 1)
            dve.wait_ge(fills, 2)
            nc.vector.memset(pr[:, :, :, :].rearrange("p a b s -> p (a b s)")[:, 0:SLOTS // P // SLOT_FILLS * ROW]
                             .rearrange("p (s d) -> p s d", d=ROW)[:, :, D].bitcast(U32), NOWHERE).then_inc(fills, 1)
            dve.sem_inc(left[0], 1)
            dve.sem_inc(left[1], 1)
            dve.sem_inc(h1_saved, 16)
            dve.wait_ge(fband_in, 16)
            for a in range(ANGLES):
                angle(0, a)
                if a == 6:
                    nc.vector.memset(v[:, :, :, :], 1.0)
                    nc.vector.memset(run[:, 0, :], 0.0)
                    nc.vector.memset(mx[0][:, :, :], 0.0)
                    nc.vector.memset(mx[1][:, :, :], 0.0).then_inc(preset, 1)
                if a >= 8 and a < 8 + HEADS:
                    if a == 8:
                        dve.wait_ge(const_in, 16)
                        nc.vector.tensor_copy(hTh[HALF:P, 0, :], cst[HALF:P, C_ONE:C_ONE + 1].to_broadcast([P - HALF, SEQ]))
                        nc.vector.tensor_copy(dst[:, :], cst[:, C_DST:C_DST + TILES * TOPK])
                    hd = a - 8
                    nc.vector.tensor_copy(kx[HALF:P, hd, :],
                                          cst[HALF:P, C_ID + HALF + hd:C_ID + HALF + hd + 1].to_broadcast([P - HALF, SEQ])
                                          ).then_inc(preset, 1)
            dve.wait_ge(parts_in, 1)
            nc.vector.tensor_tensor(wql[:, :, :], wq_raw, wqh[:, :, :].bitcast(F32), ALU.subtract).then_inc(preset, 1)
            dve.wait_ge(preset, PRESETS)
            for a in range(RING_T):
                angle(1, a)
            transposed(0)
            split(0, 0)
            split(0, 1)
            attention(0, 1, 2, has_tail=False)
            with dve.Fori(1, BATCHES - 2) as i:
                attention(i, i + 1, i + 2)
            attention(BATCHES - 2, BATCHES - 1, None)
            attention(BATCHES - 1, None, None)
            normalise(BATCHES - 1, QUADS - 1)
            tail(BATCHES - 1, BATCHES - 1, range(UNITS, UNITS + TAIL_UNITS), lambda x: None)

        @block.scalar
        def _(act):
            def product(bt, a):
                c, f = (a // BANDS, a % BANDS) if a < 4 * BANDS else (4, BANDS + a - 4 * BANDS)
                if a % BANDS == 0:
                    act.wait_ge(x_in[c], (bt + 1) * 16)
                if not isinstance(bt, int) or bt * KTILES + 2 * a > 2 * RING_T - 2:
                    act.wait_ge(feat_in, bt * KTILES + 2 * (a - RING_T) + 1)
                nc.scalar.activation(frac[:, a % RING_T, :], xt[:, c, :], ACT.Copy,
                                     scale=fb[:, f:f + 1]).then_inc(frac_in, 1)

            def features(bt, a, more=True):
                s = a % RING_T
                act.wait_ge(sine_arg, bt * ANGLES + a + 1)
                act.wait_ge(feat_free, bt * KTILES + 2 * a + 1)
                nc.scalar.activation(feat[:, 2 * a % RING_F, :], frac[:, s, :], ACT.Sin,
                                     scale=-TWO_PI).then_inc(feat_in, 1)
                act.wait_ge(cosine_arg, bt * ANGLES + a + 1)
                act.wait_ge(feat_free, bt * KTILES + 2 * a + 2)
                nc.scalar.activation(feat[:, (2 * a + 1) % RING_F, :], turn[:, s, :], ACT.Sin,
                                     bias=cst[:, C_HPI:C_HPI + 1], scale=-TWO_PI).then_inc(feat_in, 1)
                if a + RING_T < ANGLES:
                    product(bt, a + RING_T)
                elif more:
                    product(bt + 1, a + RING_T - ANGLES)

            def embedding_leaves(bt):
                act.wait_ge(feat_free, bt * KTILES + KTILES + RING_F)
                if not isinstance(bt, int):
                    act.wait_ge(hres_in, bt)
                elif bt > 0:
                    act.wait_ge(hres_in, bt)
                nc.scalar.activation(h[:, :, :], tokacc[:, :, 0:D], ACT.Copy).then_inc(h_in, 1)

            def tail(j, between):
                between(0)
                act.wait_ge(h1_in, j + 1)
                act.wait_ge(z_free, j + 1)
                for t in range(TILES):
                    last = nc.scalar.activation(z[:, t, 0, 0:D], h1[:, t, :], ACT.Square, accum_out=ss[:, t:t + 1])
                last.then_inc(ss_in, 1)
                for x in range(1, 4):
                    between(x)

            def attention(i, bt, nxt, has_tail=True):
                ahead = following(lambda n, a: features(n, a, nxt is not None), bt, nxt)
                last_one = isinstance(i, int) and i == BATCHES - 1

                def gap(x):
                    for a in T_ANGLES[x]:
                        ahead(a)

                act.wait_ge(v_full, i + 1)
                for x in range(2):
                    last = nc.scalar.activation(v[:, 2 * x:2 * x + 2, :, 0:HD],
                                                tokacc[:, 2 * x:2 * x + 2, 0:D]
                                                .rearrange("p t (h d) -> p t h d", d=HD), ACT.Copy)
                last.then_inc(v_in, 1)
                for u in range(QS, P_UNITS):
                    if u < KS and (u - QS) % 2 == 0:
                        p = filled_up(act, i, u)
                        nc.scalar.activation(qx[0:HALF, 2 * (u - QS):2 * (u - QS) + 2, :], p[0:HALF, :, :], ACT.Copy
                                             ).then_inc(left[place(i, u)[0]], 1)
                    if u >= KS:
                        p = filled_up(act, i, u)
                        nc.scalar.activation(heads(u - KS, 0), p[0:HALF, :, :], ACT.Copy,
                                             scale=cst[0:HALF, C_MASK:C_MASK + 1]).then_inc(kx_in, 1)
                    for a in P_ANGLES.get(u, []):
                        ahead(a)
                if has_tail:
                    if not last_one:
                        tail(i - 1, gap)
                else:
                    for x in range(4):
                        gap(x)
                def early_rows():
                    act.wait_ge(mrow_full, i + 1)
                    nc.scalar.activation(qx[HALF:P, 0:2, :], psM[HALF:P, :].unsqueeze(1).to_broadcast([P - HALF, 2, SEQ]),
                                         ACT.Copy, scale=-1.0).then_inc(mrow_in, 1)

                for u in range(A_UNITS):
                    if u == ROWS_AT + 1:
                        early_rows()
                    for a in a_angles(u):
                        if a == ANGLES - 1 and bt is not None:
                            embedding_leaves(bt)
                        ahead(a)

                def leave(q):
                    act.wait_ge(pr_free, i * NPV + TILES * (q + 1) + 2)
                    nc.scalar.activation(osb[:, q, :], psO, ACT.Copy).then_inc(osb_in, 1)

                def groups(first, end):
                    for n in range(first, end):
                        act.wait_ge(pr_free, i * NPV + n + 1)
                        for j in range(2):
                            u = b_unit(i, n, j)
                            p = filled_up(act, i, u)
                            nc.scalar.activation(pr[:, n % 2, 2 * j:2 * j + 2, :], p[:, :, :], ACT.Exp,
                                                 scale=HD ** -0.5).then_inc(left[place(i, u)[0]], 1)
                        if n % TILES == 0 and n > 0:
                            if last_one and n == TILES:
                                filled_up(act, i, tail_units(i)[0])
                            leave(n // TILES - 1)

                if last_one:
                    groups(0, LATE_TAIL[1])
                    tail(i - 1, lambda x: None)
                    groups(LATE_TAIL[1], NPV)
                else:
                    groups(0, NPV)
                leave(QUADS - 1)

            act.dma_start(fb[:, :], fband).then_inc(fband_in, 16)
            act.dma_start(cst[:, :], consts).then_inc(const_in, 16)
            act.wait_ge(fband_in, 16)
            for a in range(RING_T):
                product(0, a)
            act.wait_ge(const_in, 16)
            for a in range(ANGLES):
                features(0, a)
                if a == 12:
                    act.wait_ge(loaded, 16 * 5)
                    nc.scalar.activation(wqh[:, :, :], wq_raw, ACT.Copy).then_inc(parts_in, 1)
                    for w in range(2):
                        nc.scalar.activation(spr[:, w, :, :, :].rearrange("p j h n -> p (j h n)"), spread_raw[w],
                                             ACT.Copy).then_inc(parts_in, 1)
            embedding_leaves(0)
            for a in range(RING_T):
                features(1, a)
            act.wait_ge(filled, 16 * FILLS)
            act.wait_ge(preset, PRESETS)
            attention(0, 1, 2, has_tail=False)
            with act.Fori(1, BATCHES - 2) as i:
                attention(i, i + 1, i + 2)
            attention(BATCHES - 2, BATCHES - 1, None)
            attention(BATCHES - 1, None, None)
            tail(BATCHES - 1, lambda x: None)

        @block.tensor
        def _(pe):
            def embed(bt, a):
                for kt in (2 * a, 2 * a + 1):
                    pe.wait_ge(feat_in, bt * KTILES + kt + 1)
                    if kt == 0 and not (isinstance(bt, int) and bt == 0):
                        pe.wait_ge(v_in, bt)
                    if isinstance(bt, int) and bt == 0 and kt % (KTILES // WPIECES) == 0:
                        pe.wait_ge(wk_in[kt // (KTILES // WPIECES)], 16)
                    for t in range(TILES):
                        last = nc.tensor.matmul(tokacc[:, t, 0:D], feat[:, kt % RING_F, t * P:(t + 1) * P],
                                                wk[:, kt, :], start=(kt == 0 and t % 2 == 0),
                                                stop=(kt == KTILES - 1), skip_group_check=True)
                    last.then_inc(feat_free, 1)

            def pair_free(i, u):
                p, n = place(i, u)
                pe.wait_ge(left[p], n + 1)
                return pair[p]

            def transposes(src, p, done):
                for k in range(2):
                    for t in range(TILES):
                        last = nc.tensor.transpose(p[0:HALF, k, t * P:(t + 1) * P],
                                                   src[:, t, k * HALF:(k + 1) * HALF], ident)
                last.then_inc(done, 1)

            def tail(j, i, units, between):
                pe.wait_ge(onorm_in, j * QUADS + QUADS)
                p = pair_free(i, units[0])
                for t in range(TILES):
                    for q in range(QUADS):
                        last = nc.tensor.matmul(p[:, t // 2, (t % 2) * 256:(t % 2) * 256 + D],
                                                osb[:, q, t * P:(t + 1) * P], wp[:, q, :],
                                                start=(q == 0), stop=(q == QUADS - 1))
                last.then_inc(full, 1)
                between(0)
                pe.wait_ge(h1_in, j + 1)
                transposes(h1, pair_free(i, units[1]), full)
                between(1)
                has_left(pe, i, units[1])
                p = pair_free(i, units[2])
                for t in range(TILES):
                    for k in range(2):
                        last = nc.tensor.matmul(p[:, 0, t * E:(t + 1) * E], h1T[:, k, t * P:(t + 1) * P], gw[:, k, :],
                                                start=(k == 0), stop=(k == 1))
                last.then_inc(full, 1)
                between(2)
                pe.wait_ge(picks_in, j + 1)
                p = pair_free(i, units[3])
                nc.tensor.matmul(p[:, 0, 0:TILES * E], cst[:, C_UP:C_UP + P],
                                 both[:, :, :].rearrange("p t e -> p (t e)"), start=True, stop=False)
                nc.tensor.matmul(p[:, 0, 0:TILES * E], cst[:, C_ONE:C_ONE + P],
                                 run[:, 0:TILES, :].rearrange("p t e -> p (t e)"), start=False, stop=True).then_inc(full, 1)
                between(3)

            terms = [(w, hh, k) for w, hh in ((wqh, hTh), (wql, hTh), (wqh, hTl)) for k in range(2)]
            rows_of = lambda hh, k: slice(0, HALF + 1 if k == 0 and hh is hTh else HALF)

            def products(bt, w, steps):
                for n in steps:
                    g, x = n // 6, n % 6
                    ww, hh, k = terms[x]
                    rows = rows_of(hh, k)
                    if n == 0 and w:
                        pe.wait_ge(low_in, 2 * bt + w)
                    cols = slice(w * D + g * HALF, w * D + (g + 1) * HALF)
                    ins = nc.tensor.matmul(raw[:, g, :], ww[rows, k, cols], hh[rows, k, :],
                                           start=(x == 0), stop=(x == 5))
                    if n == 11:
                        ins.then_inc(raw_full, 1)

            def maxima_rows(x, done):
                for t in range(TILES):
                    last = nc.tensor.matmul(side[HALF:P, 1, t * P:(t + 1) * P], mx[x][:, t, :], ident, start=True, stop=True)
                last.then_inc(done, 1)

            def attention(i, bt, has_tail=True):
                last_one = isinstance(i, int) and i == BATCHES - 1
                angle = lambda a: bt is not None and embed(bt, a)

                def gap(x):
                    for a in T_ANGLES[x]:
                        angle(a)

                pe.wait_ge(low_in, 2 * i + 2)
                for t in range(TILES):
                    for n, (ww, hh, k) in enumerate(terms):
                        last = nc.tensor.matmul(tokacc[:, t, 0:D],
                                                hh[rows_of(hh, k), k, t * P:(t + 1) * P],
                                                ww[rows_of(hh, k), k, 2 * D:3 * D], start=(n == 0), stop=(n == 5))
                last.then_inc(v_full, 1)
                for u in range(QS, P_UNITS):
                    w, first = (0, QS) if u < KS else (1, KS)
                    p = pair_free(i, u)
                    for s in range(2):
                        g = 2 * (u - first) + s
                        nc.tensor.matmul(p[0:HALF, s, :], spr[:, w, g % 3, 0, :], high[:, w, g // 3, :],
                                         start=True, stop=False)
                        last = nc.tensor.matmul(p[0:HALF, s, :], spr[:, w, g % 3, 1, :], low[:, w, g // 3, :],
                                                start=False, stop=True)
                    last.then_inc(full, 1)
                    for a in P_ANGLES.get(u, []):
                        angle(a)
                if has_tail:
                    if not last_one:
                        tail(i - 1, i, tail_units(i), gap)
                else:
                    for x in range(4):
                        gap(x)
                has_left(pe, i, P_UNITS - 2)
                has_left(pe, i, P_UNITS - 1)
                for u in range(A_UNITS):
                    if u == ROWS_AT:
                        has_left(pe, i, first_a(i) + 2 * EARLY - 2)
                        has_left(pe, i, first_a(i) + 2 * EARLY - 1)
                        maxima_rows(0, mrow_full)
                    hd, t = u // 2, 2 * (u % 2)
                    p = pair_free(i, first_a(i) + u)
                    for s in range(2):
                        last = nc.tensor.matmul(p[:, s, :], qx[0:HALF, hd // 2, (t + s) * P:(t + s + 1) * P],
                                                kx[0:HALF, hd, :], start=True, stop=True)
                    last.then_inc(full, 1)
                    for a in a_angles(u):
                        angle(a)
                pe.wait_ge(mrow_in, i + 1)
                def weigh(n):
                    q, t = n // TILES, n % TILES
                    has_left(pe, i, b_unit(i, n))
                    has_left(pe, i, b_unit(i, n, 1))
                    if t == 0 and not (isinstance(i, int) and i * QUADS + q == 0):
                        pe.wait_ge(osb_in, i * QUADS + q)
                    for j in range(4):
                        last = nc.tensor.matmul(side[32 * j:32 * j + 32, 0, :], v[:, t, 4 * q + j, :], pr[:, n % 2, j, :],
                                                start=(t == 0), stop=(t == TILES - 1))
                    last.then_inc(pr_free, 1)

                def group(n):
                    t = n % TILES
                    if n == TILES:
                        pe.wait_ge(mdup_in, i + 1)
                    if n == 2 * TILES:
                        pe.wait_ge(mlate_in, i + 1)
                    for s in range(2):
                        p = pair_free(i, b_unit(i, n, s))
                        for m in range(2):
                            hd = 4 * (n // TILES) + 2 * s + m
                            last = nc.tensor.matmul(p[:, m, :], kx[:, hd, t * P:(t + 1) * P], qx[:, hd // 2, :],
                                                    start=True, stop=True)
                        last.then_inc(full, 1)
                    if n == H_AT and bt is not None:
                        pe.wait_ge(h_in, bt + 1)
                        transposes(h, raw, hT_full)
                    if n in Q_STEPS and bt is not None:
                        pe.wait_ge(hTl_in, bt + 1)
                        products(bt, 0, Q_STEPS[n])
                    if n in K_STEPS and bt is not None:
                        products(bt, 1, K_STEPS[n])
                    if n == LATE_ROWS_AT:
                        pe.wait_ge(mrow_in, i + 1)
                        has_left(pe, i, first_a(i) + A_UNITS - 2)
                        has_left(pe, i, first_a(i) + A_UNITS - 1)
                        maxima_rows(1, mlate_full)
                    if n:
                        weigh(n - 1)

                def groups(x):
                    for n in range(LATE_TAIL[x], (LATE_TAIL + [NPV])[x + 1]):
                        group(n)

                if last_one:
                    for n in range(LATE_TAIL[0]):
                        group(n)
                    tail(i - 1, i, tail_units(i), groups)
                else:
                    for n in range(NPV):
                        group(n)
                weigh(NPV - 1)

            pe.sem_inc(feat_free, RING_F)
            pe.sem_inc(pr_free, 2)
            for a in range(ANGLES):
                embed(0, a)
            pe.wait_ge(loaded, 16 * 5)
            pe.wait_ge(parts_in, 3)
            pe.wait_ge(const_in, 16)
            pe.wait_ge(preset, PRESETS)
            pe.wait_ge(h_in, 1)
            transposes(h, raw, hT_full)
            pe.wait_ge(hTl_in, 1)
            products(0, 0, range(12))
            products(0, 1, range(12))
            attention(0, 1, has_tail=False)
            with pe.Fori(1, BATCHES - 1) as i:
                attention(i, i + 1)
            attention(BATCHES - 1, None)
            tail(BATCHES - 1, BATCHES - 1, range(UNITS, UNITS + TAIL_UNITS), lambda x: None)

        @block.gpsimd
        def _(pool):
            nhalf = cst[:, C_NHALF:C_NHALF + TILES]

            def keep_h(i):
                pool.wait_ge(h_in, i + 1)
                pool.sem_inc(alone, 1)
                nc.gpsimd.tensor_copy(hres[:, :, :], h[:, :, :]).then_inc(hres_in, 1)

            def tail(j):
                pool.wait_ge(var_in, j + 1)
                pool.sem_inc(alone, 1)
                nc.gpsimd.tensor_scalar(rstd[:, :], mv[:, :, 1], 1e-5, None, ALU.add).then_inc(pool_step, 1)
                pool.wait_ge(pool_step, j * POOL_STEPS + 1)
                nc.gpsimd.tensor_tensor(rstd[:, :], rstd[:, :], nhalf, ALU.pow).then_inc(rstd_in, 1)
                pool.wait_ge(ss_in, j + 1)
                pool.sem_inc(alone, 1)
                nc.gpsimd.tensor_scalar(rz[:, :], ss[:, :], 4.0 / D, 1e-6, ALU.mult, ALU.add).then_inc(pool_step, 1)
                pool.wait_ge(pool_step, j * POOL_STEPS + 2)
                nc.gpsimd.tensor_tensor(rz[:, :], rz[:, :], nhalf, ALU.pow).then_inc(rz_in, 1)

            def scatter(j):
                pool.wait_ge(z_in, j + 1)
                pool.sem_inc(alone, 1)
                for t in range(TILES):
                    for k in range(TOPK):
                        c = t * TOPK + k
                        nc.gpsimd.indirect_dma_start(
                            out=buf, out_offset=bass.IndirectOffsetOnAxis(ap=sidx[:, c:c + 1], axis=0),
                            in_=z[:, t, k, :], in_offset=None, bounds_check=SLOTS - 1,
                            oob_is_err=False).then_inc(scattered, 16)
                pool.wait_ge(scattered, (j + 1) * 16 * TILES * TOPK)
                pool.sem_inc(z_free, 1)

            pool.sem_inc(z_free, 1)
            pool.wait_ge(const_in, 16)
            pool.wait_ge(filled, 16 * FILLS)
            keep_h(0)
            with pool.Fori(1, BATCHES) as i:
                tail(i - 1)
                keep_h(i)
                scatter(i - 1)
            tail(BATCHES - 1)
            scatter(BATCHES - 1)


def experts(nc, w13, w2, buf, ybuf, h1d, cst, firsts, h1_all, cw, gap_all, kept_all):
    NG, GS = 5, 2 * P
    CH = HID // P
    PG = 2 * NG
    NT = BATCHES * TILES
    with ExitStack() as ctx:
        sb = lambda name, shape, dt=F32: ctx.enter_context(nc.sbuf_tensor(name, shape, dt))
        ps = lambda name, shape: ctx.enter_context(nc.psum_tensor(name, shape, F32))
        sem = lambda name: ctx.enter_context(nc.semaphore(name))
        nws, w13_first, w2_first = firsts
        nwp = sb("nwp", [P, 3, 1])
        nwq = sb("nwq", [P, 3, 1])
        w13r = [w13_first, sb("w13r1", [P, 3, 2 * HID])]
        w2r = [w2_first, sb("w2r1", [P, CH, D])]
        w13h = [sb(f"w13h{p}", [P, 3, 2 * HID], F32R) for p in range(2)]
        w13l = [sb(f"w13l{p}", [P, 2, 2 * HID], F32R) for p in range(2)]
        w2h = [sb(f"w2h{p}", [P, CH, D], F32R) for p in range(2)]
        w2l = [sb(f"w2l{p}", [P, CH, D], F32R) for p in range(2)]
        zin = [sb(f"zin{s}", [P, 2, ROW]) for s in range(NG)]
        zz = [sb(f"zz{s}", [P, 3, GS], F32R) for s in range(2)]
        sg = sb("sg", [P, CH, GS])
        av = sb("av", [P, CH, GS])
        ah = [sb(f"ah{s}", [P, CH, GS], F32R) for s in range(2)]
        al = [sb(f"al{s}", [P, CH, GS], F32R) for s in range(2)]
        ysb = [sb(f"ysb{s}", [P, 2, D]) for s in range(2)]
        second = sb("second", [P, NT])
        total = sb("total", [P, NT])
        keepw = sb("keepw", [P, NT])
        psT = ps("psT", [P, 4, GS])
        psG = [ps(f"psG{c}", [P, 2, GS]) for c in range(CH)]
        psY = [ps(f"psY{s}", [P, 2, 256]) for s in range(2)]

        w_in = [sem(f"w_in{p}") for p in range(2)]
        z_got = [sem(f"z_got{s}") for s in range(NG)]
        h1_got = sem("h1_got")
        exp_in, weight_step, alone = sem("exp_in"), sem("weight_step"), sem("alone2")
        zT_full = sem("zT_full")
        zh_in, zl_in = sem("zh_in"), sem("zl_in")
        nwp_in = sem("nwp_in")
        wh_in, wl_in = sem("wh_in"), sem("wl_in")
        g_full, g_free = sem("g_full"), sem("g_free")
        sg_in, av_in, ah_in, al_in = sem("sg_in"), sem("av_in"), sem("ah_in"), sem("al_in")
        y_full, y_in = sem("y_full"), sem("y_in")
        y_out = [sem(f"y_out{s}") for s in range(2)]
        ident = cst[:, C_ID:C_ID + P]
        block = ctx.enter_context(nc.Block())

        def following(ep, m, more):
            return (ep, m + 1) if m + 1 < PG else (ep + 1, 0) if more else None

        @block.sync
        def _(sp):
            def weights(ep, p):
                if not (isinstance(ep, int) and ep == 0):
                    sp.wait_ge(wl_in, 3 * (2 * ep + p) - 3)
                sp.dma_start(w13r[p][:, :, :], w13[bass.ds(2 * ep + p, 1)].rearrange("a p k n -> (a p) k n")).then_inc(w_in[p], 16)
                sp.dma_start(w2r[p][:, :, :], w2[bass.ds(2 * ep + p, 1)].rearrange("a p k n -> (a p) k n")).then_inc(w_in[p], 16)

            def rows(ep, m):
                if m >= NG or not (isinstance(ep, int) and ep == 0):
                    sp.wait_ge(y_out[(m + 1) % 2], 32 * (NG * ep + (m - NG) // 2 + 1))
                sp.dma_start(zin[m % NG][:, :, :],
                             buf[bass.ds(ep * 2 * CAP + m * GS, GS), :].rearrange("(s p) d -> p s d", p=P)
                             ).then_inc(z_got[m % NG], 16)

            def pair(ep, more, first=False):
                for m in range(PG):
                    rows(ep, m)
                    if first and m == 1:
                        weights(0, 1)
                    if more and m == 3:
                        weights(ep + 1, 0)
                    if more and m == 8:
                        weights(ep + 1, 1)
                    if first and m == 4:
                        sp.dma_start(h1_all[:, :, :].rearrange("p (i t) d -> p i (t d)", t=TILES),
                                     h1d.rearrange("i p n -> p i n")).then_inc(h1_got, 16)

            pair(0, True, first=True)
            with sp.Fori(1, E // 2 - 1) as ep:
                pair(ep, True)
            pair(E // 2 - 1, False)

        @block.tensor
        def _(pe):
            def turn(ep, m):
                pe.wait_ge(z_got[m % NG], (ep * 2 + m // NG + 1) * 16)
                pe.wait_ge(zl_in, ep * PG + m + 2)
                for s in range(2):
                    rows = slice(s * P, (s + 1) * P)
                    nc.tensor.matmul(psT[64:P, 1, rows], zin[m % NG][:, s, 0:64], ident, start=True, stop=True)
                    for c, first, n in ((0, 0, P), (1, P, 64), (2, 64, P)):
                        last = nc.tensor.transpose(psT[0:n, c, rows], zin[m % NG][:, s, first:first + n], ident)
                last.then_inc(zT_full, 1)

            def hidden(ep, m):
                p, g = m // NG, m % NG
                pe.wait_ge(zl_in, ep * PG + m + 3)
                if g == 0:
                    pe.wait_ge(wl_in, (2 * ep + p) * 3 + 3)
                for c in range(CH):
                    pe.wait_ge(g_free, (ep * PG + m) * CH + c + 1)
                    for j in range(2):
                        cols = slice(j * HID + c * P, j * HID + (c + 1) * P)
                        terms = [(w13h, 0), (w13h, 1), (w13h, 2), (w13l, 0), (w13l, 1)]
                        for x, (w, k) in enumerate(terms):
                            last = nc.tensor.matmul(psG[c][:, j, :], w[p][:, k, cols], zz[m % 2][:, k, :],
                                                    start=(x == 0), stop=(x == 4))
                    last.then_inc(g_full, 1)

            def output(ep, m):
                p = (m // NG) % 2
                pe.wait_ge(al_in, (ep * PG + m + 1) * CH + 1)
                pe.wait_ge(y_in, ep * PG + m + 1)
                for s in range(2):
                    terms = [(a, w, c) for c in range(CH) for a, w in ((ah, w2h), (ah, w2l), (al, w2h))]
                    for x, (a, w, c) in enumerate(terms):
                        last = nc.tensor.matmul(psY[m % 2][:, s, 0:D], a[m % 2][:, c, s * P:(s + 1) * P], w[p][:, c, :],
                                                start=(x == 0), stop=(x == len(terms) - 1))
                last.then_inc(y_full, 1)

            def pair(ep, more, first=False):
                for m in range(PG):
                    nxt = following(ep, m, more)
                    if nxt:
                        turn(*nxt)
                    hidden(ep, m)
                    if m:
                        output(ep, m - 1)
                    elif not first:
                        output(ep - 1, PG - 1)

            turn(0, 0)
            pair(0, True, first=True)
            with pe.Fori(1, E // 2 - 1) as ep:
                pair(ep, True)
            pair(E // 2 - 1, False)
            output(E // 2 - 1, PG - 1)

        def pieces(p, scale):
            return [(w13r[p][:, k, :], w13h[p][:, k, :], w13l[p][:, k, :] if k < 2 else None, scale[:, k, :])
                    for k in range(3)] + [(w2r[p][:, :, :], w2h[p][:, :, :], w2l[p][:, :, :], 1.0)]

        SPLITS = {1: (0, 1, [0]), 2: (0, 1, [1, 2]), 3: (0, 1, [3]), 6: (1, 0, [0]), 7: (1, 0, [1, 2]), 8: (1, 0, [3])}

        @block.scalar
        def _(act):
            def split(ep, p, x):
                raw, hi, _, scale = pieces(p, (nwp, nwq)[p])[x]
                if x == 0:
                    if p or not (isinstance(ep, int) and ep == 0):
                        act.wait_ge(w_in[p], (ep + p) * 32)
                    act.wait_ge(nwp_in, 2 * ep + p + 1)
                    if not (isinstance(ep, int) and ep == 0):
                        act.wait_ge(y_full, (ep - 1) * PG + (p + 1) * NG)
                nc.scalar.activation(hi, raw, ACT.Copy, scale=scale).then_inc(wh_in, 1)

            def group(ep, m):
                act.wait_ge(zT_full, ep * PG + m + 1)
                if not (isinstance(ep, int) and ep == 0 and m < 2):
                    act.wait_ge(g_full, (ep * PG + m - 1) * CH)
                nc.scalar.activation(zz[m % 2][:, :, :], psT[:, 0:3, :], ACT.Copy).then_inc(zh_in, 1)

            def high(ep, m, c):
                act.wait_ge(av_in, (ep * PG + m) * CH + c + 1)
                if c == 0 and not (isinstance(ep, int) and ep == 0 and m < 2):
                    act.wait_ge(y_full, ep * PG + m - 1)
                nc.scalar.activation(ah[m % 2][:, c, :], av[:, c, :], ACT.Copy).then_inc(ah_in, 1)

            def leave(ep, m):
                act.wait_ge(y_full, ep * PG + m + 1)
                if m >= 2 or not (isinstance(ep, int) and ep == 0):
                    act.wait_ge(y_out[m % 2], 32 * (ep * NG + m // 2))
                nc.scalar.activation(ysb[m % 2][:, :, :], psY[m % 2][:, :, 0:D], ACT.Copy).then_inc(y_in, 1)

            def pair(ep, more, first=False):
                for m in range(PG):
                    nxt = following(ep, m, more)
                    if nxt:
                        group(*nxt)
                    for c in range(CH):
                        act.wait_ge(g_full, (ep * PG + m) * CH + c + 1)
                        if c == 0:
                            act.wait_ge(g_free, (ep * PG + m) * CH + CH)
                        nc.scalar.activation(sg[:, c, :], psG[c][:, 0, :], ACT.Silu).then_inc(sg_in, 1)
                        if c:
                            high(ep, m, c - 1)
                    high(ep, m, CH - 1)
                    if m:
                        leave(ep, m - 1)
                    elif not first:
                        leave(ep - 1, PG - 1)
                    if m in SPLITS and (more or not SPLITS[m][0]):
                        later, p, xs = SPLITS[m]
                        for x in xs:
                            split(ep + later, p, x)

            act.sem_inc(y_in, 2)
            nc.scalar.activation(second[:, :], gap_all[:, :], ACT.Exp).then_inc(exp_in, 1)
            for x in range(3):
                split(0, 0, x)
            group(0, 0)
            split(0, 0, 3)
            pair(0, True, first=True)
            with act.Fori(1, E // 2 - 1) as ep:
                pair(ep, True)
            pair(E // 2 - 1, False)
            leave(E // 2 - 1, PG - 1)

        @block.vector
        def _(dve):
            def scale_of(ep, p):
                e = 2 * ep + p
                if not (isinstance(ep, int) and ep == 0):
                    dve.wait_ge(wl_in, 3 * e - 3)
                nc.vector.tensor_copy((nwp, nwq)[p][:, :, :], nws[:, :, bass.ds(e, 1)]).then_inc(nwp_in, 1)
                dve.wait_ge(nwp_in, e + 1)

            def split(ep, p, x):
                if x == 0:
                    scale_of(ep, p)
                raw, hi, lo, scale = pieces(p, (nwp, nwq)[p])[x]
                if lo is None:
                    return
                dve.wait_ge(wh_in, (2 * ep + p) * 4 + x + 1)
                nc.vector.scalar_tensor_tensor(out=lo, in0=raw, scalar=scale, in1=hi.bitcast(F32), op0=ALU.mult,
                                               op1=ALU.subtract).then_inc(wl_in, 1)

            def group(ep, m):
                dve.wait_ge(zh_in, ep * PG + m + 1)
                for rows, k in ((slice(64, P), 1), (slice(0, P), 2)):
                    last = nc.vector.tensor_tensor(zz[m % 2][rows, k, :], psT[rows, k, :],
                                                   zz[m % 2][rows, k, :].bitcast(F32), ALU.subtract)
                last.then_inc(zl_in, 1)

            def low(ep, m, c):
                dve.wait_ge(ah_in, (ep * PG + m) * CH + c + 1)
                nc.vector.tensor_tensor(al[m % 2][:, c, :], av[:, c, :], ah[m % 2][:, c, :].bitcast(F32),
                                        ALU.subtract).then_inc(al_in, 1)

            def pair(ep, more):
                for m in range(PG):
                    nxt = following(ep, m, more)
                    if nxt:
                        group(*nxt)
                    for c in range(CH):
                        n = (ep * PG + m) * CH + c
                        dve.wait_ge(sg_in, n + 1)
                        if c == 0:
                            dve.wait_ge(al_in, (ep * PG + m) * CH + 1)
                        nc.vector.tensor_tensor(av[:, c, :], sg[:, c, :], psG[c][:, 1, :], ALU.mult).then_inc(av_in, 1)
                        dve.wait_ge(av_in, n + 1)
                        dve.sem_inc(g_free, 1)
                        if c:
                            low(ep, m, c - 1)
                    low(ep, m, CH - 1)
                    if m in SPLITS and (more or not SPLITS[m][0]):
                        later, p, xs = SPLITS[m]
                        for x in xs:
                            split(ep + later, p, x)

            dve.sem_inc(g_free, CH)
            dve.sem_inc(al_in, 1)
            dve.sem_inc(zl_in, 2)
            for x in range(3):
                split(0, 0, x)
            group(0, 0)
            split(0, 0, 3)
            pair(0, True)
            done = [0]

            def step(ins):
                done[0] += 1
                ins.then_inc(weight_step, 1)
                dve.wait_ge(weight_step, done[0])

            dve.wait_ge(exp_in, 1)
            kept = kept_all[:, :].rearrange("p (t k) -> p t k", k=TOPK)
            step(nc.vector.tensor_scalar(total[:, :], second[:, :], 1.0, None, ALU.add))
            step(nc.vector.reciprocal(total[:, :], total[:, :]))
            step(nc.vector.tensor_tensor(cw[:, :, 0], total[:, :], kept[:, :, 0], ALU.mult))
            step(nc.vector.tensor_tensor(cw[:, :, 1], total[:, :], second[:, :], ALU.mult))
            step(nc.vector.tensor_tensor(cw[:, :, 1], cw[:, :, 1], kept[:, :, 1], ALU.mult))
            step(nc.vector.scalar_tensor_tensor(out=keepw[:, :], in0=cw[:, :, 0], scalar=1.0, in1=cw[:, :, 1],
                                                op0=ALU.add, op1=ALU.add))
            with dve.Fori(1, E // 2 - 1) as ep:
                pair(ep, True)
            pair(E // 2 - 1, False)

        @block.gpsimd
        def _(pool):
            def write(ep, m):
                pool.wait_ge(y_in, ep * PG + m + 3)
                pool.sem_inc(alone, 1)
                for s in range(2):
                    nc.gpsimd.indirect_dma_start(
                        out=ybuf, out_offset=bass.IndirectOffsetOnAxis(ap=zin[m % NG][:, s, D:ROW].bitcast(U32), axis=0),
                        in_=ysb[m % 2][:, s, :], in_offset=None, bounds_check=TOKENS * TOPK - 1,
                        oob_is_err=False).then_inc(y_out[m % 2], 16)

            for m in range(PG):
                write(0, m)
            pool.wait_ge(h1_got, 16)
            pool.wait_ge(weight_step, 6)
            for t in range(NT):
                nc.gpsimd.tensor_scalar(h1_all[:, t, :], h1_all[:, t, :], keepw[:, t:t + 1], 1.0, ALU.mult, ALU.mult)
            with pool.Fori(1, E // 2) as ep:
                for m in range(PG):
                    write(ep, m)
            for s in range(2):
                pool.wait_ge(y_out[s], 32 * NG * E // 2)


def combine(nc, ybuf, out, cst, h1_all, cw):
    with ExitStack() as ctx:
        sb = lambda name, shape, dt=F32: ctx.enter_context(nc.sbuf_tensor(name, shape, dt))
        sem = lambda name: ctx.enter_context(nc.semaphore(name))
        f = sb("f", [P, BATCHES, TILES, TOPK, D])
        r = sb("r2", [P, BATCHES, TILES, D])
        total = sb("total2", [P, BATCHES, TILES])
        less = sb("less", [P, BATCHES, TILES])
        squares = sb("squares", [P, BATCHES, TILES])
        rstd = sb("rstd2", [P, BATCHES, TILES])
        shift = sb("shift", [P, BATCHES, TILES])
        res = sb("res", [P, BATCHES, TILES, D])
        got = [sem(f"got{b}") for b in range(BATCHES)]
        sum_step, less_in, squares_in = sem("sum_step"), sem("less_in"), sem("squares_in")
        rstd_in, pool_step = sem("rstd2_in"), sem("pool2_step")
        shift_in, res_in, written = sem("shift_in"), sem("res_in"), sem("written")
        block = ctx.enter_context(nc.Block())

        @block.sync
        def _(sp):
            for b in range(BATCHES):
                sp.dma_start(f[:, b, :, :, :].rearrange("p t k d -> p t (k d)"),
                             ybuf.rearrange("(b t p k) d -> b p t (k d)", t=TILES, p=P, k=TOPK)[b]).then_inc(got[b], 16)
            for b in range(BATCHES):
                sp.wait_ge(res_in, b + 1)
                sp.dma_start(out[b].rearrange("(t p) d -> p t d", p=P), res[:, b, :, :]).then_inc(written, 16)
            sp.wait_ge(written, BATCHES * 16)

        @block.vector
        def _(dve):
            for b in range(BATCHES):
                dve.wait_ge(got[b], 16)
                for k in range(TOPK):
                    for t in range(TILES):
                        if k:
                            dve.wait_ge(sum_step, b * TOPK * TILES + t + 1)
                        nc.vector.scalar_tensor_tensor(
                            out=r[:, b, t, :], in0=f[:, b, t, k, :], scalar=cw[:, b * TILES + t, k:k + 1],
                            in1=r[:, b, t, :] if k else h1_all[:, b * TILES + t, :], op0=ALU.mult, op1=ALU.add,
                            accum_out=total[:, b, t:t + 1] if k else None).then_inc(sum_step, 1)
                dve.wait_ge(sum_step, (b + 1) * TOPK * TILES)
                nc.vector.tensor_scalar(less[:, b, :], total[:, b, :], -1.0 / D, None, ALU.mult).then_inc(less_in, 1)

        @block.gpsimd
        def _(pool):
            for b in range(BATCHES):
                pool.wait_ge(squares_in, b + 1)
                nc.gpsimd.tensor_scalar(rstd[:, b, :], squares[:, b, :], 1.0 / D, 1e-5, ALU.mult, ALU.add
                                        ).then_inc(pool_step, 1)
                pool.wait_ge(pool_step, b + 1)
                nc.gpsimd.tensor_tensor(rstd[:, b, :], rstd[:, b, :], cst[:, C_NHALF:C_NHALF + TILES],
                                        ALU.pow).then_inc(rstd_in, 1)
                pool.wait_ge(rstd_in, b + 1)
                nc.gpsimd.tensor_tensor(shift[:, b, :], less[:, b, :], rstd[:, b, :], ALU.mult).then_inc(shift_in, 1)

        @block.scalar
        def _(act):
            def square(b):
                act.wait_ge(less_in, b + 1)
                for t in range(TILES):
                    last = nc.scalar.activation(f[:, b, t, 0, :], r[:, b, t, :], ACT.Square, bias=less[:, b, t:t + 1],
                                                accum_out=squares[:, b, t:t + 1])
                last.then_inc(squares_in, 1)

            square(0)
            for b in range(BATCHES):
                if b + 1 < BATCHES:
                    square(b + 1)
                act.wait_ge(shift_in, b + 1)
                for t in range(TILES):
                    last = nc.scalar.activation(res[:, b, t, :], r[:, b, t, :], ACT.Identity,
                                                scale=rstd[:, b, t:t + 1], bias=shift[:, b, t:t + 1])
                last.then_inc(res_in, 1)


def _layout(x, L0_tok_freq_bands, L0_tok_W, L0_attn_w_qkv, L0_attn_b_qkv, L0_attn_w_proj, L0_attn_b_proj,
            L0_ffn_gate_w, L0_ffn_w13, L0_ffn_w2, L0_ffn_norm_w):
    import numpy as np
    a = {}
    xv = np.asarray(x).reshape(BATCHES, SEQ, VALUES).transpose(0, 2, 1)
    xv = np.concatenate([xv, xv[:, 4 * P:]], axis=1).reshape(BATCHES, XCHUNKS, P, SEQ)
    a["x"] = np.ascontiguousarray(xv.transpose(0, 2, 1, 3))
    fr = np.asarray(L0_tok_freq_bands)
    f = np.empty((P, 9), fr.dtype)
    f[:, 0:6] = fr
    for m in range(3):
        f[:64, 6 + m], f[64:, 6 + m] = fr[2 * m], fr[2 * m + 1]
    a["fband"] = f
    w = np.asarray(L0_tok_W).T.reshape(VALUES, 2, BANDS, D)
    wk = np.empty((KTILES, P, D), w.dtype)
    for n in range(ANGLES):
        for s in range(2):
            if n < 4 * BANDS:
                c, b = n // BANDS, n % BANDS
                wk[2 * n + s] = w[c * P:(c + 1) * P, s, b]
            else:
                m = n - 4 * BANDS
                wk[2 * n + s, :64] = w[4 * P:, s, 2 * m]
                wk[2 * n + s, 64:] = w[4 * P:, s, 2 * m + 1]
    a["wtok"] = np.ascontiguousarray(wk.transpose(1, 0, 2))
    wq, bq = np.asarray(L0_attn_w_qkv), np.asarray(L0_attn_b_qkv)
    wt = np.zeros((HALF + 1, 2, 3 * D), wq.dtype)
    wt[:HALF, 0], wt[:HALF, 1], wt[HALF, 0] = wq[:, :HALF].T, wq[:, HALF:].T, bq
    a["wqkv"] = wt
    wp, bp = np.asarray(L0_attn_w_proj), np.asarray(L0_attn_b_proj)
    pw = np.zeros((QUADS, 4, 32, D), wp.dtype)
    pw[:, :, :HD] = wp.T.reshape(QUADS, 4, HD, D)
    pw[0, 0, HD] = bp
    a["wproj"] = np.ascontiguousarray(pw.reshape(QUADS, P, D).transpose(1, 0, 2))
    a["gate"] = np.ascontiguousarray(np.asarray(L0_ffn_gate_w).T.reshape(2, HALF, E).transpose(1, 0, 2))
    rows = np.concatenate([np.arange(D), np.arange(D)])
    a["nw"] = np.ascontiguousarray(np.asarray(L0_ffn_norm_w).T[rows].reshape(3, P, E).transpose(1, 0, 2))
    a["w13"] = np.ascontiguousarray(np.asarray(L0_ffn_w13).transpose(0, 2, 1)[:, rows].reshape(E, 3, P, 2 * HID).transpose(0, 2, 1, 3))
    a["w2"] = np.ascontiguousarray(np.asarray(L0_ffn_w2).transpose(0, 2, 1).reshape(E, HID // P, P, D).transpose(0, 2, 1, 3))
    sp = np.zeros((HALF, 2, 3, 2, 2, 3, HD), np.float32)
    for j in range(3):
        for s in range(2):
            for d in range(HD):
                for part in range(3):
                    sp[(2 * j + s) * HD + d, 0, j, int(part == 2), s, part, d] = 1.0
                    sp[(2 * j + s) * HD + d, 1, j, int(part == 1), s, part, d] = 1.0
    a["spread"] = sp.reshape(HALF, 12 * HALF)
    c = np.zeros((P, C_ALL), np.float32)
    c[:, C_ID:C_ID + P] = np.eye(P)
    c[:, C_UP:C_UP + P] = np.triu(np.ones((P, P)), 1)
    c[:, C_ONE:C_ONE + P] = 1.0
    c[:, C_IOTA:C_IOTA + E] = np.arange(E)
    c[:HALF // 2, C_MASK], c[HALF // 2:, C_MASK + 1] = 1.0, 1.0
    c[:, C_NHALF:C_NHALF + TILES] = -0.5
    c[:, C_HPI] = HALF_PI
    c[:, C_DST:C_DST + TILES * TOPK] = 2 * np.arange(P)[:, None] + np.array([2 * P * t + k for t in range(TILES) for k in range(TOPK)])
    a["consts"] = c
    return a


def kernel(**inputs):
    import numpy as _np
    import concourse.bacc as _bacc
    from concourse import mybir as _mybir
    from concourse.bass_utils import run_bass_kernel_spmd as _run

    nc = _bacc.Bacc("TRN2", target_bir_lowering=False, num_devices=1)
    laid = _layout(**inputs)
    aps = {n: nc.dram_tensor(f"in_{n}", a.shape, _mybir.dt.from_np(a.dtype), kind="ExternalInput").ap()
           for n, a in laid.items()}
    out = nc.dram_tensor("out_0_dram", (BATCHES, SEQ, D), _mybir.dt.float32, kind="ExternalOutput").ap()
    build(nc, out=out, **aps)
    r = _run(nc, [{f"in_{n}": a for n, a in laid.items()}], core_ids=[0])
    return r.results[0]["out_0_dram"]
```
